# Optimizing a Trainium2 kernel written in Bass

```python
import numpy as np
import jax
import jax.numpy as jnp

def _softmax(x, axis=-1):
    return jax.nn.softmax(x, axis=axis)

def _gelu(x):
    return jax.nn.gelu(x, approximate=True)

def _silu(x):
    return jax.nn.silu(x)

def _sigmoid(x):
    return jax.nn.sigmoid(x)

def _layernorm(x, axis=-1, eps=1e-05):
    m = jnp.mean(x, axis=axis, keepdims=True)
    v = jnp.var(x, axis=axis, keepdims=True)
    return (x - m) / jnp.sqrt(v + eps)

def _scatter_add(tgt, idx, src, axis=0):
    return tgt.at[idx].add(src)

def _segment_sum(src, seg, n):
    return jax.ops.segment_sum(src, seg, n)
kernel_name = 'mk_xattn_seq_d4_seqx_r8_7bd52a'

def setup_inputs(seed: int=0):
    np.random.seed(seed)
    _w = jnp.asarray

    def _rec_inputs():
        import jax
        import jax.numpy as jnp
        _rk = jax.random.key(seed)
        x = 7.22e-05 + 1 * jax.random.normal(jax.random.fold_in(_rk, 1), (32, 56, 256), jnp.float32)
        _lenS = 56 - jax.random.randint(jax.random.fold_in(_rk, 7), (32,), 0, max(1, 56 // 4) + 1, jnp.int32)
        _lenS2 = 1500 - jax.random.randint(jax.random.fold_in(_rk, 8), (32,), 0, max(1, 1500 // 4) + 1, jnp.int32)
        _ctx_2048P = jax.random.normal(jax.random.fold_in(_rk, 11), (32, 16, 256), jnp.float32)
        _ctx_2048c = jax.random.dirichlet(jax.random.fold_in(_rk, 511), 0.3 * jnp.ones((16,), jnp.float32), (32, 1500))
        _ctx_2048t = jnp.einsum('bsk,bkd->bsd', _ctx_2048c, _ctx_2048P)
        _ctx_2048t = _ctx_2048t * jax.lax.rsqrt(jnp.mean(jnp.square(_ctx_2048t)) + 1e-12) * 0.953939
        ctx_2048 = 4.13588e-05 + 0.999923 * (_ctx_2048t + 0.3 * jax.random.normal(jax.random.fold_in(_rk, 611), (32, 1500, 256), jnp.float32))
        _validS = jnp.arange(56)[None, :] < _lenS[:, None]
        _validS2 = jnp.arange(1500)[None, :] < _lenS2[:, None]
        _causal = jnp.tril(jnp.ones((56, 56), dtype=bool))
        mask_Bx1xSxS2_ff0 = jnp.where(jnp.ones((32, 1, 56, 1500), dtype=bool), 0.0, -1000000000.0).astype(jnp.float32)
        mask_BxS2_ik0 = jnp.where(jnp.broadcast_to(_validS2[:, :], (32, 1500)), 0, 1).astype(jnp.int32)
        return (x, ctx_2048, mask_Bx1xSxS2_ff0, mask_BxS2_ik0)
    x, ctx_2048, mask_Bx1xSxS2_ff0, mask_BxS2_ik0 = _rec_inputs()

    def _L0_xattn_setup():
        import jax, jax.numpy as jnp
        import numpy as np
        H = 256
        NH = 32
        KVH = 8
        HD = H // NH
        GROUPS = NH // KVH
        EPS = 1e-06
        B, L, S = (4, 128, 128)

        def _gqa_forward(hidden_state, encoder_hidden_state, encoder_attention_mask, Wq, bq, Wk, bk, Wv, bv, Wo, bo, gamma, beta):
            b, l, _ = hidden_state.shape
            s = encoder_hidden_state.shape[1]
            q = hidden_state @ Wq + bq
            k = encoder_hidden_state @ Wk + bk
            v = encoder_hidden_state @ Wv + bv
            q = q.reshape(b, l, KVH, GROUPS, HD).transpose(0, 2, 3, 1, 4)
            k = k.reshape(b, s, KVH, HD).transpose(0, 2, 1, 3)
            v = v.reshape(b, s, KVH, HD).transpose(0, 2, 1, 3)
            scale = 1.0 / jnp.sqrt(jnp.asarray(HD, q.dtype))
            scores = jnp.einsum('bkgld,bksd->bkgls', q, k) * scale
            scores = scores + encoder_attention_mask[:, :, None, :, :]
            attn = jax.nn.softmax(scores, axis=-1)
            out = jnp.einsum('bkgls,bksd->bkgld', attn, v)
            out = out.transpose(0, 3, 1, 2, 4).reshape(b, l, H)
            out = out @ Wo + bo
            x = out + hidden_state
            mu = jnp.mean(x, axis=-1, keepdims=True)
            var = jnp.var(x, axis=-1, keepdims=True)
            return (x - mu) * jax.lax.rsqrt(var + EPS) * gamma + beta
        key = jax.random.key(seed)
        ks = jax.random.split(key, 12)
        sd = 0.02
        return {'hidden_state': jax.random.normal(ks[0], (B, L, H), jnp.float32), 'encoder_hidden_state': jax.random.normal(ks[1], (B, S, H), jnp.float32), 'encoder_attention_mask': jnp.zeros((B, 1, L, S), jnp.float32), 'Wq': jax.random.normal(ks[2], (H, H), jnp.float32) * sd, 'bq': jnp.zeros((H,), jnp.float32), 'Wk': jax.random.normal(ks[3], (H, KVH * HD), jnp.float32) * sd, 'bk': jnp.zeros((KVH * HD,), jnp.float32), 'Wv': jax.random.normal(ks[4], (H, KVH * HD), jnp.float32) * sd, 'bv': jnp.zeros((KVH * HD,), jnp.float32), 'Wo': jax.random.normal(ks[5], (H, H), jnp.float32) * sd, 'bo': jnp.zeros((H,), jnp.float32), 'gamma': jnp.ones((H,), jnp.float32), 'beta': jnp.zeros((H,), jnp.float32)}
    _L0_xattn_all = _L0_xattn_setup()
    _L0_xattn_in = {k: v for k, v in _L0_xattn_all.items() if k in ('Wq', 'bq', 'Wk', 'bk', 'Wv', 'bv', 'Wo', 'bo', 'gamma', 'beta')}
    del _L0_xattn_all

    def _L1_xattn_setup():
        import jax, jax.numpy as jnp
        import numpy as np
        B, L, E, H = (4, 64, 256, 32)
        S = E // H
        EXTRA_MAA, EXTRA_DECAY = (32, 64)
        EPS = 1e-05

        def _ln(x, w, b):
            m = jnp.mean(x, axis=-1, keepdims=True)
            v = jnp.mean((x - m) ** 2, axis=-1, keepdims=True)
            return (x - m) * jax.lax.rsqrt(v + EPS) * w + b

        def _token_shift(xn, prev_row):
            first = (prev_row - xn[:, 0])[:, None]
            rest = xn[:, :-1] - xn[:, 1:]
            return jnp.concatenate([first, rest], axis=1)
        key = jax.random.key(seed)
        ks = jax.random.split(key, 24)
        rn = lambda k, shp, s=1.0: jax.random.normal(k, shp, dtype=jnp.float32) * s
        return dict(x=rn(ks[0], (B, L, E)), state=rn(ks[1], (B, 2 + S, E), 0.1), ln1_w=jnp.ones((E,), jnp.float32), ln1_b=jnp.zeros((E,), jnp.float32), ln2_w=jnp.ones((E,), jnp.float32), ln2_b=jnp.zeros((E,), jnp.float32), maa_x=rn(ks[2], (E,), 0.02), maa_w1=rn(ks[3], (E, 5 * EXTRA_MAA), 0.02), maa_w2=rn(ks[4], (5, EXTRA_MAA, E), 0.02), maa_stack=rn(ks[5], (5, E), 0.02), time_decay=rn(ks[6], (E,), 0.5), decay_w1=rn(ks[7], (E, EXTRA_DECAY), 0.02), decay_w2=rn(ks[8], (EXTRA_DECAY, E), 0.02), faaaa=rn(ks[9], (H, S), 0.1), Wr=rn(ks[10], (E, E), 0.02), Wk=rn(ks[11], (E, E), 0.02), Wv=rn(ks[12], (E, E), 0.02), Wg=rn(ks[13], (E, E), 0.02), Wo=rn(ks[14], (E, E), 0.02), gn_w=jnp.ones((E,), jnp.float32), gn_b=jnp.zeros((E,), jnp.float32), ffn_maa_k=rn(ks[15], (E,), 0.02), ffn_maa_r=rn(ks[16], (E,), 0.02), ffn_Wk=rn(ks[17], (E, E), 0.02), ffn_Wr=rn(ks[18], (E, E), 0.02), ffn_Wv=rn(ks[19], (E, E), 0.02), i=0)
    _L1_xattn_all = _L1_xattn_setup()
    _L1_xattn_in = {k: v for k, v in _L1_xattn_all.items() if k in ('ln1_w', 'ln1_b', 'ln2_w', 'ln2_b', 'maa_x', 'maa_w1', 'maa_w2', 'maa_stack', 'time_decay', 'decay_w1', 'decay_w2', 'faaaa', 'Wr', 'Wk', 'Wv', 'Wg', 'Wo', 'gn_w', 'gn_b', 'ffn_maa_k', 'ffn_maa_r', 'ffn_Wk', 'ffn_Wr', 'ffn_Wv')}
    del _L1_xattn_all

    def _L2_xattn_setup():
        import jax, jax.numpy as jnp
        import numpy as np
        B, P, K, H, NH = (4, 256, 32, 256, 16)
        DH = H // NH
        EPS = 1e-06

        def rmsnorm(x, w):
            var = jnp.mean(jnp.square(x), axis=-1, keepdims=True)
            return x * jax.lax.rsqrt(var + EPS) * w
        key = jax.random.key(seed)
        ks = jax.random.split(key, 12)
        s = 0.02
        return {'x': jax.random.normal(ks[0], (B, P, H), jnp.float32), 'latents': jax.random.normal(ks[1], (B, K, H), jnp.float32), 'attention_mask': jax.random.randint(ks[2], (B, P), 0, 2, jnp.int32), 'q_w': s * jax.random.normal(ks[3], (H, H), jnp.float32), 'q_b': jnp.zeros((H,), jnp.float32), 'kv_w': s * jax.random.normal(ks[4], (H, 2 * H), jnp.float32), 'kv_b': jnp.zeros((2 * H,), jnp.float32), 'out_w': s * jax.random.normal(ks[5], (H, H), jnp.float32), 'out_b': jnp.zeros((H,), jnp.float32), 'postnorm_w': jnp.ones((H,), jnp.float32), 'mlp_w1': s * jax.random.normal(ks[6], (H, 4 * H), jnp.float32), 'mlp_b1': jnp.zeros((4 * H,), jnp.float32), 'mlp_w2': s * jax.random.normal(ks[7], (4 * H, H), jnp.float32), 'mlp_b2': jnp.zeros((H,), jnp.float32)}
    _L2_xattn_all = _L2_xattn_setup()
    _L2_xattn_in = {k: v for k, v in _L2_xattn_all.items() if k in ('q_w', 'q_b', 'kv_w', 'kv_b', 'out_w', 'out_b', 'postnorm_w', 'mlp_w1', 'mlp_b1', 'mlp_w2', 'mlp_b2')}
    del _L2_xattn_all

    def _L3_xattn_setup():
        import jax, jax.numpy as jnp
        import numpy as np
        E, H, L, B = (256, 32, 128, 4)
        S = E // H
        DM, DD = (32, 64)

        def _ln(x, w, b, eps=1e-05):
            m = x.mean(-1, keepdims=True)
            v = ((x - m) ** 2).mean(-1, keepdims=True)
            return (x - m) / jnp.sqrt(v + eps) * w + b

        def _block(x, state, ln1_w, ln1_b, ln2_w, ln2_b, maa_x, maa_w1, maa_w2, maa_stack, time_decay, td_w1, td_w2, u, Wr, Wk, Wv, Wg, Wo, gn_w, gn_b, ffn_maa_k, ffn_maa_r, Wfk, Wfr, Wfv):
            b, l, e = x.shape
            h = u.shape[0]
            s_ = e // h
            xa = _ln(x, ln1_w, ln1_b)
            sx = jnp.concatenate([state[:, 1:2] - xa[:, :1], xa[:, :-1] - xa[:, 1:]], axis=1)
            xxx = jnp.tanh((xa + sx * maa_x) @ maa_w1).reshape(b, l, 5, DM)
            xxx = jnp.einsum('blfd,fde->blfe', xxx, maa_w2)
            xm = xa[:, :, None] + sx[:, :, None] * (maa_stack + xxx)
            xk, xw, xv, xr, xg = (xm[:, :, j] for j in range(5))
            w = jnp.exp(-jnp.exp(time_decay + jnp.tanh(xw @ td_w1) @ td_w2)).reshape(b, l, h, s_)
            r = (xr @ Wr.T).reshape(b, l, h, s_)
            k = (xk @ Wk.T).reshape(b, l, h, s_)
            v = (xv @ Wv.T).reshape(b, l, h, s_)
            g = jax.nn.silu(xg @ Wg.T)
            s0 = state[:, 2:2 + s_].reshape(b, h, s_, s_)

            def step(s, rkvw):
                r_t, k_t, v_t, w_t = rkvw
                a = k_t[..., :, None] * v_t[..., None, :]
                out = jnp.einsum('bhi,bhij->bhj', r_t, u * a + s)
                s = a + w_t[..., :, None] * s
                return (s, out)
            rkvw = tuple((jnp.moveaxis(t, 1, 0) for t in (r, k, v, w)))
            _, out = jax.lax.scan(step, s0, rkvw)
            out = jnp.moveaxis(out, 0, 1).reshape(b, l, e)
            og = out.reshape(b, l, h, s_)
            m = og.mean(-1, keepdims=True)
            va = ((og - m) ** 2).mean(-1, keepdims=True)
            og = ((og - m) / jnp.sqrt(va + 1e-05)).reshape(b, l, e) * gn_w + gn_b
            x1 = x + og * g @ Wo.T
            xc = _ln(x1, ln2_w, ln2_b)
            sx2 = jnp.concatenate([state[:, 0:1] - xc[:, :1], xc[:, :-1] - xc[:, 1:]], axis=1)
            xk2 = xc + sx2 * ffn_maa_k
            xr2 = xc + sx2 * ffn_maa_r
            rr = jax.nn.sigmoid(xr2 @ Wfr.T)
            kk = jnp.square(jax.nn.relu(xk2 @ Wfk.T))
            return x1 + rr * (kk @ Wfv.T)
        key = jax.random.key(seed)
        ks = jax.random.split(key, 24)
        sc = 0.02
        d = {'x': jax.random.normal(ks[0], (B, L, E), jnp.float32), 'state': jax.random.normal(ks[1], (B, 2 + S, E), jnp.float32) * 0.1, 'ln1_w': jnp.ones((E,), jnp.float32), 'ln1_b': jnp.zeros((E,), jnp.float32), 'ln2_w': jnp.ones((E,), jnp.float32), 'ln2_b': jnp.zeros((E,), jnp.float32), 'maa_x': jax.random.normal(ks[2], (E,), jnp.float32) * 0.1, 'maa_w1': jax.random.normal(ks[3], (E, 5 * DM), jnp.float32) * sc, 'maa_w2': jax.random.normal(ks[4], (5, DM, E), jnp.float32) * sc, 'maa_stack': jax.random.normal(ks[5], (1, 5, E), jnp.float32) * 0.1, 'time_decay': jax.random.normal(ks[6], (E,), jnp.float32) * 0.5, 'td_w1': jax.random.normal(ks[7], (E, DD), jnp.float32) * sc, 'td_w2': jax.random.normal(ks[8], (DD, E), jnp.float32) * sc, 'u': jax.random.normal(ks[9], (H, S, 1), jnp.float32) * 0.1, 'Wr': jax.random.normal(ks[10], (E, E), jnp.float32) * sc, 'Wk': jax.random.normal(ks[11], (E, E), jnp.float32) * sc, 'Wv': jax.random.normal(ks[12], (E, E), jnp.float32) * sc, 'Wg': jax.random.normal(ks[13], (E, E), jnp.float32) * sc, 'Wo': jax.random.normal(ks[14], (E, E), jnp.float32) * sc, 'gn_w': jnp.ones((E,), jnp.float32), 'gn_b': jnp.zeros((E,), jnp.float32), 'ffn_maa_k': jax.random.normal(ks[15], (E,), jnp.float32) * 0.1, 'ffn_maa_r': jax.random.normal(ks[16], (E,), jnp.float32) * 0.1, 'Wfk': jax.random.normal(ks[17], (E, E), jnp.float32) * sc, 'Wfr': jax.random.normal(ks[18], (E, E), jnp.float32) * sc, 'Wfv': jax.random.normal(ks[19], (E, E), jnp.float32) * sc}
        return d
    _L3_xattn_all = _L3_xattn_setup()
    _L3_xattn_in = {k: v for k, v in _L3_xattn_all.items() if k in ('ln1_w', 'ln1_b', 'ln2_w', 'ln2_b', 'maa_x', 'maa_w1', 'maa_w2', 'maa_stack', 'time_decay', 'td_w1', 'td_w2', 'u', 'Wr', 'Wk', 'Wv', 'Wg', 'Wo', 'gn_w', 'gn_b', 'ffn_maa_k', 'ffn_maa_r', 'Wfk', 'Wfr', 'Wfv')}
    del _L3_xattn_all
    return {'x': x, 'ctx_2048': ctx_2048, 'mask_Bx1xSxS2_ff0': mask_Bx1xSxS2_ff0, 'mask_BxS2_ik0': mask_BxS2_ik0, 'L0_xattn_Wq': _L0_xattn_in['Wq'], 'L0_xattn_bq': _L0_xattn_in['bq'], 'L0_xattn_Wk': _L0_xattn_in['Wk'], 'L0_xattn_bk': _L0_xattn_in['bk'], 'L0_xattn_Wv': _L0_xattn_in['Wv'], 'L0_xattn_bv': _L0_xattn_in['bv'], 'L0_xattn_Wo': _L0_xattn_in['Wo'], 'L0_xattn_bo': _L0_xattn_in['bo'], 'L0_xattn_gamma': _L0_xattn_in['gamma'], 'L0_xattn_beta': _L0_xattn_in['beta'], 'L1_xattn_ln1_w': _L1_xattn_in['ln1_w'], 'L1_xattn_ln1_b': _L1_xattn_in['ln1_b'], 'L1_xattn_ln2_w': _L1_xattn_in['ln2_w'], 'L1_xattn_ln2_b': _L1_xattn_in['ln2_b'], 'L1_xattn_maa_x': _L1_xattn_in['maa_x'], 'L1_xattn_maa_w1': _L1_xattn_in['maa_w1'], 'L1_xattn_maa_w2': _L1_xattn_in['maa_w2'], 'L1_xattn_maa_stack': _L1_xattn_in['maa_stack'], 'L1_xattn_time_decay': _L1_xattn_in['time_decay'], 'L1_xattn_decay_w1': _L1_xattn_in['decay_w1'], 'L1_xattn_decay_w2': _L1_xattn_in['decay_w2'], 'L1_xattn_faaaa': _L1_xattn_in['faaaa'], 'L1_xattn_Wr': _L1_xattn_in['Wr'], 'L1_xattn_Wk': _L1_xattn_in['Wk'], 'L1_xattn_Wv': _L1_xattn_in['Wv'], 'L1_xattn_Wg': _L1_xattn_in['Wg'], 'L1_xattn_Wo': _L1_xattn_in['Wo'], 'L1_xattn_gn_w': _L1_xattn_in['gn_w'], 'L1_xattn_gn_b': _L1_xattn_in['gn_b'], 'L1_xattn_ffn_maa_k': _L1_xattn_in['ffn_maa_k'], 'L1_xattn_ffn_maa_r': _L1_xattn_in['ffn_maa_r'], 'L1_xattn_ffn_Wk': _L1_xattn_in['ffn_Wk'], 'L1_xattn_ffn_Wr': _L1_xattn_in['ffn_Wr'], 'L1_xattn_ffn_Wv': _L1_xattn_in['ffn_Wv'], 'L2_xattn_q_w': _L2_xattn_in['q_w'], 'L2_xattn_q_b': _L2_xattn_in['q_b'], 'L2_xattn_kv_w': _L2_xattn_in['kv_w'], 'L2_xattn_kv_b': _L2_xattn_in['kv_b'], 'L2_xattn_out_w': _L2_xattn_in['out_w'], 'L2_xattn_out_b': _L2_xattn_in['out_b'], 'L2_xattn_postnorm_w': _L2_xattn_in['postnorm_w'], 'L2_xattn_mlp_w1': _L2_xattn_in['mlp_w1'], 'L2_xattn_mlp_b1': _L2_xattn_in['mlp_b1'], 'L2_xattn_mlp_w2': _L2_xattn_in['mlp_w2'], 'L2_xattn_mlp_b2': _L2_xattn_in['mlp_b2'], 'L3_xattn_ln1_w': _L3_xattn_in['ln1_w'], 'L3_xattn_ln1_b': _L3_xattn_in['ln1_b'], 'L3_xattn_ln2_w': _L3_xattn_in['ln2_w'], 'L3_xattn_ln2_b': _L3_xattn_in['ln2_b'], 'L3_xattn_maa_x': _L3_xattn_in['maa_x'], 'L3_xattn_maa_w1': _L3_xattn_in['maa_w1'], 'L3_xattn_maa_w2': _L3_xattn_in['maa_w2'], 'L3_xattn_maa_stack': _L3_xattn_in['maa_stack'], 'L3_xattn_time_decay': _L3_xattn_in['time_decay'], 'L3_xattn_td_w1': _L3_xattn_in['td_w1'], 'L3_xattn_td_w2': _L3_xattn_in['td_w2'], 'L3_xattn_u': _L3_xattn_in['u'], 'L3_xattn_Wr': _L3_xattn_in['Wr'], 'L3_xattn_Wk': _L3_xattn_in['Wk'], 'L3_xattn_Wv': _L3_xattn_in['Wv'], 'L3_xattn_Wg': _L3_xattn_in['Wg'], 'L3_xattn_Wo': _L3_xattn_in['Wo'], 'L3_xattn_gn_w': _L3_xattn_in['gn_w'], 'L3_xattn_gn_b': _L3_xattn_in['gn_b'], 'L3_xattn_ffn_maa_k': _L3_xattn_in['ffn_maa_k'], 'L3_xattn_ffn_maa_r': _L3_xattn_in['ffn_maa_r'], 'L3_xattn_Wfk': _L3_xattn_in['Wfk'], 'L3_xattn_Wfr': _L3_xattn_in['Wfr'], 'L3_xattn_Wfv': _L3_xattn_in['Wfv']}

def reference(x, ctx_2048, mask_Bx1xSxS2_ff0, mask_BxS2_ik0, L0_xattn_Wq, L0_xattn_bq, L0_xattn_Wk, L0_xattn_bk, L0_xattn_Wv, L0_xattn_bv, L0_xattn_Wo, L0_xattn_bo, L0_xattn_gamma, L0_xattn_beta, L1_xattn_ln1_w, L1_xattn_ln1_b, L1_xattn_ln2_w, L1_xattn_ln2_b, L1_xattn_maa_x, L1_xattn_maa_w1, L1_xattn_maa_w2, L1_xattn_maa_stack, L1_xattn_time_decay, L1_xattn_decay_w1, L1_xattn_decay_w2, L1_xattn_faaaa, L1_xattn_Wr, L1_xattn_Wk, L1_xattn_Wv, L1_xattn_Wg, L1_xattn_Wo, L1_xattn_gn_w, L1_xattn_gn_b, L1_xattn_ffn_maa_k, L1_xattn_ffn_maa_r, L1_xattn_ffn_Wk, L1_xattn_ffn_Wr, L1_xattn_ffn_Wv, L2_xattn_q_w, L2_xattn_q_b, L2_xattn_kv_w, L2_xattn_kv_b, L2_xattn_out_w, L2_xattn_out_b, L2_xattn_postnorm_w, L2_xattn_mlp_w1, L2_xattn_mlp_b1, L2_xattn_mlp_w2, L2_xattn_mlp_b2, L3_xattn_ln1_w, L3_xattn_ln1_b, L3_xattn_ln2_w, L3_xattn_ln2_b, L3_xattn_maa_x, L3_xattn_maa_w1, L3_xattn_maa_w2, L3_xattn_maa_stack, L3_xattn_time_decay, L3_xattn_td_w1, L3_xattn_td_w2, L3_xattn_u, L3_xattn_Wr, L3_xattn_Wk, L3_xattn_Wv, L3_xattn_Wg, L3_xattn_Wo, L3_xattn_gn_w, L3_xattn_gn_b, L3_xattn_ffn_maa_k, L3_xattn_ffn_maa_r, L3_xattn_Wfk, L3_xattn_Wfr, L3_xattn_Wfv):
    import jax
    import jax.numpy as jnp

    def _L0_xattn_ref(hidden_state, encoder_hidden_state, encoder_attention_mask, Wq, bq, Wk, bk, Wv, bv, Wo, bo, gamma, beta):
        import jax, jax.numpy as jnp
        import numpy as np
        H = 256
        NH = 32
        KVH = 8
        HD = H // NH
        GROUPS = NH // KVH
        EPS = 1e-06
        B, L, S = (4, 128, 128)

        def _gqa_forward(hidden_state, encoder_hidden_state, encoder_attention_mask, Wq, bq, Wk, bk, Wv, bv, Wo, bo, gamma, beta):
            b, l, _ = hidden_state.shape
            s = encoder_hidden_state.shape[1]
            q = hidden_state @ Wq + bq
            k = encoder_hidden_state @ Wk + bk
            v = encoder_hidden_state @ Wv + bv
            q = q.reshape(b, l, KVH, GROUPS, HD).transpose(0, 2, 3, 1, 4)
            k = k.reshape(b, s, KVH, HD).transpose(0, 2, 1, 3)
            v = v.reshape(b, s, KVH, HD).transpose(0, 2, 1, 3)
            scale = 1.0 / jnp.sqrt(jnp.asarray(HD, q.dtype))
            scores = jnp.einsum('bkgld,bksd->bkgls', q, k) * scale
            scores = scores + encoder_attention_mask[:, :, None, :, :]
            attn = jax.nn.softmax(scores, axis=-1)
            out = jnp.einsum('bkgls,bksd->bkgld', attn, v)
            out = out.transpose(0, 3, 1, 2, 4).reshape(b, l, H)
            out = out @ Wo + bo
            x = out + hidden_state
            mu = jnp.mean(x, axis=-1, keepdims=True)
            var = jnp.var(x, axis=-1, keepdims=True)
            return (x - mu) * jax.lax.rsqrt(var + EPS) * gamma + beta
        return _gqa_forward(hidden_state, encoder_hidden_state, encoder_attention_mask, Wq, bq, Wk, bk, Wv, bv, Wo, bo, gamma, beta)

    def _L1_xattn_ref(x, state, ln1_w, ln1_b, ln2_w, ln2_b, maa_x, maa_w1, maa_w2, maa_stack, time_decay, decay_w1, decay_w2, faaaa, Wr, Wk, Wv, Wg, Wo, gn_w, gn_b, ffn_maa_k, ffn_maa_r, ffn_Wk, ffn_Wr, ffn_Wv, i):
        import jax, jax.numpy as jnp
        import numpy as np
        B, L, E, H = (4, 64, 256, 32)
        S = E // H
        EXTRA_MAA, EXTRA_DECAY = (32, 64)
        EPS = 1e-05

        def _ln(x, w, b):
            m = jnp.mean(x, axis=-1, keepdims=True)
            v = jnp.mean((x - m) ** 2, axis=-1, keepdims=True)
            return (x - m) * jax.lax.rsqrt(v + EPS) * w + b

        def _token_shift(xn, prev_row):
            first = (prev_row - xn[:, 0])[:, None]
            rest = xn[:, :-1] - xn[:, 1:]
            return jnp.concatenate([first, rest], axis=1)
        b, l = (x.shape[0], x.shape[1])
        i0 = (2 + S) * i + 0
        i1 = (2 + S) * i + 1
        xn = _ln(x, ln1_w, ln1_b)
        sx = _token_shift(xn, state[:, i1])
        xxx = jnp.tanh((xn + sx * maa_x) @ maa_w1).reshape(b, l, 5, 1, EXTRA_MAA)
        xxx = jnp.matmul(xxx, maa_w2).reshape(b, l, 5, E)
        x5 = xn[:, :, None] + sx[:, :, None] * (maa_stack + xxx)
        w = jnp.exp(-jnp.exp(time_decay + jnp.tanh(x5[:, :, 1] @ decay_w1) @ decay_w2))
        w = w.reshape(b, l, H, S)
        r = (x5[:, :, 3] @ Wr.T).reshape(b, l, H, S)
        k = (x5[:, :, 0] @ Wk.T).reshape(b, l, H, S)
        v = (x5[:, :, 2] @ Wv.T).reshape(b, l, H, S)
        g = jax.nn.silu(x5[:, :, 4] @ Wg.T)
        s0 = state[:, (2 + S) * i + 2:(2 + S) * (i + 1)].reshape(b, H, S, S)
        u = faaaa[None, :, :, None]

        def step(s, rkvw):
            r_t, k_t, v_t, w_t = rkvw
            a = k_t[:, :, :, None] * v_t[:, :, None, :]
            out = jnp.einsum('bhk,bhkd->bhd', r_t, u * a + s)
            return (a + w_t[:, :, :, None] * s, out)
        xs = tuple((jnp.moveaxis(t, 1, 0) for t in (r, k, v, w)))
        _, outs = jax.lax.scan(step, s0, xs)
        att = jnp.moveaxis(outs, 0, 1).reshape(b, l, E)
        a4 = att.reshape(b, l, H, S)
        m = jnp.mean(a4, axis=-1, keepdims=True)
        var = jnp.mean((a4 - m) ** 2, axis=-1, keepdims=True)
        att = ((a4 - m) * jax.lax.rsqrt(var + EPS)).reshape(b, l, E) * gn_w + gn_b
        x = x + att * g @ Wo.T
        xn2 = _ln(x, ln2_w, ln2_b)
        sx2 = _token_shift(xn2, state[:, i0])
        xk = xn2 + sx2 * ffn_maa_k
        xr = xn2 + sx2 * ffn_maa_r
        rr = jax.nn.sigmoid(xr @ ffn_Wr.T)
        kk = jnp.square(jax.nn.relu(xk @ ffn_Wk.T))
        x = x + rr * (kk @ ffn_Wv.T)
        return x

    def _L2_xattn_ref(x, latents, attention_mask, q_w, q_b, kv_w, kv_b, out_w, out_b, postnorm_w, mlp_w1, mlp_b1, mlp_w2, mlp_b2):
        import jax, jax.numpy as jnp
        import numpy as np
        B, P, K, H, NH = (4, 256, 32, 256, 16)
        DH = H // NH
        EPS = 1e-06

        def rmsnorm(x, w):
            var = jnp.mean(jnp.square(x), axis=-1, keepdims=True)
            return x * jax.lax.rsqrt(var + EPS) * w
        b, p, _ = x.shape
        k_len = latents.shape[1]
        residual = latents
        h = jnp.concatenate([x, latents], axis=1)
        q = (latents @ q_w + q_b).reshape(b, k_len, NH, DH)
        kv = (h @ kv_w + kv_b).reshape(b, p + k_len, NH, DH, 2)
        kmat, v = (kv[..., 0], kv[..., 1])
        attn = jnp.einsum('bkhd,bnhd->bhkn', q, kmat) / DH
        full_mask = jnp.concatenate([attention_mask.astype(bool), jnp.ones((b, k_len), bool)], axis=-1)
        attn = jnp.where(full_mask[:, None, None, :], attn, -jnp.inf)
        attn = jax.nn.softmax(attn.astype(jnp.float32), axis=-1).astype(q.dtype)
        attn_out = jnp.einsum('bhkn,bnhd->bkhd', attn, v).reshape(b, k_len, H)
        attn_out = attn_out @ out_w + out_b + residual
        out = rmsnorm(attn_out, postnorm_w)
        out = jax.nn.gelu(out @ mlp_w1 + mlp_b1) @ mlp_w2 + mlp_b2
        return out + residual

    def _L3_xattn_ref(x, state, ln1_w, ln1_b, ln2_w, ln2_b, maa_x, maa_w1, maa_w2, maa_stack, time_decay, td_w1, td_w2, u, Wr, Wk, Wv, Wg, Wo, gn_w, gn_b, ffn_maa_k, ffn_maa_r, Wfk, Wfr, Wfv):
        import jax, jax.numpy as jnp
        import numpy as np
        E, H, L, B = (256, 32, 128, 4)
        S = E // H
        DM, DD = (32, 64)

        def _ln(x, w, b, eps=1e-05):
            m = x.mean(-1, keepdims=True)
            v = ((x - m) ** 2).mean(-1, keepdims=True)
            return (x - m) / jnp.sqrt(v + eps) * w + b

        def _block(x, state, ln1_w, ln1_b, ln2_w, ln2_b, maa_x, maa_w1, maa_w2, maa_stack, time_decay, td_w1, td_w2, u, Wr, Wk, Wv, Wg, Wo, gn_w, gn_b, ffn_maa_k, ffn_maa_r, Wfk, Wfr, Wfv):
            b, l, e = x.shape
            h = u.shape[0]
            s_ = e // h
            xa = _ln(x, ln1_w, ln1_b)
            sx = jnp.concatenate([state[:, 1:2] - xa[:, :1], xa[:, :-1] - xa[:, 1:]], axis=1)
            xxx = jnp.tanh((xa + sx * maa_x) @ maa_w1).reshape(b, l, 5, DM)
            xxx = jnp.einsum('blfd,fde->blfe', xxx, maa_w2)
            xm = xa[:, :, None] + sx[:, :, None] * (maa_stack + xxx)
            xk, xw, xv, xr, xg = (xm[:, :, j] for j in range(5))
            w = jnp.exp(-jnp.exp(time_decay + jnp.tanh(xw @ td_w1) @ td_w2)).reshape(b, l, h, s_)
            r = (xr @ Wr.T).reshape(b, l, h, s_)
            k = (xk @ Wk.T).reshape(b, l, h, s_)
            v = (xv @ Wv.T).reshape(b, l, h, s_)
            g = jax.nn.silu(xg @ Wg.T)
            s0 = state[:, 2:2 + s_].reshape(b, h, s_, s_)

            def step(s, rkvw):
                r_t, k_t, v_t, w_t = rkvw
                a = k_t[..., :, None] * v_t[..., None, :]
                out = jnp.einsum('bhi,bhij->bhj', r_t, u * a + s)
                s = a + w_t[..., :, None] * s
                return (s, out)
            rkvw = tuple((jnp.moveaxis(t, 1, 0) for t in (r, k, v, w)))
            _, out = jax.lax.scan(step, s0, rkvw)
            out = jnp.moveaxis(out, 0, 1).reshape(b, l, e)
            og = out.reshape(b, l, h, s_)
            m = og.mean(-1, keepdims=True)
            va = ((og - m) ** 2).mean(-1, keepdims=True)
            og = ((og - m) / jnp.sqrt(va + 1e-05)).reshape(b, l, e) * gn_w + gn_b
            x1 = x + og * g @ Wo.T
            xc = _ln(x1, ln2_w, ln2_b)
            sx2 = jnp.concatenate([state[:, 0:1] - xc[:, :1], xc[:, :-1] - xc[:, 1:]], axis=1)
            xk2 = xc + sx2 * ffn_maa_k
            xr2 = xc + sx2 * ffn_maa_r
            rr = jax.nn.sigmoid(xr2 @ Wfr.T)
            kk = jnp.square(jax.nn.relu(xk2 @ Wfk.T))
            return x1 + rr * (kk @ Wfv.T)
        return _block(x, state, ln1_w, ln1_b, ln2_w, ln2_b, maa_x, maa_w1, maa_w2, maa_stack, time_decay, td_w1, td_w2, u, Wr, Wk, Wv, Wg, Wo, gn_w, gn_b, ffn_maa_k, ffn_maa_r, Wfk, Wfr, Wfv)
    x = _L0_xattn_ref(x, ctx_2048, mask_Bx1xSxS2_ff0, L0_xattn_Wq, L0_xattn_bq, L0_xattn_Wk, L0_xattn_bk, L0_xattn_Wv, L0_xattn_bv, L0_xattn_Wo, L0_xattn_bo, L0_xattn_gamma, L0_xattn_beta)
    x = _L1_xattn_ref(x, ctx_2048, L1_xattn_ln1_w, L1_xattn_ln1_b, L1_xattn_ln2_w, L1_xattn_ln2_b, L1_xattn_maa_x, L1_xattn_maa_w1, L1_xattn_maa_w2, L1_xattn_maa_stack, L1_xattn_time_decay, L1_xattn_decay_w1, L1_xattn_decay_w2, L1_xattn_faaaa, L1_xattn_Wr, L1_xattn_Wk, L1_xattn_Wv, L1_xattn_Wg, L1_xattn_Wo, L1_xattn_gn_w, L1_xattn_gn_b, L1_xattn_ffn_maa_k, L1_xattn_ffn_maa_r, L1_xattn_ffn_Wk, L1_xattn_ffn_Wr, L1_xattn_ffn_Wv, 0)
    x = _L2_xattn_ref(ctx_2048, x, mask_BxS2_ik0, L2_xattn_q_w, L2_xattn_q_b, L2_xattn_kv_w, L2_xattn_kv_b, L2_xattn_out_w, L2_xattn_out_b, L2_xattn_postnorm_w, L2_xattn_mlp_w1, L2_xattn_mlp_b1, L2_xattn_mlp_w2, L2_xattn_mlp_b2)
    x = _L3_xattn_ref(x, ctx_2048, L3_xattn_ln1_w, L3_xattn_ln1_b, L3_xattn_ln2_w, L3_xattn_ln2_b, L3_xattn_maa_x, L3_xattn_maa_w1, L3_xattn_maa_w2, L3_xattn_maa_stack, L3_xattn_time_decay, L3_xattn_td_w1, L3_xattn_td_w2, L3_xattn_u, L3_xattn_Wr, L3_xattn_Wk, L3_xattn_Wv, L3_xattn_Wg, L3_xattn_Wo, L3_xattn_gn_w, L3_xattn_gn_b, L3_xattn_ffn_maa_k, L3_xattn_ffn_maa_r, L3_xattn_Wfk, L3_xattn_Wfr, L3_xattn_Wfv)
    return x

_drawn_inputs = setup_inputs


def setup_inputs(seed=0):
    import zlib

    import numpy as np

    out = dict(_drawn_inputs(seed))
    spreads = {'L0_xattn_bq': (0.0, 0.8),
     'L0_xattn_bk': (0.0, 2.0),
     'L0_xattn_bv': (0.0, 0.1),
     'L0_xattn_bo': (0.0, 0.1),
     'L0_xattn_gamma': (1.0, 0.2),
     'L0_xattn_beta': (0.0, 0.1),
     'L1_xattn_ln1_w': (1.0, 0.6),
     'L1_xattn_ln1_b': (0.0, 0.589),
     'L1_xattn_ln2_w': (1.0, 0.6),
     'L1_xattn_ln2_b': (0.0, 0.8),
     'L1_xattn_gn_w': (1.0, 0.6),
     'L1_xattn_gn_b': (0.0, 0.8),
     'L2_xattn_q_b': (0.0, 2.0),
     'L2_xattn_kv_b': (0.0, 2.0),
     'L2_xattn_out_b': (0.0, 2.0),
     'L2_xattn_postnorm_w': (1.0, 0.6),
     'L2_xattn_mlp_b1': (0.0, 0.404),
     'L2_xattn_mlp_b2': (0.0, 0.1),
     'L3_xattn_ln1_w': (1.0, 0.568),
     'L3_xattn_ln1_b': (0.0, 0.568),
     'L3_xattn_ln2_w': (1.0, 0.6),
     'L3_xattn_ln2_b': (0.0, 0.8),
     'L3_xattn_gn_w': (1.0, 0.6),
     'L3_xattn_gn_b': (0.0, 0.8)}
    factors = {'L0_xattn_Wq': 8.0,
     'L0_xattn_Wk': 8.0,
     'L1_xattn_maa_x': 8.0,
     'L1_xattn_maa_w1': 8.0,
     'L1_xattn_maa_w2': 8.0,
     'L1_xattn_maa_stack': 8.0,
     'L1_xattn_time_decay': 2.894,
     'L1_xattn_decay_w1': 8.0,
     'L1_xattn_decay_w2': 8.0,
     'L1_xattn_faaaa': 6.243,
     'L1_xattn_ffn_maa_k': 8.0,
     'L1_xattn_ffn_maa_r': 8.0,
     'L1_xattn_ffn_Wk': 2.969,
     'L1_xattn_ffn_Wr': 8.0,
     'L1_xattn_ffn_Wv': 2.757,
     'L2_xattn_q_w': 8.0,
     'L2_xattn_kv_w': 8.0,
     'L2_xattn_out_w': 8.0,
     'L3_xattn_maa_x': 8.0,
     'L3_xattn_maa_w1': 7.681,
     'L3_xattn_maa_w2': 7.729,
     'L3_xattn_maa_stack': 2.876,
     'L3_xattn_time_decay': 2.782,
     'L3_xattn_td_w1': 8.0,
     'L3_xattn_td_w2': 8.0,
     'L3_xattn_u': 5.834,
     'L3_xattn_ffn_maa_k': 8.0,
     'L3_xattn_ffn_maa_r': 8.0,
     'L3_xattn_Wfk': 2.828,
     'L3_xattn_Wfr': 8.0}
    for name, (base, spread) in spreads.items():
        noise = np.random.default_rng([zlib.crc32(name.encode()), seed]).standard_normal(out[name].shape)
        drawn = base * np.exp(spread * noise) if base else spread * noise
        out[name] = jnp.asarray(drawn.astype(out[name].dtype))
    for name, factor in factors.items():
        out[name] = (out[name] * factor).astype(out[name].dtype)
    return out
```

```python
import numpy as np
from contextlib import ExitStack

import concourse.bass as bass
from concourse import mybir
from concourse.alu_op_type import AluOpType as ALU

F32 = mybir.dt.float32
BF16 = mybir.dt.bfloat16
I32 = mybir.dt.int32
ACT = mybir.ActivationFunctionType
AX_X = mybir.AxisListType.X

P = 128
B, L, E = 32, 56, 256
S = 1500
KC = E // P
T = B * L
PAIRS = B // 2
HALF = 64
NEG_BIG = -3.0e38

KVH, G, HD = 8, 4, 8
ST = 125
NT = S // ST
SC = 500
NC = S // SC
NJ = KVH // 2
QW = G * L
PW = 2 * QW
NR = NJ * PW // (2 * L)
K_PIECES = (0, 0, 0, 1, 1, 2)
Q_PIECES = (0, 1, 2, 0, 1, 0)
NS = len(K_PIECES)
SROWS = 16 * NS
MROWS = SROWS + 3


def natural(b):
    return HALF * (b % 2)


def wait_apart(eng, passed, which, value):
    eng.wait_ge(which, value)
    eng.sem_inc(passed, 1)


def clear(nc, sems):
    with nc.Block() as block:
        @block.gpsimd
        def _(pool):
            for s in sems:
                pool.sem_clear(s)


def layer0(nc, x_nat, a, passed):
    q_scr = nc.dram_tensor("q_scr", [3, KVH * HD, B, QW], BF16).ap()
    k_scr = nc.dram_tensor("k_scr", [2, 3, KVH * HD, S], BF16).ap()
    sems = []
    with ExitStack() as ctx:
        def sb(name, shape, dt=F32):
            return ctx.enter_context(nc.sbuf_tensor(name, shape, dt))

        def sem(name):
            sems.append(ctx.enter_context(nc.semaphore(name)))
            return sems[-1]

        ident = sb("ident", [P, P])
        identb = sb("identb", [P, P], BF16)
        wq = sb("wq", [P, KC, G, KVH * HD])
        bq = sb("bq", [KVH * HD, G])
        wkv = sb("wkv", [P, KC, P])
        bkv = sb("bkv", [P, 1])
        wo = sb("wo", [P, 2 * G, E])
        bo = sb("bo", [P, E])
        den_sel = sb("den_sel", [P, P])
        mask_sel = sb("mask_sel", [L, PW])
        ones = sb("ones", [P, 1])
        ctx_t = sb("ctx_t", [P, KC, T])
        kv_t = sb("kv_t", [P, S])
        k_piece = sb("k_piece", [KVH * HD, 3, S], BF16)
        k_rest = sb("k_rest", [KVH * HD, S])
        ks = [sb(f"ks{i}", [MROWS, NJ, S], BF16) for i in range(2)]
        qs = [sb(f"qs{i}", [MROWS, NJ, 2, QW], BF16) for i in range(2)]
        vp = [sb(f"vp{i}", [ST, NT, KVH, 32]) for i in range(2)]
        mask = [sb(f"mask{i}", [2 * L, S]) for i in range(2)]
        probs = [sb(f"probs{i}", [ST, NJ, PW]) for i in range(2)]
        masked = sb("masked", [2 * L, 2, SC])
        part_max = sb("part_max", [2 * L, NR, NC])
        row_max = sb("row_max", [2 * L, NR])
        neg_rest = sb("neg_rest", [2 * L, NR])
        neg_piece = sb("neg_piece", [2 * L, 3, NR], BF16)
        neg_t = sb("neg_t", [3 * NR, 2 * L], BF16)
        mask_abs = sb("mask_abs", [2 * L, S], BF16)
        mask_sum = sb("mask_sum", [2 * L, 1])
        flag = sb("flag", [1, 2], I32)
        o_raw = sb("o_raw", [P, PW])
        den_inv = sb("den_inv", [P, PW])
        o_n = sb("o_n", [P, PW])
        ps = ctx.enter_context(nc.psum_tensor("ps_a", [P, 8, 512], F32))
        FRONT, ACC, MISC = (4, 5), 6, 7

        CH = 8
        CW = CH * L
        with ExitStack() as early:
            q32 = early.enter_context(nc.sbuf_tensor("q32", [KVH * HD, CH, QW], F32))
            qr = early.enter_context(nc.sbuf_tensor("qr", [KVH * HD, CH, QW], F32))
            qp = [early.enter_context(nc.sbuf_tensor(f"qp{i}", [KVH * HD, 3, CH, QW], BF16)) for i in range(2)]
            loaded = sem("a_loaded")
            preset = sem("a_preset")
            q_mm = sem("q_mm")
            q_add = sem("q_add")
            q_hi = sem("q_hi")
            q_r1 = sem("q_r1")
            q_mid = sem("q_mid")
            q_lo = sem("q_lo")
            q_out = [sem(f"q_out{i}") for i in range(2)]
            x_bias = sem("x_bias")
            LOADS = 11
            with nc.Block() as block:
                @block.sync
                def _(sp):
                    for dst, src in ((ctx_t, a["x_t"].rearrange("(c p) t -> p c t", p=P)),
                                     (wq, a["wq"]), (bq, a["bq"])):
                        sp.dma_start(dst[:], src).then_inc(loaded, 16)
                    for dst, src in ((ident, a["ident"]), (wkv, a["wkv"]), (bkv, a["bkv"]),
                                     (wo, a["wo"]), (bo, a["bo"]), (den_sel, a["den_sel"]),
                                     (mask_sel, a["mask_sel"]), (x_nat, a["x_nat"])):
                        sp.dma_start(dst[:], src).then_inc(loaded, 16)
                    for c in range(B // CH):
                        sp.wait_ge(q_lo, c + 1)
                        sp.dma_start(q_scr[:, :, c * CH:(c + 1) * CH, :].rearrange("r d b n -> d r b n"),
                                     qp[c % 2][:]).then_inc(q_out[c % 2], 16)
                    for i in range(2):
                        sp.wait_ge(q_out[i], 16 * (B // CH // 2))

                @block.gpsimd
                def _(pool):
                    sets = [(ones[:], 1.0)]
                    for i in range(2):
                        sets += [(qs[i][:], 0.0), (ks[i][SROWS:MROWS], 1.0), (vp[i][:], 0.0),
                                 (vp[i][:, :, :, HD:HD + 1], 1.0)]
                    for n, (where, value) in enumerate(sets):
                        pool.memset(where, value).then_inc(preset, 1)
                        pool.wait_ge(preset, n + 1)

                @block.tensor
                def _(pe):
                    pe.wait_ge(loaded, 16 * LOADS)
                    for c in range(B // CH):
                        for g in range(G):
                            if c >= 1:
                                pe.wait_ge(q_add, G * (c - 1) + g + 1)
                            for k in range(KC):
                                mm = pe.matmul(ps[0:KVH * HD, g, 0:CW], wq[:, k, g, :],
                                               ctx_t[:, k, c * CW:(c + 1) * CW], start=(k == 0), stop=(k == KC - 1))
                            mm.then_inc(q_mm, 1)

                @block.vector
                def _(dve):
                    dve.wait_ge(loaded, 16 * LOADS)
                    for c in range(B // CH):
                        for g in range(G):
                            dve.wait_ge(q_mm, G * c + g + 1)
                            if c >= 1:
                                dve.wait_ge(q_hi, c)
                                dve.wait_ge(q_r1, c)
                            dve.tensor_scalar(q32[:, :, g * L:(g + 1) * L],
                                              ps[0:KVH * HD, g, 0:CW].rearrange("p (b l) -> p b l", l=L),
                                              bq[:, g:g + 1], float(HD) ** -0.5, ALU.add, ALU.mult).then_inc(q_add, 1)
                        dve.wait_ge(q_hi, c + 1)
                        if c >= 1:
                            dve.wait_ge(q_lo, c)
                        dve.tensor_tensor(qr[:], q32[:], qp[c % 2][:, 0], ALU.subtract).then_inc(q_r1, 1)
                        dve.wait_ge(q_mid, c + 1)
                        dve.tensor_tensor(qp[c % 2][:, 2], qr[:], qp[c % 2][:, 1], ALU.subtract).then_inc(q_lo, 1)
                    dve.tensor_copy(identb[:], ident[:]).then_inc(x_bias, 1)
                    dve.tensor_tensor(x_nat[:], x_nat[:], bo[:].unsqueeze(1).to_broadcast([P, PAIRS, E]),
                                      ALU.add).then_inc(x_bias, 1)
                    dve.wait_ge(x_bias, 2)

                @block.scalar
                def _(act):
                    for c in range(B // CH):
                        act.wait_ge(q_add, G * (c + 1))
                        if c >= 2:
                            act.wait_ge(q_out[c % 2], 16 * (c // 2))
                        act.activation(qp[c % 2][:, 0], q32[:], ACT.Copy).then_inc(q_hi, 1)
                        act.wait_ge(q_r1, c + 1)
                        act.activation(qp[c % 2][:, 1], qr[:], ACT.Copy).then_inc(q_mid, 1)

        ctx_in, mask_in, k_in, q_in, neg_in, k_out = map(sem, "ctx_in mask_in k_in q_in neg_in k_out".split())
        kv_mm, kv_read, split_done, rest_done, hi_done, mid_done = map(
            sem, "kv_mm kv_read split_done rest_done hi_done mid_done".split())
        vt_mm, vt_read, row_mm, row_read = map(sem, "vt_mm vt_read row_mm row_read".split())
        chain, neg_mm, negt_done = map(sem, "chain neg_mm negt_done".split())
        abs_done, flag_mm, flag_done = map(sem, "abs_done flag_mm flag_done".split())
        score_mm, probs_done, pv_mm, acc_read = map(sem, "score_mm probs_done pv_mm acc_read".split())
        den_mm, inv_done, norm_done, out_mm, x_done = map(sem, "den_mm inv_done norm_done out_mm x_done".split())
        CHAIN = 5
        q_view = q_scr.rearrange("r (j h d) b n -> r h d j b n", h=2, d=HD)
        k_view = k_scr.rearrange("i r (j d) s -> i r d j s", d=2 * HD)
        ctx_view = a["ctx_t"].rearrange("b (c p) s -> b p c s", p=P)
        m_view = a["mask0"]

        def at(ap, b):
            return ap[b] if isinstance(b, int) else ap[bass.ds(b, 1)].rearrange("o p s -> (o p) s")

        def at4(ap, b):
            return ap[b] if isinstance(b, int) else ap[bass.ds(b, 1)].rearrange("o p c s -> p (o c) s")

        def sp_body(sp, b, par, prev, cur, front, front2, ctx3):
            nx = 1 - par
            if front:
                if prev:
                    wait_apart(sp, passed, score_mm, 24 * b)
                sp.wait_ge(k_out, 16 * (b + 2))
                for s, r in enumerate(K_PIECES):
                    sp.dma_start(ks[nx][16 * s:16 * s + 16], k_view[nx, r]).then_inc(k_in, 16)
                for s, r in enumerate(Q_PIECES):
                    for h in range(2):
                        sp.dma_start(qs[nx][16 * s + HD * h:16 * s + HD * h + HD, :, h:h + 1, :],
                                     q_view[r, h][:, :, bass.ds(b + 1, 1), :]).then_inc(q_in, 16)
                for i in range(2):
                    sp.dma_start(mask[nx][i * L:(i + 1) * L], at(m_view, b + 1)).then_inc(mask_in, 16)
            if ctx3:
                sp.wait_ge(kv_mm, NC * (b + 3))
                sp.dma_start(ctx_t[:, :, 0:S], at4(ctx_view, b + 3)).then_inc(ctx_in, 16)
            if front2:
                wait_apart(sp, passed, split_done, b + 3)
                if not isinstance(b, int) or b >= 0:
                    sp.wait_ge(k_in, 16 * NS * (b + 1))
                sp.dma_start(k_scr[par].rearrange("r d s -> d r s"), k_piece[:]).then_inc(k_out, 16)
            if front:
                sp.wait_ge(negt_done, b + 2)
                for r in range(3):
                    sp.dma_start(qs[nx][SROWS + r:SROWS + r + 1].rearrange("p j h n -> p (j h n)"),
                                 neg_t[r * NR:(r + 1) * NR, :]).then_inc(neg_in, 16)

        def kv_project(pe, n):
            pe.wait_ge(ctx_in, 16 * (n + 1))
            for c in range(NC):
                bank = FRONT[c % 2]
                if c >= 2:
                    pe.wait_ge(kv_read, NC * n + c - 1)
                for k in range(KC):
                    mm = pe.matmul(ps[:, bank, 0:SC], wkv[:, k], ctx_t[:, k, c * SC:(c + 1) * SC],
                                   start=(k == 0), stop=(k == KC - 1))
                mm.then_inc(kv_mm, 1)

        def pe_scores(pe, b, t, par, any_mask):
            for j in range(0, NJ, 2):
                wait = 24 * b + 2 * (t - 1) + j // 2 + 1
                if not isinstance(wait, int) or wait > 0:
                    pe.wait_ge(probs_done, wait)

                def products(with_mask):
                    for i in (j, j + 1):
                        mm = pe.matmul(ps[0:ST, i, 0:PW], ks[par][:, i, t * ST:(t + 1) * ST],
                                       qs[par][:, i].rearrange("p h n -> p (h n)"), start=True, stop=not with_mask)
                        if with_mask:
                            mm = pe.matmul(ps[0:ST, i, 0:PW], mask[par][0:L, t * ST:(t + 1) * ST], mask_sel[:],
                                           start=False, stop=True)
                    mm.then_inc(score_mm, 1)
                with pe.If(any_mask):
                    products(True)
                with pe.Else():
                    products(False)

        def pe_pv(pe, b, t, par):
            if t == 0:
                pe.wait_ge(vt_read, 3 * (b + 1))
                if not isinstance(b, int) or b > 0:
                    pe.wait_ge(acc_read, b)
            for j in range(NJ):
                if j % 2 == 0:
                    pe.wait_ge(probs_done, 24 * b + 2 * t + j // 2 + 1)
                for h in range(2):
                    mm = pe.matmul(ps[32 * j:32 * j + 32, ACC, h * QW:(h + 1) * QW], vp[par][:, t, 2 * j + h, :],
                                   probs[t % 2][:, j, h * QW:(h + 1) * QW], start=(t == 0 and h == 0),
                                   stop=(t == NT - 1), skip_group_check=True)
            mm.then_inc(pv_mm, 1)

        def pe_rows(pe, n, par, lo, hi):
            for u in range(lo, hi):
                if u < 2:
                    pe.wait_ge(kv_read, NC * (n + 1))
                    pe.wait_ge(vt_read, 3 * (n + 1))
                else:
                    pe.wait_ge(row_read, NR * NC * n + u - 1)
                r, c = divmod(u, NC)
                j, h, gp = r // 4, r // 2 % 2, r % 2
                pe.matmul(ps[0:2 * L, FRONT[u % 2], 0:SC], qs[par][0:SROWS, j, h, gp * 2 * L:(gp + 1) * 2 * L],
                          ks[par][0:SROWS, j, c * SC:(c + 1) * SC], start=True, stop=True).then_inc(row_mm, 1)

        def pe_body(pe, b, par, prev, cur, front, front2, ctx3):
            nx = 1 - par
            if cur or prev:
                wait_apart(pe, passed, flag_done, b + 1 if cur else b)
            if prev:
                masked_prev = pe.value_load(flag[0:1, nx:nx + 1], min_val=0, max_val=1)
            if cur:
                masked_cur = pe.value_load(flag[0:1, par:par + 1], min_val=0, max_val=1)
            if cur:
                wait_apart(pe, passed, chain, CHAIN * (b + 1))
                pe.transpose(ps[0:3 * NR, MISC, :].bitcast(BF16)[:, 0:2 * L], neg_piece[:].rearrange("p r n -> p (r n)"),
                             identb[0:2 * L, 0:2 * L]).then_inc(neg_mm, 1)
            if prev:
                for i in range(2):
                    pe_scores(pe, b - 1, NT - 2 + i, nx, masked_prev)
                    pe_pv(pe, b - 1, NT - 3 + i, nx)
            if cur:
                pe.wait_ge(k_in, 16 * NS * (b + 1))
                pe.wait_ge(q_in, 32 * NS * (b + 1))
                pe.wait_ge(neg_in, 48 * (b + 1))
                pe_scores(pe, b, 0, par, masked_cur)
            if prev:
                pe_pv(pe, b - 1, NT - 1, nx)
            if front:
                pe.wait_ge(row_read, NR * NC * (b + 1)) if (not isinstance(b, int) or b >= 0) else None
                for c in range(3):
                    if c >= 2:
                        pe.wait_ge(vt_read, 3 * (b + 1) + c - 1)
                    pe.wait_ge(kv_read, NC * (b + 2))
                    for i in range(4):
                        t = 4 * c + i
                        mm = pe.transpose(ps[0:ST, FRONT[c % 2], i * P:(i + 1) * P], kv_t[:, t * ST:(t + 1) * ST],
                                          ident[:])
                    mm.then_inc(vt_mm, 1)
            if front2:
                pe.wait_ge(vt_read, 3 * (b + 2))
                kv_project(pe, b + 2)
            row_units = 0
            for t in range(1, NT - 2):
                if cur:
                    pe_scores(pe, b, t, par, masked_cur)
                    pe_pv(pe, b, t - 1, par)
                if front:
                    if t == 1:
                        pe.wait_ge(k_in, 16 * NS * (b + 2))
                        pe.wait_ge(q_in, 32 * NS * (b + 2))
                        pe.wait_ge(kv_read, NC * (b + 3 if front2 else b + 2))
                    upto = NR * NC * t // (NT - 3)
                    pe_rows(pe, b + 1, nx, row_units, upto)
                    row_units = upto
                if prev and t == 3:
                    pe.wait_ge(acc_read, b)
                    if cur:
                        pe.wait_ge(negt_done, b + 1)
                    else:
                        pe.wait_ge(x_done, b - 1)
                    pe.matmul(ps[:, MISC, 0:PW], den_sel[:], o_raw[:], start=True, stop=True).then_inc(den_mm, 1)
                if prev and t == 6:
                    pe.wait_ge(inv_done, b)
                    pe.wait_ge(norm_done, b + 1)
                    first = natural(1 - par)
                    for c in range(2 * G):
                        mm = pe.matmul(ps[first:first + L, MISC, 0:E], o_n[:, c * L:(c + 1) * L], wo[:, c],
                                       start=(c == 0), stop=(c == 2 * G - 1))
                    mm.then_inc(out_mm, 1)
                if front and t == 8:
                    if prev:
                        pe.wait_ge(x_done, b)
                    elif cur:
                        pe.wait_ge(negt_done, b + 1)
                    wait_apart(pe, passed, abs_done, b + 2)
                    pe.matmul(ps[0:1, MISC, 0:1], mask_sum[0:L], ones[0:L], start=True, stop=True).then_inc(flag_mm, 1)

        def act_scores(act, b, t):
            for i in range(2):
                act.wait_ge(score_mm, 24 * b + 2 * t + i + 1)
                wait = 12 * b + t - 1
                if not isinstance(wait, int) or wait > 0:
                    act.wait_ge(pv_mm, wait)
                act.activation(probs[t % 2][:, 2 * i:2 * i + 2, :], ps[0:ST, 2 * i:2 * i + 2, 0:PW],
                               ACT.Exp).then_inc(probs_done, 1)

        def kv_evacuate(act, n):
            for c in range(NC):
                act.wait_ge(kv_mm, NC * n + c + 1)
                act.activation(kv_t[:, c * SC:(c + 1) * SC], ps[:, FRONT[c % 2], 0:SC], ACT.Identity,
                               bias=bkv[:]).then_inc(kv_read, 1)

        def act_body(act, b, par, prev, cur, front, front2, ctx3):
            nx = 1 - par
            if prev:
                for i in range(2):
                    act_scores(act, b - 1, NT - 2 + i)
            if cur:
                act_scores(act, b, 0)
            if prev:
                act.wait_ge(pv_mm, NT * b)
                act.wait_ge(norm_done, b)
                act.activation(o_raw[:], ps[:, ACC, 0:PW], ACT.Copy).then_inc(acc_read, 1)
            if front2:
                act.wait_ge(split_done, b + 2)
                kv_evacuate(act, b + 2)
            for t in range(1, NT - 2):
                if cur:
                    act_scores(act, b, t)
                if front and t == 5:
                    act.wait_ge(mask_in, 32 * (b + 2))
                    if not isinstance(b, int) or b >= 0:
                        act.wait_ge(flag_mm, b + 1)
                    act.activation(mask_abs[0:L], mask[nx][0:L], ACT.Abs,
                                   accum_out=mask_sum[0:L]).then_inc(abs_done, 1)

        def dve_body(dve, b, par, prev, cur, front, front2, ctx3):
            nx = 1 - par
            if cur:
                dve.wait_ge(neg_mm, b + 1)
                if not isinstance(b, int) or b > 0:
                    dve.wait_ge(neg_in, 48 * b)
                dve.tensor_copy(neg_t[:], ps[0:3 * NR, MISC, :].bitcast(BF16)[:, 0:2 * L]).then_inc(negt_done, 1)
            if front:
                for c in range(3):
                    dve.wait_ge(vt_mm, 3 * (b + 1) + c + 1)
                    if prev and c == 0:
                        dve.wait_ge(pv_mm, NT * b)
                    dve.tensor_copy(vp[nx][:, 4 * c:4 * c + 4, :, 0:HD],
                                    ps[0:ST, FRONT[c % 2], :].rearrange("p (t h) -> p t h", t=4)[:, :, HALF:P]
                                    .rearrange("p t (k d) -> p t k d", d=HD)).then_inc(vt_read, 1)
                dve.wait_ge(mask_in, 32 * (b + 2))
            row_units = 0
            for t in range(1, NT - 2):
                if front:
                    upto = NR * NC * t // (NT - 3)
                    for u in range(row_units, upto):
                        r, c = divmod(u, NC)
                        wait_apart(dve, passed, row_mm, NR * NC * (b + 1) + u + 1)
                        dve.tensor_tensor_reduce(
                            out=masked[:, u % 2], in0=ps[0:2 * L, FRONT[u % 2], 0:SC], in1=mask[nx][:, c * SC:(c + 1) * SC],
                            scale=1.0, scalar=NEG_BIG, op0=ALU.add, op1=ALU.max,
                            accum_out=part_max[:, r, c:c + 1]).then_inc(row_read, 1)
                    row_units = upto
                if prev and t == 4:
                    dve.wait_ge(den_mm, b)
                    dve.wait_ge(norm_done, b)
                    dve.reciprocal(den_inv[:], ps[:, MISC, 0:PW]).then_inc(inv_done, 1)
                if prev and t == 7:
                    dve.wait_ge(out_mm, b + 1)
                    first = natural(1 - par)
                    tile = (b - 1) // 2
                    rows = x_nat[first:first + L, bass.ds(tile, 1), :].rearrange("p o e -> p (o e)")
                    dve.tensor_tensor(rows, ps[first:first + L, MISC, 0:E], rows, ALU.add).then_inc(x_done, 1)
                if front and t == 9:
                    dve.wait_ge(flag_mm, b + 2)
                    dve.tensor_scalar(flag[0:1, nx:nx + 1], ps[0:1, MISC, 0:1], 0.0, None,
                                      ALU.is_gt).then_inc(flag_done, 1)
            if front:
                k = CHAIN * (b + 1)
                dve.wait_ge(row_read, NR * NC * (b + 2))
                if not isinstance(b, int) or b >= 0:
                    dve.wait_ge(neg_mm, b + 1)
                dve.tensor_reduce(row_max[:], part_max[:], AX_X, ALU.max).then_inc(chain, 1)
                dve.wait_ge(chain, k + 1)
                dve.tensor_scalar(neg_piece[:, 0], row_max[:], -1.0, None, ALU.mult).then_inc(chain, 1)
                dve.wait_ge(chain, k + 2)
                dve.scalar_tensor_tensor(neg_rest[:], row_max[:], -1.0, neg_piece[:, 0], ALU.mult,
                                         ALU.subtract).then_inc(chain, 1)
                dve.wait_ge(chain, k + 3)
                dve.tensor_copy(neg_piece[:, 1], neg_rest[:]).then_inc(chain, 1)
                dve.wait_ge(chain, k + 4)
                dve.tensor_tensor(neg_piece[:, 2], neg_rest[:], neg_piece[:, 1], ALU.subtract).then_inc(chain, 1)

        def split_k(pool, n):
            kk = kv_t[0:KVH * HD]
            pool.wait_ge(kv_read, NC * (n + 1))
            wait = n
            if not isinstance(wait, int) or wait > 0:
                wait_apart(pool, passed, k_out, 16 * wait)
            pool.tensor_copy(k_piece[:, 0], kk).then_inc(hi_done, 1)
            pool.wait_ge(hi_done, n + 1)
            pool.tensor_tensor(k_rest[:], kk, k_piece[:, 0], ALU.subtract).then_inc(rest_done, 1)
            wait_apart(pool, passed, rest_done, n + 1)
            pool.tensor_copy(k_piece[:, 1], k_rest[:]).then_inc(mid_done, 1)
            pool.wait_ge(mid_done, n + 1)
            pool.tensor_tensor(k_piece[:, 2], k_rest[:], k_piece[:, 1], ALU.subtract).then_inc(split_done, 1)

        def pool_body(pool, b, par, prev, cur, front, front2, ctx3):
            if prev:
                pool.wait_ge(inv_done, b)
                pool.wait_ge(out_mm, b)
                pool.tensor_tensor(o_n[:], o_raw[:], den_inv[:], ALU.mult).then_inc(norm_done, 1)
            if front2:
                split_k(pool, b + 2)

        def all_bodies(eng, body):
            def one(b, par):
                known = isinstance(b, int)
                body(eng, b, par, not known or b >= 1, not known or 0 <= b < B, not known or b + 1 < B,
                     not known or b + 2 < B, not known or b + 3 < B)
            one(-1, 1)
            one(0, 0)
            with eng.Fori(1, B - 4, 2) as b:
                one(b, 1)
                one(b + 1, 0)
            for b in range(B - 3, B + 1):
                one(b, b % 2)

        with nc.Block() as block:
            @block.sync
            def _(sp):
                sp.dma_start(ctx_t[:, :, 0:S], ctx_view[0]).then_inc(ctx_in, 16)
                sp.wait_ge(kv_mm, NC)
                sp.dma_start(ctx_t[:, :, 0:S], ctx_view[1]).then_inc(ctx_in, 16)
                sp.wait_ge(split_done, 1)
                sp.dma_start(k_scr[0].rearrange("r d s -> d r s"), k_piece[:]).then_inc(k_out, 16)
                all_bodies(sp, sp_body)
                sp.wait_ge(k_out, 16 * B)

            @block.tensor
            def _(pe):
                pe.sem_inc(out_mm, 1)
                kv_project(pe, 0)
                all_bodies(pe, pe_body)

            @block.scalar
            def _(act):
                kv_evacuate(act, 0)
                all_bodies(act, act_body)

            @block.vector
            def _(dve):
                all_bodies(dve, dve_body)

            @block.gpsimd
            def _(pool):
                pool.sem_inc(norm_done, 1)
                split_k(pool, 0)
                all_bodies(pool, pool_body)
        clear(nc, sems)


CB = 8
CP = CB // 2
N = CB * L
H, HS = 32, 8
MIX = (1, 0, 2, 3, 4)
VEC = ("ln1_w", "ln1_b", "ln2_w", "ln2_b", "maa_x", "m0", "m1", "m2", "m3", "m4", "td", "gn_w", "gn_b", "u",
       "fmk", "fmr")
LN_EPS = 1e-5
PRODUCTS = {"xt": 2, "lora": 2, "mix": 10, "dec1": 1, "dec2": 2, "key": 2, "val": 2, "rec": 2, "gate": 2,
            "vb": 16, "bonus": 2, "y": 2, "mean": 2, "var": 2, "att": 2, "xt2": 2, "fk": 2, "fr": 2, "fv": 2}


def product_order():
    out = [("xt", 0), ("xt", 1), ("lora", 0), ("lora", 1)]
    projections = {0: ["key"], 1: ["dec1", "dec2"], 2: ["val"], 3: ["rec"], 4: ["gate"]}
    for n in range(len(MIX) + 1):
        if n < len(MIX):
            out += [("mix", 2 * n), ("mix", 2 * n + 1)]
        if n >= 1:
            for name in projections[MIX[n - 1]]:
                out += [(name, i) for i in range(PRODUCTS[name])]
    out += [("vb", i) for i in range(HS + 2)] + [("bonus", 0)]
    out += [("vb", i) for i in range(HS + 2, KC * HS)] + [("bonus", 1)]
    for name in ("mean", "var", "att", "xt2", "fk", "fr", "fv"):
        out += [(name, i) for i in range(2)]
    return out


def rwkv(nc, x_nat, a, tag, after_layer0, passed):
    sems = []
    with ExitStack() as ctx:
        def sb(name, shape, dt=F32):
            return ctx.enter_context(nc.sbuf_tensor(f"{tag}_{name}", shape, dt))

        def sem(name):
            sems.append(ctx.enter_context(nc.semaphore(f"{tag}_{name}")))
            return sems[-1]

        ident = sb("ident", [P, P])
        vec = sb("vec", [P, KC, len(VEC)])
        w1 = sb("w1", [P, KC, 2 * P])
        w2 = sb("w2", [P, 5, E])
        dw1 = sb("dw1", [P, KC, P])
        dw2 = sb("dw2", [P, E])
        wr, wk, wv, wg, wo, fk, fr, fv = [sb(n, [P, KC, E]) for n in "wr wk wv wg wo fk fr fv".split()]
        vsel = sb("vsel", [P, HS, P])
        osel = sb("osel", [P, HS, P])
        head_sum = sb("head_sum", [P, P])
        head_mean = sb("head_mean", [P, P])
        st = sb("st", [P, 2, KC, B])
        s0 = sb("s0", [P, KC, HS, B])
        loads = [(ident, "ident"), (vec, tag + "vec"), (w1, tag + "w1"), (w2, tag + "w2"), (dw1, tag + "dw1"),
                 (dw2, tag + "dw2"), (wr, tag + "wr"), (wk, tag + "wk"), (wv, tag + "wv"), (wg, tag + "wg"),
                 (wo, tag + "wo"), (fk, tag + "fk"), (fr, tag + "fr"), (fv, tag + "fv"), (vsel, "vsel"),
                 (osel, "osel"), (head_sum, "head_sum"), (head_mean, "head_mean"), (st, "st"), (s0, "s0")]
        if after_layer0:
            ln0_g, ln0_b = sb("ln0_g", [P, E]), sb("ln0_b", [P, E])
            loads += [(ln0_g, "ln0_g"), (ln0_b, "ln0_b")]
        eps = sb("eps", [P, 2])
        stats = sb("stats", [P, CP, 6])
        mv = sb("mv", [P, CP, 2])
        sd = sb("sd", [P, CP])
        rstd = sb("rstd", [P, CP])
        shift = sb("shift", [P, CP])
        xhat = sb("xhat", [P, CP, E])
        xn = sb("xn", [P, KC, N])
        sx = sb("sx", [P, KC, N])
        xx = sb("xx", [P, KC, N])
        th = sb("th", [P, KC, N])
        part = sb("part", [P, 2, KC, N])
        mixed = sb("mixed", [P, 2, KC, N])
        hw = sb("hw", [P, N])
        dec_e = sb("dec_e", [P, KC, N])
        w = sb("w", [P, KC, N])
        kt, vt, rt, gt = [sb(n, [P, KC, N]) for n in ("kt", "vt", "rt", "gt")]
        g_th = sb("g_th", [P, KC, N])
        kv = sb("kv", [P, 3, N])
        state = sb("state", [P, 3, N])
        rs = sb("rs", [P, 3, N])
        ruk = sb("ruk", [P, KC, N])
        cv = sb("cv", [P, KC, N])
        yo = sb("yo", [P, KC, N])
        dev = sb("dev", [P, KC, N])
        sq = sb("sq", [P, KC, N])
        gsd = sb("gsd", [P, KC, N])
        grs = sb("grs", [P, KC, N])
        og = sb("og", [P, KC, N + 8])
        xk2 = sb("xk2", [P, KC, N])
        xr2 = sb("xr2", [P, KC, N + 8])
        relu = sb("relu", [P, KC, N])
        kk = sb("kk", [P, KC, N + 8])
        r_th = sb("r_th", [P, 2, 2 * E])
        rv = sb("rv", [P, 2, 2 * E])
        ps = ctx.enter_context(nc.psum_tensor(f"ps_{tag}", [P, 8, 512], F32))

        made = {n: sem(n + "_made") for n in PRODUCTS}
        used = {n: sem(n + "_used") for n in PRODUCTS}
        names = ("loaded preset stat aggr0 aggr1 aggr2 sd0 sd1 sd2 r0 r1 r2 z0 z1 z2 ln0a ln0b ln0c xhat1 xhat2 "
                 "sxa sxb xx part mixed kv_first state rs ruk sq grs og xk2 xr2 "
                 "sx2a sx2b kk x2 dec_w g_th summed").split()
        s = {n: sem(n) for n in names}
        order = product_order()
        bank = {}
        before = {}
        last = {}
        for lap in range(2):
            n = 0
            for unit in order:
                b = n % 7
                n += 1
                before[unit] = (last.get(b), lap)
                bank[unit] = b
                last[b] = (unit, lap)
        Y_BANK = 7

        def v(k, name):
            i = VEC.index(name)
            return vec[:, k, i:i + 1]

        def by_batch(ap):
            return ap.rearrange("p (b l) -> p b l", l=L)

        with nc.Block() as block:
            @block.sync
            def _(sp):
                for dst, name in loads:
                    sp.dma_start(dst[:], a[name]).then_inc(s["loaded"], 16)
                sp.wait_ge(s["loaded"], 16 * len(loads))

            @block.tensor
            def _(pe):
                pe.wait_ge(s["loaded"], 16 * len(loads))
                pe.wait_ge(s["preset"], 6)
                cell = {}

                def room(unit, c):
                    (prev, prev_lap), lap = before[unit]
                    name, i = prev
                    count = PRODUCTS[name]
                    if prev_lap == lap:
                        pe.wait_ge(used[name], count * c + i + 1)
                    elif not isinstance(c, int) or c > 0:
                        pe.wait_ge(used[name], count * c)

                def out(unit, rows=P, n=N):
                    return ps[0:rows, bank[unit], 0:n]

                def project(unit, c, w_sb, x_sb, m):
                    room(unit, c)
                    for k in range(KC):
                        mm = pe.matmul(out(unit), w_sb[:, k, m * P:(m + 1) * P], x_sb[:, k, 0:N],
                                       start=(k == 0), stop=(k == KC - 1))
                    mm.then_inc(made[unit[0]], 1)

                def natural_rows_of(unit, c, x_sb, w_sb):
                    room(unit, c)
                    i = unit[1]
                    for g in range(2):
                        for r in range(2):
                            t0 = ((2 * i + g) * 2 + r) * L
                            for k in range(KC):
                                mm = pe.matmul(ps[HALF * r:HALF * r + HALF, bank[unit], g * E:(g + 1) * E],
                                               x_sb[:, k, t0:t0 + HALF], w_sb[:, k, :],
                                               start=(k == 0), stop=(k == KC - 1))
                    mm.then_inc(made[unit[0]], 1)

                def turn(unit, c):
                    room(unit, c)
                    for g in range(CP):
                        mm = pe.transpose(ps[:, bank[unit], g * P:(g + 1) * P],
                                          xhat[:, g, unit[1] * P:(unit[1] + 1) * P], ident[:])
                    mm.then_inc(made[unit[0]], 1)

                def chunk(c):
                    for unit in order:
                        name, i = unit
                        if name == "xt":
                            pe.wait_ge(s["xhat1"], CP * (c + 1))
                            turn(unit, c)
                        elif name == "xt2":
                            pe.wait_ge(s["xhat2"], CP * (c + 1))
                            turn(unit, c)
                        elif name == "lora":
                            pe.wait_ge(s["xx"], 2 * (c + 1))
                            project(unit, c, w1, xx, i)
                        elif name == "mix":
                            j = MIX[i // 2]
                            pe.wait_ge(used["lora"], 2 * (c + 1))
                            room(unit, c)
                            pe.matmul(out(unit), w2[:, j, (i % 2) * P:(i % 2 + 1) * P], th[:, j // 4, :],
                                      start=True, stop=True).then_inc(made["mix"], 1)
                        elif name in ("dec1", "key", "val", "rec", "gate"):
                            n = MIX.index({"dec1": 1, "key": 0, "val": 2, "rec": 3, "gate": 4}[name])
                            pe.wait_ge(s["mixed"], 5 * c + n + 1)
                            w_sb = {"dec1": dw1, "key": wk, "val": wv, "rec": wr, "gate": wg}[name]
                            project(unit, c, w_sb, mixed[:, n % 2], i)
                        elif name == "dec2":
                            pe.wait_ge(used["dec1"], c + 1)
                            room(unit, c)
                            pe.matmul(out(unit), dw2[:, i * P:(i + 1) * P], hw[:], start=True,
                                      stop=True).then_inc(made["dec2"], 1)
                        elif name == "vb":
                            k, j = i // HS, i % HS
                            if j == 0:
                                pe.wait_ge(used["val"], 2 * c + k + 1)
                            room(unit, c)
                            pe.matmul(out(unit), vsel[:, j], vt[:, k], start=True, stop=True).then_inc(made["vb"], 1)
                            if i >= 2:
                                sum_state(c, i - 2)
                        elif name == "bonus":
                            pe.wait_ge(s["ruk"], 2 * c + i + 1)
                            room(unit, c)
                            pe.matmul(out(unit), head_sum[:], ruk[:, i], start=True, stop=True)\
                              .then_inc(made["bonus"], 1)
                            if i == 1:
                                sum_state(c, KC * HS - 2)
                                sum_state(c, KC * HS - 1)
                        elif name == "mean":
                            pe.wait_ge(used["y"], 2 * c + i + 1)
                            room(unit, c)
                            pe.matmul(out(unit), head_mean[:], yo[:, i], start=True, stop=True)\
                              .then_inc(made["mean"], 1)
                        elif name == "var":
                            pe.wait_ge(s["sq"], 2 * c + i + 1)
                            room(unit, c)
                            pe.matmul(out(unit), head_mean[:], sq[:, i], start=True, stop=True)\
                              .then_inc(made["var"], 1)
                        elif name == "att":
                            pe.wait_ge(s["og"], 2 * (c + 1))
                            natural_rows_of(unit, c, og, wo)
                        elif name == "fk":
                            pe.wait_ge(s["xk2"], 2 * (c + 1))
                            project(unit, c, fk, xk2, i)
                        elif name == "fr":
                            pe.wait_ge(s["xr2"], 2 * (c + 1))
                            natural_rows_of(unit, c, xr2, fr)
                        elif name == "fv":
                            pe.wait_ge(s["kk"], 2 * (c + 1))
                            natural_rows_of(unit, c, kk, fv)

                def sum_state(c, i):
                    k, j = divmod(i, HS)
                    if j == 0 and (not isinstance(c, int) or c + k > 0):
                        pe.wait_ge(used["y"], 2 * c + k)
                    pe.wait_ge(s["rs"], 16 * c + HS * k + j + 1)
                    mm = pe.matmul(ps[:, Y_BANK, 0:N], osel[:, j], rs[:, (HS * k + j) % 3], start=(j == 0),
                                   stop=(j == HS - 1))
                    mm.then_inc(s["summed"], 1)

                chunk(0)
                with pe.Fori(1, B // CB) as c:
                    chunk(c)

            @block.scalar
            def _(act):
                act.wait_ge(s["loaded"], 16 * len(loads))
                act.wait_ge(s["preset"], 6)

                def deviation(c, n, which):
                    act.wait_ge(s[f"aggr{n}"], CP * (c + 1))
                    act.activation(sd[:], mv[:, :, 1], ACT.Sqrt, bias=eps[:, which:which + 1]).then_inc(s[f"sd{n}"], 1)

                def read(name, c, i, out_ap, func, in_ap=None, **more):
                    act.wait_ge(made[name], PRODUCTS[name] * c + i + 1)
                    in_ap = ps[:, bank[name, i], 0:N] if in_ap is None else in_ap
                    return act.activation(out_ap, in_ap, func, **more)

                def chunk(c):
                    if after_layer0:
                        deviation(c, 0, 1)
                    deviation(c, 1, 0)
                    for k in range(KC):
                        src = ps[:, bank["xt", k], :].rearrange("p (b l) -> p b l", l=HALF)[:, :, 0:L]
                        read("xt", c, k, by_batch(xn[:, k]), ACT.Identity, src, scale=v(k, "ln1_w"),
                             bias=v(k, "ln1_b")).then_inc(used["xt"], 1)
                    for i in range(2):
                        read("lora", c, i, th[:, i], ACT.Tanh).then_inc(used["lora"], 1)
                    read("dec1", c, 0, hw[:], ACT.Tanh).then_inc(used["dec1"], 1)
                    for k in range(KC):
                        read("dec2", c, k, dec_e[:, k], ACT.Exp, bias=v(k, "td")).then_inc(used["dec2"], 1)
                    for k in range(KC):
                        act.wait_ge(used["dec2"], 2 * c + k + 1)
                        act.activation(by_batch(w[:, k])[:, :, 1:L], by_batch(dec_e[:, k])[:, :, 0:L - 1], ACT.Exp,
                                       scale=-1.0).then_inc(s["dec_w"], 1)
                    for name, dst in (("key", kt), ("val", vt), ("rec", rt)):
                        for k in range(KC):
                            read(name, c, k, dst[:, k], ACT.Copy).then_inc(used[name], 1)
                    for k in range(KC):
                        read("gate", c, k, g_th[:, k], ACT.Tanh, scale=0.5).then_inc(s["g_th"], 1)
                    for k in range(KC):
                        act.wait_ge(used["mean"], 2 * c + k + 1)
                        act.activation(sq[:, k], dev[:, k], ACT.Square).then_inc(s["sq"], 1)
                    for k in range(KC):
                        read("var", c, k, gsd[:, k], ACT.Sqrt, bias=eps[:, 0:1]).then_inc(used["var"], 1)
                    deviation(c, 2, 0)
                    for k in range(KC):
                        src = ps[:, bank["xt2", k], :].rearrange("p (b l) -> p b l", l=HALF)[:, :, 0:L]
                        read("xt2", c, k, by_batch(xn[:, k]), ACT.Identity, src, scale=v(k, "ln2_w"),
                             bias=v(k, "ln2_b")).then_inc(used["xt2"], 1)
                    for k in range(KC):
                        read("fk", c, k, relu[:, k], ACT.Relu).then_inc(used["fk"], 1)
                    for i in range(2):
                        read("fr", c, i, r_th[:, i], ACT.Tanh, ps[:, bank["fr", i], :], scale=0.5)\
                            .then_inc(used["fr"], 1)

                with act.Fori(0, B // CB) as c:
                    chunk(c)

            @block.vector
            def _(dve):
                dve.wait_ge(s["loaded"], 16 * len(loads))
                dve.wait_ge(s["preset"], 6)

                def normalize(c, n, rows, done):
                    for g in range(CP):
                        dve.bn_stats(stats[:, g], rows[:, g]).then_inc(s["stat"], 1)
                    per = CP * (3 if after_layer0 else 2)
                    first = {0: 0, 1: CP if after_layer0 else 0, 2: per - CP}[n]
                    wait_apart(dve, passed, s["stat"], per * c + first + CP)
                    for g in range(CP):
                        dve.bn_aggr(mv[:, g], stats[:, g]).then_inc(s[f"aggr{n}"], 1)
                    dve.wait_ge(s[f"sd{n}"], c + 1)
                    dve.reciprocal(rstd[:], sd[:]).then_inc(s[f"r{n}"], 1)
                    dve.wait_ge(s[f"r{n}"], c + 1)
                    dve.scalar_tensor_tensor(shift[:], mv[:, :, 0], -1.0, rstd[:], ALU.mult, ALU.mult)\
                       .then_inc(s[f"z{n}"], 1)
                    dve.wait_ge(s[f"z{n}"], c + 1)
                    for g in range(CP):
                        dve.tensor_scalar(xhat[:, g], rows[:, g], rstd[:, g:g + 1], shift[:, g:g + 1],
                                          ALU.mult, ALU.add).then_inc(s[done], 1)

                def token_shift(c, row, xa, xb):
                    name = "xt" if row == 1 else "xt2"
                    dve.wait_ge(used[name], 2 * (c + 1))
                    x4 = xn[:].rearrange("p k (b l) -> p k b l", l=L)
                    s4 = sx[:].rearrange("p k (b l) -> p k b l", l=L)
                    dve.tensor_tensor(s4[:, :, :, 1:L], x4[:, :, :, 0:L - 1], x4[:, :, :, 1:L], ALU.subtract)\
                       .then_inc(s[xa], 1)
                    dve.tensor_tensor(s4[:, :, :, 0], st[:, row][:, :, bass.ds(c * CB, CB)], x4[:, :, :, 0],
                                      ALU.subtract).then_inc(s[xb], 1)
                    dve.wait_ge(s[xa], c + 1)
                    dve.wait_ge(s[xb], c + 1)

                def chunk(c):
                    rows = x_nat[:, bass.ds(c * CP, CP), :]
                    if after_layer0:
                        normalize(c, 0, rows, "ln0a")
                        dve.wait_ge(s["ln0a"], CP * (c + 1))
                        dve.tensor_tensor(xhat[:], xhat[:], ln0_g[:].unsqueeze(1).to_broadcast([P, CP, E]), ALU.mult)\
                           .then_inc(s["ln0b"], 1)
                        dve.wait_ge(s["ln0b"], c + 1)
                        dve.tensor_tensor(rows, xhat[:], ln0_b[:].unsqueeze(1).to_broadcast([P, CP, E]), ALU.add)\
                           .then_inc(s["ln0c"], 1)
                        wait_apart(dve, passed, s["ln0c"], c + 1)
                    normalize(c, 1, rows, "xhat1")
                    token_shift(c, 1, "sxa", "sxb")
                    for k in range(KC):
                        dve.scalar_tensor_tensor(xx[:, k], sx[:, k], v(k, "maa_x"), xn[:, k], ALU.mult, ALU.add)\
                           .then_inc(s["xx"], 1)
                    for n, j in enumerate(MIX):
                        for k in range(KC):
                            dve.wait_ge(made["mix"], 10 * c + 2 * n + k + 1)
                            if n >= 2:
                                dve.wait_ge(s["mixed"], 5 * c + n - 1)
                            dve.scalar_tensor_tensor(part[:, n % 2, k], ps[:, bank["mix", 2 * n + k], 0:N],
                                                     v(k, f"m{j}"), sx[:, k], ALU.add, ALU.mult)\
                               .then_inc(used["mix"], 1)
                    dve.wait_ge(used["rec"], 2 * (c + 1))
                    for k in range(KC):
                        dve.scalar_tensor_tensor(ruk[:, k], rt[:, k], v(k, "u"), kt[:, k], ALU.mult, ALU.mult)\
                           .then_inc(s["ruk"], 1)
                    for k in range(KC):
                        dve.wait_ge(made["gate"], 2 * c + k + 1)
                        dve.wait_ge(s["g_th"], 2 * c + k + 1)
                        dve.scalar_tensor_tensor(gt[:, k], g_th[:, k], 1.0, ps[:, bank["gate", k], 0:N],
                                                 ALU.add, ALU.mult).then_inc(used["gate"], 1)

                    def head_output(k):
                        dve.wait_ge(made["bonus"], 2 * c + k + 1)
                        dve.tensor_tensor(cv[:, k], ps[:, bank["bonus", k], 0:N], vt[:, k], ALU.mult)\
                           .then_inc(used["bonus"], 1)
                        dve.wait_ge(s["summed"], 16 * c + HS * (k + 1))
                        dve.wait_ge(used["bonus"], 2 * c + k + 1)
                        dve.tensor_tensor(yo[:, k], ps[:, Y_BANK, 0:N], cv[:, k], ALU.add).then_inc(used["y"], 1)

                    dve.wait_ge(s["dec_w"], 2 * (c + 1))
                    for i in range(KC * HS + 1):
                        if i < KC * HS:
                            k, j = divmod(i, HS)
                            dve.wait_ge(made["vb"], 16 * c + i + 1)
                            if i >= 3:
                                dve.wait_ge(s["state"], 16 * c + i - 2)
                            dve.tensor_tensor(by_batch(kv[:, i % 3])[:, :, 1:L], by_batch(kt[:, k])[:, :, 0:L - 1],
                                              by_batch(ps[:, bank["vb", i], 0:N])[:, :, 0:L - 1], ALU.mult)\
                               .then_inc(used["vb"], 1)
                        if i >= 1:
                            m = i - 1
                            k = m // HS
                            dve.wait_ge(used["vb"], 16 * c + m + 1)
                            dve.wait_ge(s["kv_first"], 16 * c + m + 1)
                            if m >= 3:
                                dve.wait_ge(s["rs"], 16 * c + m - 2)
                            dve.tensor_tensor_scan(state[:, m % 3], w[:, k], kv[:, m % 3], 0.0, ALU.mult, ALU.add)\
                               .then_inc(s["state"], 1)
                        if i == HS + 2:
                            head_output(0)
                    head_output(1)
                    for k in range(KC):
                        dve.wait_ge(made["mean"], 2 * c + k + 1)
                        dve.tensor_tensor(dev[:, k], yo[:, k], ps[:, bank["mean", k], 0:N], ALU.subtract)\
                           .then_inc(used["mean"], 1)
                    for k in range(KC):
                        dve.wait_ge(used["var"], 2 * c + k + 1)
                        dve.reciprocal(grs[:, k], gsd[:, k]).then_inc(s["grs"], 1)
                        dve.wait_ge(s["grs"], 3 * (2 * c + k) + 1)
                        dve.tensor_tensor(yo[:, k], dev[:, k], grs[:, k], ALU.mult).then_inc(s["grs"], 1)
                        dve.wait_ge(s["grs"], 3 * (2 * c + k) + 2)
                        dve.tensor_scalar(yo[:, k], yo[:, k], v(k, "gn_w"), v(k, "gn_b"), ALU.mult, ALU.add)\
                           .then_inc(s["grs"], 1)
                        dve.wait_ge(s["grs"], 3 * (2 * c + k) + 3)
                        dve.scalar_tensor_tensor(og[:, k, 0:N], yo[:, k], 0.5, gt[:, k], ALU.mult, ALU.mult)\
                           .then_inc(s["og"], 1)
                    for i in range(2):
                        dve.wait_ge(made["att"], 2 * c + i + 1)
                        two = x_nat[:, bass.ds(c * CP + 2 * i, 2), :]
                        dve.tensor_tensor(two, ps[:, bank["att", i], :].rearrange("p (g e) -> p g e", g=2), two,
                                          ALU.add).then_inc(used["att"], 1)
                    wait_apart(dve, passed, used["att"], 2 * (c + 1))
                    normalize(c, 2, rows, "xhat2")
                    token_shift(c, 0, "sx2a", "sx2b")
                    for name, dst, vname in (("xk2", xk2, "fmk"), ("xr2", xr2, "fmr")):
                        for k in range(KC):
                            dve.scalar_tensor_tensor(dst[:, k, 0:N], sx[:, k], v(k, vname), xn[:, k], ALU.mult,
                                                     ALU.add).then_inc(s[name], 1)
                    for i in range(2):
                        dve.wait_ge(made["fv"], 2 * c + i + 1)
                        dve.wait_ge(used["fr"], 2 * c + i + 1)
                        dve.scalar_tensor_tensor(rv[:, i], r_th[:, i], 1.0, ps[:, bank["fv", i], :], ALU.add,
                                                 ALU.mult).then_inc(used["fv"], 1)
                    for i in range(2):
                        dve.wait_ge(used["fv"], 2 * c + i + 1)
                        two = x_nat[:, bass.ds(c * CP + 2 * i, 2), :]
                        dve.scalar_tensor_tensor(two, rv[:, i].rearrange("p (g e) -> p g e", g=2), 0.5, two,
                                                 ALU.mult, ALU.add).then_inc(s["x2"], 1)
                    dve.wait_ge(s["x2"], 2 * (c + 1))

                with dve.Fori(0, B // CB) as c:
                    chunk(c)

            @block.gpsimd
            def _(pool):
                sets = [(eps[:, 0:1], LN_EPS), (eps[:, 1:2], 1e-6), (w[:], 0.0), (og[:, :, N:N + 8], 0.0),
                        (xr2[:, :, N:N + 8], 0.0), (kk[:, :, N:N + 8], 0.0)]
                for n, (where, value) in enumerate(sets):
                    pool.memset(where, value).then_inc(s["preset"], 1)
                    pool.wait_ge(s["preset"], n + 1)
                pool.wait_ge(s["loaded"], 16 * len(loads))

                def chunk(c):
                    for n in range(len(MIX)):
                        pool.wait_ge(used["mix"], 10 * c + 2 * n + 2)
                        if n >= 2:
                            name = ("dec1", "key", "val")[n - 2]
                            pool.wait_ge(made[name], PRODUCTS[name] * (c + 1))
                        pool.tensor_tensor(mixed[:, n % 2], part[:, n % 2], xn[:], ALU.add).then_inc(s["mixed"], 1)
                    pool.wait_ge(used["rec"], 2 * (c + 1))
                    for i in range(KC * HS + 1):
                        if i < KC * HS:
                            k, j = divmod(i, HS)
                            if i >= 3:
                                pool.wait_ge(s["state"], 16 * c + i - 2)
                            pool.tensor_copy(by_batch(kv[:, i % 3])[:, :, 0], s0[:, k, j, :][:, bass.ds(c * CB, CB)])\
                                .then_inc(s["kv_first"], 1)
                        if i >= 1:
                            m = i - 1
                            k = m // HS
                            pool.wait_ge(s["state"], 16 * c + m + 1)
                            if m >= 3:
                                pool.wait_ge(s["summed"], 16 * c + m - 2)
                            pool.tensor_tensor(rs[:, m % 3], rt[:, k], state[:, m % 3], ALU.mult).then_inc(s["rs"], 1)
                    for k in range(KC):
                        pool.wait_ge(used["fk"], 2 * c + k + 1)
                        pool.tensor_tensor(kk[:, k, 0:N], relu[:, k], relu[:, k], ALU.mult).then_inc(s["kk"], 1)

                with pool.Fori(0, B // CB) as c:
                    chunk(c)
        clear(nc, sems)


NH2, HD2 = 16, 16
NQ = 4
SQ = S // NQ
TQ = SQ // ST
NP = NH2 // 2
SLOT = NH2 // KC * L
TILES = NQ * TQ + 1
S2 = S + L
MASKED = -1.0e30
RMS_EPS = 1e-6
FF = 4 * E
FC = FF // P


def latent_attention(nc, x_nat, y_nat, a, passed):
    mb_scr = nc.dram_tensor("mb_scr", [B, NQ, SQ], F32).ap()
    sems = []
    with ExitStack() as ctx:
        def sb(name, shape, dt=F32):
            return ctx.enter_context(nc.sbuf_tensor("c_" + name, shape, dt))

        def sem(name):
            sems.append(ctx.enter_context(nc.semaphore("c_" + name)))
            return sems[-1]

        ident = sb("ident", [P, P])
        identb = sb("identb", [P, P], BF16)
        kv_w = sb("kv_w", [P, KC, 2 * E])
        kv_b = sb("kv_b", [P, 4])
        q_w = sb("q_w", [P, KC, E])
        q_b = sb("q_b", [P, KC])
        out_w = sb("out_w", [P, KC, E])
        out_b = sb("out_b", [P, E])
        head_scale = sb("head_scale", [P, 8])
        odd_mask = sb("odd_mask", [P, 2])
        qt = sb("qt", [P, KC, T])
        kv_lat = sb("kv_lat", [P, 4, T])
        mask_i = sb("mask_i", [P, SQ], I32)
        mask_b = sb("mask_b", [P, SQ])
        mask_a = sb("mask_a", [P, SQ])
        active = sb("active", [P, 1])
        flags = sb("flags", [1, P], I32)
        mask_ti = sb("mask_ti", [ST, B, NT], I32)
        bias_t = sb("bias_t", [ST, B, NT])
        ps = ctx.enter_context(nc.psum_tensor("ps_c", [P, 8, 512], F32))
        loads = [(ident, "ident"), (kv_w, "c_kv_w"), (kv_b, "c_kv_b"), (q_w, "c_q_w"),
                 (q_b, "c_q_b"), (out_w, "c_out_w"), (out_b, "c_out_b"), (head_scale, "head_scale"),
                 (odd_mask, "odd_mask"), (mask_i, "mask_q"), (mask_ti, "mask_t")]

        with ExitStack() as early:
            x_t = early.enter_context(nc.sbuf_tensor("c_x_t", [P, KC, T], F32))
            loaded, turned, copied, made, kept, neg, act_row, act_t, fl, bt, yb, mb_out = [
                sem("0_" + n)
                for n in "loaded turned copied made kept neg act_row act_t fl bt yb mb_out".split()]
            CW = T // 4
            G4 = PAIRS // 4
            UNITS = [(c, m) for c in range(4) for m in range(6)]
            with nc.Block() as block:
                @block.sync
                def _(sp):
                    for dst, name in loads:
                        sp.dma_start(dst[:], a[name]).then_inc(loaded, 16)
                    sp.wait_ge(neg, 1)
                    sp.dma_start(mb_scr.rearrange("b q s -> (b q) s"), mask_b[:]).then_inc(mb_out, 16)
                    sp.wait_ge(mb_out, 16)

                @block.tensor
                def _(pe):
                    pe.wait_ge(loaded, 16 * len(loads))
                    for c in range(4):
                        for k in range(KC):
                            for g in range(G4):
                                mm = pe.transpose(ps[:, 2 * c + k, g * P:(g + 1) * P],
                                                  x_nat[:, c * G4 + g, k * P:(k + 1) * P], ident[:])
                            mm.then_inc(turned, 1)
                    for n, (c, m) in enumerate(UNITS):
                        pe.wait_ge(copied, 2 * c + 2)
                        if n < 8:
                            pe.wait_ge(copied, n + 1)
                        else:
                            pe.wait_ge(kept, n - 7)
                        for k in range(KC):
                            w = q_w[:, k, m * P:(m + 1) * P] if m < 2 else kv_w[:, k, (m - 2) * P:(m - 1) * P]
                            mm = pe.matmul(ps[:, n % 8, 0:CW], w, x_t[:, k, c * CW:(c + 1) * CW],
                                           start=(k == 0), stop=(k == KC - 1))
                        mm.then_inc(made, 1)
                    pe.wait_ge(act_row, 1)
                    pe.wait_ge(kept, len(UNITS) - 7)
                    pe.transpose(ps[0:1, 0, 0:P], active[:], ident[:]).then_inc(act_t, 1)

                @block.scalar
                def _(act):
                    act.wait_ge(loaded, 16 * len(loads))
                    for c in range(4):
                        for k in range(KC):
                            act.wait_ge(turned, 2 * c + k + 1)
                            act.activation(x_t[:, k, c * CW:(c + 1) * CW].rearrange("p (b l) -> p b l", l=L),
                                           ps[:, 2 * c + k, :].rearrange("p (b l) -> p b l", l=HALF)[:, :, 0:L],
                                           ACT.Copy).then_inc(copied, 1)
                    for n, (c, m) in enumerate(UNITS):
                        act.wait_ge(made, n + 1)
                        if m < 2:
                            dst, bias = qt[:, m, c * CW:(c + 1) * CW], q_b[:, m:m + 1]
                        else:
                            dst, bias = kv_lat[:, m - 2, c * CW:(c + 1) * CW], kv_b[:, m - 2:m - 1]
                        act.activation(dst, ps[:, n % 8, 0:CW], ACT.Identity, bias=bias).then_inc(kept, 1)

                @block.vector
                def _(dve):
                    dve.wait_ge(loaded, 16 * len(loads))
                    dve.tensor_copy(identb[:], ident[:]).then_inc(bt, 1)
                    dve.tensor_scalar(mask_b[:], mask_i[:], 0.0, MASKED, ALU.is_equal, ALU.mult).then_inc(neg, 1)
                    dve.tensor_scalar(mask_a[:], mask_i[:], 0.0, None, ALU.not_equal).then_inc(fl, 1)
                    dve.wait_ge(fl, 1)
                    dve.tensor_reduce(active[:], mask_a[:], AX_X, ALU.max).then_inc(act_row, 1)
                    dve.tensor_scalar(bias_t[:], mask_ti[:], 0.0, MASKED, ALU.is_equal, ALU.mult).then_inc(bt, 1)
                    dve.tensor_tensor(y_nat[:], x_nat[:], out_b[:].unsqueeze(1).to_broadcast([P, PAIRS, E]),
                                      ALU.add).then_inc(yb, 1)
                    dve.wait_ge(act_t, 1)
                    dve.tensor_copy(flags[:], ps[0:1, 0, 0:P]).then_inc(fl, 1)

        ctx_q = [sb(f"ctx_q{i}", [P, KC, SQ]) for i in range(2)]
        mb = [sb(f"mb{i}", [2 * L, SQ]) for i in range(2)]
        kt = [sb(f"kt{i}", [P, KC, S2]) for i in range(2)]
        vt_q = sb("vt_q", [P, KC, SQ])
        v_lat = sb("v_lat", [P, KC, L])
        v_nat = [sb(f"v_nat{i}", [ST, NT + 1, E]) for i in range(2)]
        q_blk = [sb(f"q_blk{i}", [P, KC, 8, L]) for i in range(2)]
        probs = sb("probs", [ST, 2, KC, SLOT])
        masked = sb("masked", [2 * L, 2, SQ])
        part_max = sb("part_max", [2 * L, NP, NQ + 1])
        row_max = sb("row_max", [2 * L, NP])
        neg_rest = sb("neg_rest", [2 * L, NP])
        neg_piece = sb("neg_piece", [2 * L, 3, NP], BF16)
        neg_t = sb("neg_t", [3 * NP, 2 * L], BF16)
        neg_row = sb("neg_row", [P, KC, SLOT], BF16)
        ones3 = sb("ones3", [P, ST], BF16)
        ones_v = sb("ones_v", [ST, 32])
        num = sb("num", [P, KC, 2, L])
        den = sb("den", [P, KC, 2, L])
        o_even = sb("o_even", [P, KC, L])
        o = sb("o", [P, KC, L])
        AC, DE = 6, 7
        preset, neg_in = sem("preset"), sem("neg_in")
        ctx_in = [sem(f"ctx_in{i}") for i in range(2)]
        mb_in = [sem(f"mb_in{i}") for i in range(2)]
        kv_mm, kv_rd, vt_mm, vt_rd, row_mm, row_rd = map(sem, "kv_mm kv_rd vt_mm vt_rd row_mm row_rd".split())
        lat_kv, lat_q, latrow_mm, latrow_rd, latv_mm, latv_rd = map(
            sem, "lat_kv lat_q latrow_mm latrow_rd latv_mm latv_rd".split())
        chain, neg_mm, negt = map(sem, "chain neg_mm negt".split())
        sc_mm, pr, pv_mm, num_rd, den_rd, o_sem, out_mm, y_done = map(
            sem, "sc_mm pr pv_mm num_rd den_rd o_sem out_mm y_done".split())
        CHAIN, O_STEPS = 5, 4
        ctx_view = a["ctx_t"].rearrange("b (c p) s -> b p c s", p=P)

        def flag_of(eng, b, q):
            return eng.value_load(flags[0:1, bass.ds(b * NQ + q, 1)], min_val=0, max_val=1)

        def pass_over(eng, done):
            for which, base, n in done:
                if not isinstance(base, int) or base > 0:
                    eng.wait_ge(which, base)
                eng.sem_inc(which, n)

        def plus(x):
            return not isinstance(x, int) or x > 0

        def sp_body(sp, b, par, one, two, three):
            if two:
                wait_apart(sp, passed, negt, b)
                if plus(b - 1):
                    sp.wait_ge(sc_mm, TILES * (b - 1))
                for r in range(3):
                    sp.dma_start(neg_row[r:r + 1].rearrange("p k n -> p (k n)"), neg_t[r * NP:(r + 1) * NP, :])\
                      .then_inc(neg_in, 16)
            if one:
                for q in range(NQ):
                    n = b * NQ + q
                    with sp.If(flag_of(sp, b, q)):
                        if plus(n - 1):
                            wait_apart(sp, passed, kv_mm, 4 * (n - 1))
                            sp.wait_ge(row_rd, NP * (n - 1))
                        sp.dma_start(ctx_q[q % 2][:], ctx_view[bass.ds(b, 1)].rearrange("o p c s -> p (o c) s")
                                     [:, :, q * SQ:(q + 1) * SQ]).then_inc(ctx_in[q % 2], 16)
                        sp.dma_start(mb[q % 2][:], mb_scr[bass.ds(b, 1), q, :].to_broadcast([2 * L, SQ]))\
                          .then_inc(mb_in[q % 2], 16)
                    with sp.Else():
                        pass_over(sp, [(ctx_in[q % 2], 16 * (2 * b + q // 2), 16), (mb_in[q % 2], 16 * (2 * b + q // 2), 16)])

        def pe_body(pe, b, par, one, two, three):
            old = 1 - par
            if two:
                pe.wait_ge(chain, CHAIN * b)
                pe.transpose(ps[0:3 * NP, 2, :].bitcast(BF16)[:, 0:2 * L], neg_piece[:].rearrange("p r n -> p (r n)"),
                             identb[0:2 * L, 0:2 * L]).then_inc(neg_mm, 1)
            if three:
                pe.wait_ge(o_sem, O_STEPS * (b - 1))
                first = natural(par)
                for k in range(KC):
                    mm = pe.matmul(ps[first:first + L, 3, 0:E], o[:, k], out_w[:, k], start=(k == 0),
                                   stop=(k == KC - 1))
                mm.then_inc(out_mm, 1)
            if one:
                pe.wait_ge(lat_kv, 2 * (b + 1))
                pe.wait_ge(lat_q, b + 1)
                for p in range(NP):
                    k, i = divmod(p, 4)
                    mm = pe.matmul(ps[0:2 * L, 0, p * L:(p + 1) * L],
                                   q_blk[par][:, k, 2 * i:2 * i + 2].rearrange("p h l -> p (h l)"),
                                   kt[par][:, k, S:S2], start=True, stop=True)
                mm.then_inc(latrow_mm, 1)
                for k in range(KC):
                    mm = pe.transpose(ps[0:L, 1, k * P:(k + 1) * P], v_lat[:, k], ident[:])
                mm.then_inc(latv_mm, 1)

            def keys(q):
                n = b * NQ + q
                if q == 0:
                    pe.wait_ge(latrow_rd, b + 1)
                    pe.wait_ge(latv_rd, b + 1)
                    if two:
                        pe.wait_ge(negt, b)
                    if three:
                        pe.wait_ge(y_done, b - 1)
                with pe.If(flag_of(pe, b, q)):
                    pe.wait_ge(ctx_in[q % 2], 16 * (2 * b + q // 2 + 1))
                    if plus(n):
                        pe.wait_ge(row_rd, NP * n)
                    for m in range(4):
                        for k in range(KC):
                            mm = pe.matmul(ps[:, m, 0:SQ], kv_w[:, k, m * P:(m + 1) * P], ctx_q[q % 2][:, k],
                                           start=(k == 0), stop=(k == KC - 1))
                        mm.then_inc(kv_mm, 1)
                    pe.wait_ge(kv_rd, 4 * n + 4)
                    for t in range(TQ):
                        for k in range(KC):
                            mm = pe.transpose(ps[0:ST, t // 2, (t % 2 * 2 + k) * P:(t % 2 * 2 + k + 1) * P],
                                              vt_q[:, k, t * ST:(t + 1) * ST], ident[:])
                        if t % 2 == 1 or t == TQ - 1:
                            mm.then_inc(vt_mm, 1)
                    for p in range(NP):
                        if p in (2, 3):
                            pe.wait_ge(vt_rd, 2 * n + p - 1)
                        if p >= 4:
                            pe.wait_ge(row_rd, NP * n + p - 3)
                        k, i = divmod(p, 4)
                        pe.matmul(ps[0:2 * L, (2 + p) % 4, 0:SQ],
                                  q_blk[par][:, k, 2 * i:2 * i + 2].rearrange("p h l -> p (h l)"),
                                  kt[par][:, k, q * SQ:(q + 1) * SQ], start=True, stop=True).then_inc(row_mm, 1)
                with pe.Else():
                    pass_over(pe, [(kv_mm, 4 * n, 4), (vt_mm, 2 * n, 2), (row_mm, NP * n, NP)])

            def scores(n, rows, tokens):
                at = TILES * (b - 1) + n
                if plus(at):
                    pe.wait_ge(pr, at)
                for k in range(KC):
                    pe.matmul(ps[0:rows, 4 + k, 0:SLOT], kt[old][:, k, tokens],
                              q_blk[old][:, k].rearrange("p h l -> p (h l)"), start=True, stop=False)
                    mm = pe.matmul(ps[0:rows, 4 + k, 0:SLOT], ones3[:, 0:rows], neg_row[:, k], start=False, stop=True)
                mm.then_inc(sc_mm, 1)

            def sums(n, rows, tile):
                at = TILES * (b - 1) + n
                if n == 0 and plus(b - 1):
                    pe.wait_ge(num_rd, b - 1)
                    pe.wait_ge(den_rd, b - 1)
                wait_apart(pe, passed, pr, at + 1)
                for p in range(NP):
                    k, i = divmod(p, 4)
                    where = slice(k * 2 * L, (k + 1) * 2 * L)
                    rhs = probs[0:rows, (old + n) % 2, k, i * 2 * L:(i + 1) * 2 * L]
                    mm = None
                    for bank, lhs in ((AC, v_nat[old][0:rows, tile, p * 32:p * 32 + 32]), (DE, ones_v[0:rows])):
                        mm = pe.matmul(ps[32 * i:32 * i + 32, bank, where], lhs, rhs, start=(n == 0 and k == 0),
                                       stop=(n == TILES - 1), skip_group_check=True)
                mm.then_inc(pv_mm, 1)

            def values(q):
                base = TILES * (b - 1) + 1 + q * TQ
                with pe.If(flag_of(pe, b - 1, q)):
                    for t in range(TQ + 1):
                        tile = q * TQ + t
                        if t < TQ:
                            scores(1 + tile, ST, slice(tile * ST, (tile + 1) * ST))
                        if t >= 1:
                            sums(tile, ST, tile - 1)
                with pe.Else():
                    pass_over(pe, [(sc_mm, base, TQ), (pv_mm, base, TQ)])

            for q in range(NQ):
                if one:
                    keys(q)
                if two:
                    if q == 0:
                        pe.wait_ge(neg_in, 48 * b)
                        scores(0, L, slice(S, S2))
                        sums(0, L, NT)
                    values(q)

        def act_body(act, b, par, one, two, three):
            def exps(n, rows, bias):
                at = TILES * (b - 1) + n
                act.wait_ge(sc_mm, at + 1)
                if plus(at - 1):
                    act.wait_ge(pv_mm, at - 1)
                more = {} if bias is None else {"bias": bias}
                act.activation(probs[0:rows, (1 - par + n) % 2], ps[0:rows, 4:6, 0:SLOT], ACT.Exp, **more)\
                   .then_inc(pr, 1)

            for q in range(NQ):
                if one:
                    n = b * NQ + q
                    with act.If(flag_of(act, b, q)):
                        if plus(b - 1):
                            act.wait_ge(sc_mm, TILES * (b - 1))
                        for m in range(4):
                            act.wait_ge(kv_mm, 4 * n + m + 1)
                            dst = kt[par][:, m, q * SQ:(q + 1) * SQ] if m < KC else vt_q[:, m - KC]
                            act.activation(dst, ps[:, m, 0:SQ], ACT.Identity, bias=kv_b[:, m:m + 1]).then_inc(kv_rd, 1)
                    with act.Else():
                        pass_over(act, [(kv_rd, 4 * n, 4)])
                if two:
                    if q == 0:
                        exps(0, L, None)
                    base = TILES * (b - 1) + 1 + q * TQ
                    with act.If(flag_of(act, b - 1, q)):
                        for t in range(TQ):
                            tile = q * TQ + t
                            exps(1 + tile, ST, bias_t[:, bass.ds(b - 1, 1), tile])
                    with act.Else():
                        pass_over(act, [(pr, base, TQ)])
            if two:
                act.wait_ge(pv_mm, TILES * b)
                if plus(b - 1):
                    act.wait_ge(o_sem, O_STEPS * (b - 1))
                act.activation(num[:].rearrange("p k h l -> p (k h l)"), ps[:, AC, 0:2 * KC * L], ACT.Copy)\
                   .then_inc(num_rd, 1)

        def dve_body(dve, b, par, one, two, three):
            if two:
                dve.wait_ge(neg_mm, b)
                if plus(b - 1):
                    dve.wait_ge(neg_in, 48 * (b - 1))
                dve.tensor_copy(neg_t[:], ps[0:3 * NP, 2, :].bitcast(BF16)[:, 0:2 * L]).then_inc(negt, 1)
            if three:
                dve.wait_ge(out_mm, b)
                first = natural(par)
                rows = y_nat[first:first + L, bass.ds((b - 2) // 2, 1), :].rearrange("p o e -> p (o e)")
                dve.tensor_tensor(rows, ps[first:first + L, 3, 0:E], rows, ALU.add).then_inc(y_done, 1)
            if one:
                if plus(b - 1):
                    dve.wait_ge(sc_mm, TILES * (b - 1))
                dve.tensor_tensor(q_blk[par][:],
                                  qt[:, :, bass.ds(b * L, L)].unsqueeze(2).to_broadcast([P, KC, 8, L]),
                                  head_scale[:].unsqueeze(1).unsqueeze(3).to_broadcast([P, KC, 8, L]), ALU.mult)\
                   .then_inc(lat_q, 1)
                dve.wait_ge(latrow_mm, b + 1)
                dve.tensor_reduce(part_max[:, :, NQ], ps[0:2 * L, 0, 0:NP * L].rearrange("p (h l) -> p h l", l=L),
                                  AX_X, ALU.max).then_inc(latrow_rd, 1)
                dve.wait_ge(latv_mm, b + 1)
                if plus(b - 1):
                    dve.wait_ge(pv_mm, TILES * (b - 1))
                dve.tensor_copy(v_nat[par][0:L, NT, :], ps[0:L, 1, 0:E]).then_inc(latv_rd, 1)
                for q in range(NQ):
                    n = b * NQ + q
                    with dve.If(flag_of(dve, b, q)):
                        for i, tiles in enumerate(((0, 2), (2, TQ))):
                            dve.wait_ge(vt_mm, 2 * n + i + 1)
                            t0, t1 = q * TQ + tiles[0], q * TQ + tiles[1]
                            dve.tensor_copy(v_nat[par][:, t0:t1, :].rearrange("p t e -> p (t e)"),
                                            ps[0:ST, i, 0:(t1 - t0) * E]).then_inc(vt_rd, 1)
                        dve.wait_ge(mb_in[q % 2], 16 * (2 * b + q // 2 + 1))
                        for p in range(NP):
                            if p >= 2 or plus(n):
                                dve.wait_ge(row_rd, NP * n + p - 1)
                            wait_apart(dve, passed, row_mm, NP * n + p + 1)
                            dve.tensor_tensor_reduce(
                                out=masked[:, p % 2], in0=ps[0:2 * L, (2 + p) % 4, 0:SQ], in1=mb[q % 2][:], scale=1.0,
                                scalar=NEG_BIG, op0=ALU.add, op1=ALU.max,
                                accum_out=part_max[:, p, q:q + 1]).then_inc(row_rd, 1)
                    with dve.Else():
                        pass_over(dve, [(vt_rd, 2 * n, 2), (row_rd, NP * n, NP - 1)])
                        dve.memset(part_max[:, :, q], NEG_BIG).then_inc(row_rd, 1)
                k = CHAIN * b
                dve.wait_ge(row_rd, NP * NQ * (b + 1))
                dve.wait_ge(latrow_rd, b + 1)
                if plus(b):
                    dve.wait_ge(neg_mm, b)
                dve.tensor_reduce(row_max[:], part_max[:], AX_X, ALU.max).then_inc(chain, 1)
                dve.wait_ge(chain, k + 1)
                dve.tensor_scalar(neg_piece[:, 0], row_max[:], -1.0, None, ALU.mult).then_inc(chain, 1)
                dve.wait_ge(chain, k + 2)
                dve.scalar_tensor_tensor(neg_rest[:], row_max[:], -1.0, neg_piece[:, 0], ALU.mult,
                                         ALU.subtract).then_inc(chain, 1)
                dve.wait_ge(chain, k + 3)
                dve.tensor_copy(neg_piece[:, 1], neg_rest[:]).then_inc(chain, 1)
                dve.wait_ge(chain, k + 4)
                dve.tensor_tensor(neg_piece[:, 2], neg_rest[:], neg_piece[:, 1], ALU.subtract).then_inc(chain, 1)
            if two:
                dve.wait_ge(pv_mm, TILES * b)
                if plus(b - 1):
                    dve.wait_ge(o_sem, O_STEPS * (b - 1))
                dve.reciprocal(den[:].rearrange("p k h l -> p (k h l)"), ps[:, DE, 0:2 * KC * L]).then_inc(den_rd, 1)

        def pool_body(pool, b, par, one, two, three):
            if three:
                pool.wait_ge(num_rd, b - 1)
                pool.wait_ge(den_rd, b - 1)
                done = O_STEPS * (b - 2)
                pool.tensor_tensor(num[:], num[:], den[:], ALU.mult).then_inc(o_sem, 1)
                wait_apart(pool, passed, o_sem, done + 1)
                pool.tensor_scalar(o_even[:], num[:, :, 0], odd_mask[:, 0:1], None, ALU.mult).then_inc(o_sem, 1)
                wait_apart(pool, passed, out_mm, b - 1)
                pool.tensor_scalar(o[:], num[:, :, 1], odd_mask[:, 1:2], None, ALU.mult).then_inc(o_sem, 1)
                pool.wait_ge(o_sem, done + 3)
                pool.tensor_tensor(o[:], o[:], o_even[:], ALU.add).then_inc(o_sem, 1)
            if one:
                if plus(b - 1):
                    pool.wait_ge(sc_mm, TILES * (b - 1))
                pool.tensor_copy(kt[par][:, :, S:S2], kv_lat[:, 0:KC, bass.ds(b * L, L)]).then_inc(lat_kv, 1)
                if plus(b):
                    pool.wait_ge(latv_mm, b)
                pool.tensor_copy(v_lat[:], kv_lat[:, KC:2 * KC, bass.ds(b * L, L)]).then_inc(lat_kv, 1)

        def all_bodies(eng, body):
            def one(b, par):
                known = isinstance(b, int)
                body(eng, b, par, not known or b < B, not known or 1 <= b <= B, not known or b >= 2)
            one(0, 0)
            one(1, 1)
            with eng.Fori(2, B - 1, 2) as b:
                one(b, 0)
                one(b + 1, 1)
            one(B, 0)
            one(B + 1, 1)

        with nc.Block() as block:
            @block.sync
            def _(sp):
                sp.wait_ge(preset, 4)
                all_bodies(sp, sp_body)

            @block.tensor
            def _(pe):
                pe.wait_ge(preset, 4)
                pe.sem_inc(out_mm, 1)
                all_bodies(pe, pe_body)

            @block.scalar
            def _(act):
                all_bodies(act, act_body)

            @block.vector
            def _(dve):
                all_bodies(dve, dve_body)

            @block.gpsimd
            def _(pool):
                sets = [(neg_row[:], 0.0), (ones3[:], 0.0), (ones3[0:3], 1.0), (ones_v[:], 1.0)]
                for n, (where, value) in enumerate(sets):
                    pool.memset(where, value).then_inc(preset, 1)
                    pool.wait_ge(preset, n + 1)
                all_bodies(pool, pool_body)
        clear(nc, sems)


def mlp(nc, x_nat, y_nat, a):
    GM = 4
    NM = GM * P
    with ExitStack() as ctx:
        def sb(name, shape, dt=F32):
            return ctx.enter_context(nc.sbuf_tensor("m_" + name, shape, dt))

        ident = sb("ident", [P, P])
        w1 = sb("w1", [P, KC, FF])
        b1 = sb("b1", [P, FC])
        w2 = sb("w2", [P, FC, E])
        b2 = sb("b2", [P, E])
        norm_w = sb("norm_w", [P, KC])
        loads = [(ident, "ident"), (w1, "mlp_w1"), (b1, "mlp_b1"), (w2, "mlp_w2"), (b2, "mlp_b2"),
                 (norm_w, "postnorm")]
        eps = sb("eps", [P, 1])
        square = sb("square", [P, 2, E])
        sum_sq = sb("sum_sq", [P, PAIRS])
        rms = sb("rms", [P, PAIRS])
        rrms = sb("rrms", [P, PAIRS])
        yn = sb("yn", [P, GM, E])
        yt = sb("yt", [P, KC, NM])
        h = sb("h", [P, FC, NM])
        ps = ctx.enter_context(nc.psum_tensor("ps_m", [P, 8, 512], F32))
        sems = loaded, preset, squared, rms_set, rrms_set, based, normed, turned, yt_set, hid_mm, hid, out_mm, out_rd = [
            ctx.enter_context(nc.semaphore("m_" + n)) for n in
            "loaded preset squared rms_set rrms_set based normed turned yt_set hid_mm hid out_mm out_rd".split()]

        def later(c):
            return not isinstance(c, int) or c > 0

        with nc.Block() as block:
            @block.sync
            def _(sp):
                for dst, name in loads:
                    sp.dma_start(dst[:], a[name]).then_inc(loaded, 16)
                sp.wait_ge(loaded, 16 * len(loads))

            @block.gpsimd
            def _(pool):
                pool.memset(eps[:], RMS_EPS).then_inc(preset, 1)

            @block.tensor
            def _(pe):
                pe.wait_ge(loaded, 16 * len(loads))

                def output(c, m):
                    pe.wait_ge(hid, FC * c + m + 1)
                    for g in range(GM):
                        mm = pe.matmul(ps[:, 6 + g // 2, g % 2 * E:(g % 2 + 1) * E], h[:, m, g * P:(g + 1) * P],
                                       w2[:, m], start=(m == 0 and g % 2 == 0), stop=(m == FC - 1),
                                       skip_group_check=True)
                    return mm

                pe.sem_inc(out_mm, 1)
                with pe.Fori(0, PAIRS // GM) as c:
                    for k in range(KC):
                        pe.wait_ge(normed, GM * (c + 1))
                        for g in range(GM):
                            mm = pe.transpose(ps[:, k, g * P:(g + 1) * P], yn[:, g, k * P:(k + 1) * P], ident[:])
                        mm.then_inc(turned, 1)
                    pe.wait_ge(yt_set, KC * (c + 1))
                    for m in range(FC):
                        if m >= 4:
                            pe.wait_ge(hid, FC * c + m - 3)
                        for k in range(KC):
                            mm = pe.matmul(ps[:, 2 + m % 4, :], w1[:, k, m * P:(m + 1) * P], yt[:, k],
                                           start=(k == 0), stop=(k == KC - 1))
                        mm.then_inc(hid_mm, 1)
                        if m >= 2:
                            if m == 2:
                                pe.wait_ge(out_rd, 2 * (c + 1))
                            output(c, m - 2)
                    output(c, FC - 2)
                    output(c, FC - 1).then_inc(out_mm, 1)

            @block.scalar
            def _(act):
                act.wait_ge(loaded, 16 * len(loads))
                for g in range(PAIRS):
                    if g >= 2:
                        act.wait_ge(squared, g - 1)
                    act.activation(square[:, g % 2], y_nat[:, g], ACT.Square,
                                   accum_out=sum_sq[:, g:g + 1]).then_inc(squared, 1)
                act.wait_ge(preset, 1)
                act.wait_ge(squared, PAIRS)
                act.activation(rms[:], sum_sq[:], ACT.Sqrt, scale=1.0 / E, bias=eps[:]).then_inc(rms_set, 1)
                with act.Fori(0, PAIRS // GM) as c:
                    for k in range(KC):
                        act.wait_ge(turned, KC * c + k + 1)
                        act.activation(yt[:, k], ps[:, k], ACT.Identity, scale=norm_w[:, k:k + 1]).then_inc(yt_set, 1)
                    for m in range(FC):
                        act.wait_ge(hid_mm, FC * c + m + 1)
                        if m == 0:
                            act.wait_ge(out_mm, c + 1)
                        act.activation(h[:, m], ps[:, 2 + m % 4], ACT.Gelu_apprx_tanh,
                                       bias=b1[:, m:m + 1]).then_inc(hid, 1)

            @block.vector
            def _(dve):
                dve.wait_ge(loaded, 16 * len(loads))
                dve.tensor_tensor(x_nat[:], x_nat[:], b2[:].unsqueeze(1).to_broadcast([P, PAIRS, E]),
                                  ALU.add).then_inc(based, 1)
                dve.wait_ge(rms_set, 1)
                dve.reciprocal(rrms[:], rms[:]).then_inc(rrms_set, 1)
                dve.wait_ge(rrms_set, 1)
                dve.wait_ge(based, 1)

                def normalise(c, g):
                    if later(c):
                        dve.wait_ge(turned, KC * c)
                    tile = bass.ds(c * GM + g, 1)
                    dve.tensor_scalar(yn[:, g], y_nat[:, tile, :].rearrange("p o e -> p (o e)"), rrms[:, tile], None,
                                      ALU.mult).then_inc(normed, 1)

                def output_rows(c):
                    dve.wait_ge(out_mm, c + 2)
                    for i in range(2):
                        rows = x_nat[:, bass.ds(c * GM + 2 * i, 2), :].rearrange("p g e -> p (g e)")
                        dve.tensor_tensor(rows, ps[:, 6 + i], rows, ALU.add).then_inc(out_rd, 1)

                dve.sem_inc(out_rd, 2)
                for g in range(GM):
                    normalise(0, g)
                with dve.Fori(0, PAIRS // GM - 1) as c:
                    for g in range(GM):
                        normalise(c + 1, g)
                    output_rows(c)
                output_rows(PAIRS // GM - 1)
        clear(nc, sems)


def rows_first(w):
    return w.reshape(-1, P, w.shape[-1]).transpose(1, 0, 2)


def natural_rows(x):
    n = np.zeros((2, HALF, PAIRS, x.shape[-1]), x.dtype)
    n[:, :L] = x.reshape(PAIRS, 2, L, -1).transpose(1, 2, 0, 3)
    return n.reshape(P, PAIRS, -1)


def layout(i):
    d = {}
    x, c = i["x"], i["ctx_2048"]
    d["x_nat"] = natural_rows(x)
    d["x_t"] = x.reshape(T, E).T
    d["ctx_t"] = c.transpose(0, 2, 1)
    d["mask0"] = np.concatenate([i["mask_Bx1xSxS2_ff0"][:, 0]], 1)
    d["ident"] = np.eye(P, dtype=np.float32)
    w = i["L0_xattn_Wq"].reshape(E, KVH, G, HD).transpose(0, 2, 1, 3).reshape(E, G * KVH * HD)
    d["wq"] = rows_first(w).reshape(P, KC, G, KVH * HD)
    d["bq"] = i["L0_xattn_bq"].reshape(KVH, G, HD).transpose(0, 2, 1).reshape(KVH * HD, G)
    d["wkv"] = rows_first(np.concatenate([i["L0_xattn_Wk"], i["L0_xattn_Wv"]], 1))
    d["bkv"] = np.concatenate([i["L0_xattn_bk"], i["L0_xattn_bv"]]).reshape(P, 1)
    wo = np.zeros((NJ, 32, 2, G, E), np.float32)
    wo[:, :HD] = i["L0_xattn_Wo"].reshape(NJ, 2, G, HD, E).transpose(0, 3, 1, 2, 4)
    d["wo"] = wo.reshape(P, 2 * G, E)
    d["bo"] = np.broadcast_to(i["L0_xattn_bo"], (P, E))
    d["ln0_g"] = np.broadcast_to(i["L0_xattn_gamma"], (P, E))
    d["ln0_b"] = np.broadcast_to(i["L0_xattn_beta"], (P, E))
    sel = np.zeros((NJ, 32, NJ, 32), np.float32)
    for j in range(NJ):
        sel[j, HD, j, :] = 1.0
    d["den_sel"] = sel.reshape(P, P)
    d["mask_sel"] = np.tile(np.eye(L, dtype=np.float32), (1, 2 * G))
    for tag, src, n in (("b", "L1_xattn_", {"u": "faaaa", "dw1": "decay_w1", "dw2": "decay_w2", "fk": "ffn_Wk",
                                           "fr": "ffn_Wr", "fv": "ffn_Wv"}),
                        ("d", "L3_xattn_", {"u": "u", "dw1": "td_w1", "dw2": "td_w2", "fk": "Wfk", "fr": "Wfr",
                                           "fv": "Wfv"})):
        m = i[src + "maa_stack"].reshape(5, E)
        vec = {"ln1_w": i[src + "ln1_w"], "ln1_b": i[src + "ln1_b"], "ln2_w": i[src + "ln2_w"],
               "ln2_b": i[src + "ln2_b"], "maa_x": i[src + "maa_x"], "td": i[src + "time_decay"],
               "gn_w": i[src + "gn_w"], "gn_b": i[src + "gn_b"], "u": i[src + n["u"]],
               "fmk": i[src + "ffn_maa_k"], "fmr": i[src + "ffn_maa_r"]} | {f"m{j}": m[j] for j in range(5)}
        d[tag + "vec"] = rows_first(np.stack([vec[k].reshape(E) for k in VEC], 1))
        w1 = np.zeros((E, 2 * P), np.float32)
        w1[:, :160] = i[src + "maa_w1"]
        d[tag + "w1"] = rows_first(w1)
        w2 = np.zeros((P, 5, E), np.float32)
        for j in range(5):
            w2[32 * (j % 4):32 * (j % 4) + 32, j] = i[src + "maa_w2"][j]
        d[tag + "w2"] = w2
        dw1 = np.zeros((E, P), np.float32)
        dw1[:, :64] = i[src + n["dw1"]]
        d[tag + "dw1"] = rows_first(dw1)
        dw2 = np.zeros((P, E), np.float32)
        dw2[:64] = i[src + n["dw2"]]
        d[tag + "dw2"] = dw2
        for k, name in (("wr", "Wr"), ("wk", "Wk"), ("wv", "Wv"), ("wg", "Wg"), ("wo", "Wo"), ("fk", n["fk"]),
                        ("fr", n["fr"]), ("fv", n["fv"])):
            d[tag + k] = rows_first(i[src + name].T)
    vsel = np.zeros((16, HS, HS, 16, HS), np.float32)
    for h in range(16):
        for j in range(HS):
            vsel[h, j, j, h, :] = 1.0
    d["vsel"] = vsel.reshape(P, HS, P)
    d["osel"] = vsel.reshape(P, HS, P).transpose(2, 1, 0)
    blocks = np.kron(np.eye(16, dtype=np.float32), np.ones((HS, HS), np.float32))
    d["head_sum"] = blocks
    d["head_mean"] = blocks / np.float32(HS)
    d["st"] = c[:, 0:2].reshape(B, 2, KC, P).transpose(3, 1, 2, 0)
    d["s0"] = c[:, 2:2 + HS].reshape(B, KC, P, HS).transpose(2, 1, 3, 0)
    kv_w, kv_b = i["L2_xattn_kv_w"].reshape(E, E, 2), i["L2_xattn_kv_b"].reshape(E, 2)
    d["c_kv_w"] = rows_first(np.concatenate([kv_w[:, :, 0], kv_w[:, :, 1]], 1))
    d["c_kv_b"] = np.concatenate([kv_b[:, 0], kv_b[:, 1]]).reshape(4, P).T
    d["c_q_w"], d["c_q_b"] = rows_first(i["L2_xattn_q_w"]), i["L2_xattn_q_b"].reshape(KC, P).T
    d["c_out_w"], d["c_out_b"] = rows_first(i["L2_xattn_out_w"]), np.broadcast_to(i["L2_xattn_out_b"], (P, E))
    d["head_scale"] = np.kron(np.eye(8, dtype=np.float32), np.ones((HD2, 1), np.float32)) / np.float32(HD2)
    d["odd_mask"] = np.kron(np.tile(np.eye(2, dtype=np.float32), (4, 1)), np.ones((HD2, 1), np.float32))
    mask = i["mask_BxS2_ik0"]
    d["mask_q"] = mask.reshape(B * NQ, SQ)
    d["mask_t"] = mask.reshape(B, NT, ST).transpose(2, 0, 1)
    d["mlp_w1"], d["mlp_b1"] = rows_first(i["L2_xattn_mlp_w1"]), i["L2_xattn_mlp_b1"].reshape(FC, P).T
    d["mlp_w2"], d["mlp_b2"] = rows_first(i["L2_xattn_mlp_w2"]), np.broadcast_to(i["L2_xattn_mlp_b2"], (P, E))
    d["postnorm"] = i["L2_xattn_postnorm_w"].reshape(KC, P).T
    return d


def program(nc, a, out):
    with nc.sbuf_tensor("x_nat", [P, PAIRS, E], F32) as x_nat, nc.semaphore("stored") as stored, \
            nc.semaphore("passed") as passed:

        layer0(nc, x_nat, a, passed)
        rwkv(nc, x_nat, a, "b", True, passed)
        with nc.sbuf_tensor("y_nat", [P, PAIRS, E], F32) as y_nat:
            latent_attention(nc, x_nat, y_nat, a, passed)
            mlp(nc, x_nat, y_nat, a)
        rwkv(nc, x_nat, a, "d", False, passed)
        with nc.Block() as block:
            @block.sync
            def _(sp):
                for par in range(2):
                    sp.dma_start(out.rearrange("(g r) l e -> r l g e", r=2)[par],
                                 x_nat[HALF * par:HALF * par + L]).then_inc(stored, 16)
                sp.wait_ge(stored, 32)


def kernel(**inputs):
    import numpy as _np
    import concourse.bacc as _bacc
    from concourse import mybir as _mybir
    from concourse.bass_utils import run_bass_kernel_spmd as _run

    arrays = layout({k: _np.asarray(v) for k, v in inputs.items()})
    nc = _bacc.Bacc("TRN2", target_bir_lowering=False, num_devices=1)
    args = {}
    feed = {}
    for name, v in arrays.items():
        v = _np.ascontiguousarray(v)
        feed[f"in_{name}"] = v
        args[name] = nc.dram_tensor(f"in_{name}", v.shape, _mybir.dt.from_np(v.dtype), kind="ExternalInput").ap()
    out = nc.dram_tensor("out_0", (B, L, E), F32, kind="ExternalOutput").ap()
    program(nc, args, out)
    r = _run(nc, [feed], core_ids=[0])
    return r.results[0]["out_0"]
```

```python
import numpy as np
from contextlib import ExitStack

import concourse.bass as bass
from concourse import mybir
from concourse.alu_op_type import AluOpType as ALU

F32 = mybir.dt.float32
BF16 = mybir.dt.bfloat16
I32 = mybir.dt.int32
ACT = mybir.ActivationFunctionType
AX_X = mybir.AxisListType.X

P = 128
B, L, E = 32, 56, 256
S = 1500
KC = E // P
T = B * L
PAIRS = B // 2
HALF = 64
NEG_BIG = -3.0e38

KVH, G, HD = 8, 4, 8
ST = 125
NT = S // ST
SC = 500
NC = S // SC
NJ = KVH // 2
QW = G * L
PW = 2 * QW
NR = NJ * PW // (2 * L)
K_PIECES = (0, 0, 0, 1, 1, 2)
Q_PIECES = (0, 1, 2, 0, 1, 0)
NS = len(K_PIECES)
SROWS = 16 * NS
MROWS = SROWS + 3


def natural(b):
    return HALF * (b % 2)


def wait_apart(eng, passed, which, value):
    eng.wait_ge(which, value)
    eng.sem_inc(passed, 1)


def clear(nc, sems):
    with nc.Block() as block:
        @block.gpsimd
        def _(pool):
            for s in sems:
                pool.sem_clear(s)


def layer0(nc, x_nat, a, passed):
    q_scr = nc.dram_tensor("q_scr", [NS, KVH * HD, B, 2, QW], BF16).ap()
    k_scr = nc.dram_tensor("k_scr", [2, NS, KVH * HD, S], BF16).ap()
    sems = []
    with ExitStack() as ctx:
        def sb(name, shape, dt=F32):
            return ctx.enter_context(nc.sbuf_tensor(name, shape, dt))

        def sem(name):
            sems.append(ctx.enter_context(nc.semaphore(name)))
            return sems[-1]

        ident = sb("ident", [P, P])
        identb = sb("identb", [P, P], BF16)
        wq = sb("wq", [P, KC, G, KVH * HD])
        bq = sb("bq", [KVH * HD, G])
        wkv = sb("wkv", [P, KC, P])
        bkv = sb("bkv", [P, 1])
        wo = sb("wo", [P, 2 * G, E])
        bo = sb("bo", [P, E])
        den_sel = sb("den_sel", [P, P])
        mask_sel = sb("mask_sel", [L, PW])
        ones = sb("ones", [P, 1])
        ctx_t = sb("ctx_t", [P, KC, S])
        kv_t = [sb(f"kv_t{i}", [P, S]) for i in range(2)]
        k_piece = sb("k_piece", [KVH * HD, 3, S], BF16)
        k_rest = sb("k_rest", [KVH * HD, S])
        ks = [sb(f"ks{i}", [MROWS, NJ, S], BF16) for i in range(2)]
        qs = [sb(f"qs{i}", [MROWS, NJ, 2, QW], BF16) for i in range(2)]
        vp = [sb(f"vp{i}", [ST, NT, KVH, 32]) for i in range(2)]
        mask = [sb(f"mask{i}", [2 * L, S]) for i in range(2)]
        probs = [sb(f"probs{i}", [ST, NJ, PW]) for i in range(2)]
        masked = sb("masked", [2 * L, 2, SC])
        part_max = sb("part_max", [2 * L, NR, NC])
        row_max = sb("row_max", [2 * L, NR])
        neg_rest = sb("neg_rest", [2 * L, NR])
        neg_piece = sb("neg_piece", [2 * L, 3, NR], BF16)
        neg_t = sb("neg_t", [3 * NR, 2 * L], BF16)
        mask_abs = sb("mask_abs", [2 * L, S], BF16)
        mask_sum = sb("mask_sum", [2 * L, 1])
        flag = sb("flag", [1, 2], I32)
        o_raw = sb("o_raw", [P, PW])
        den_inv = sb("den_inv", [P, PW])
        o_n = sb("o_n", [P, PW])
        ps = ctx.enter_context(nc.psum_tensor("ps_a", [P, 8, 512], F32))
        FRONT, ACC, MISC = (4, 5), 6, 7

        ctx_in, mask_in, k_in, q_in, neg_in, k_out = map(sem, "ctx_in mask_in k_in q_in neg_in k_out".split())
        kv_mm, kv_read, split_done, rest_done, hi_done, mid_done = map(
            sem, "kv_mm kv_read split_done rest_done hi_done mid_done".split())
        vt_mm, vt_read, row_mm, row_read = map(sem, "vt_mm vt_read row_mm row_read".split())
        chain, neg_mm, negt_done = map(sem, "chain neg_mm negt_done".split())
        abs_done, flag_mm, flag_done = map(sem, "abs_done flag_mm flag_done".split())
        score_mm, probs_done, pv_mm, acc_read = map(sem, "score_mm probs_done pv_mm acc_read".split())
        den_mm, inv_done, norm_done, out_mm, x_done = map(sem, "den_mm inv_done norm_done out_mm x_done".split())
        STEP_ROWS = (2, 4, 4, 4, 5, 4, 4, 4, 4, 4, 5, 4)
        INV_PARTS = 4
        KV_STEPS, DEN_STEP, MID_STEP, TURN_STEPS, OUT_STEP, FLAG_STEP = (1, 2, 3), 4, 5, (6, 7, 8), 9, 10
        ROWS_BY = [sum(STEP_ROWS[:t + 1]) for t in range(NT)] + [NR * NC]
        CHAIN = 5
        q_view = q_scr.rearrange("s (q j) b h n -> b (s q) j h n", j=NJ)
        k_view = k_scr.rearrange("i s (q j) x -> i (s q) j x", j=NJ)

        def store_k(sp, par):
            for r in range(3):
                slots = [s for s in range(NS) if K_PIECES[s] == r]
                sp.dma_start(k_scr[par, slots[0]:slots[-1] + 1].rearrange("s d x -> d s x"),
                             k_piece[:, r:r + 1].to_broadcast([KVH * HD, len(slots), S])).then_inc(k_out, 16)

        ctx_view = a["ctx_t"].rearrange("b (c p) s -> b p c s", p=P)
        m_view = a["mask0"]

        def at(ap, b):
            return ap[b] if isinstance(b, int) else ap[bass.ds(b, 1)].rearrange("o p s -> (o p) s")

        def at4(ap, b):
            return ap[b] if isinstance(b, int) else ap[bass.ds(b, 1)].rearrange("o p c s -> p (o c) s")

        def kv_chunk(pe, n, c):
            if c == 0:
                pe.wait_ge(ctx_in, 16 * (n + 1))
            if not isinstance(n, int) or n + c > 0:
                pe.wait_ge(kv_read, NC * n + c)
            for k in range(KC):
                mm = pe.matmul(ps[:, MISC, 0:SC], wkv[:, k], ctx_t[:, k, c * SC:(c + 1) * SC],
                               start=(k == 0), stop=(k == KC - 1))
            mm.then_inc(kv_mm, 1)

        def kv_evacuate(act, n, c, to):
            act.wait_ge(kv_mm, NC * n + c + 1)
            act.activation(to[:, c * SC:(c + 1) * SC], ps[:, MISC, 0:SC], ACT.Identity, bias=bkv[:])\
               .then_inc(kv_read, 1)

        def round_high(act, n, kk):
            act.wait_ge(kv_read, NC * (n + 1))
            if not isinstance(n, int) or n > 0:
                act.wait_ge(k_out, 48 * n)
            act.activation(k_piece[:, 0], kk, ACT.Copy).then_inc(hi_done, 1)

        def round_middle(act, n):
            act.wait_ge(rest_done, n + 1)
            act.activation(k_piece[:, 1], k_rest[:], ACT.Copy).then_inc(mid_done, 1)

        def split_k(pool, n, kk):
            pool.wait_ge(kv_read, NC * (n + 1))
            pool.wait_ge(hi_done, n + 1)
            pool.tensor_tensor(k_rest[:], kk, k_piece[:, 0], ALU.subtract).then_inc(rest_done, 1)
            pool.wait_ge(mid_done, n + 1)
            pool.tensor_tensor(k_piece[:, 2], k_rest[:], k_piece[:, 1], ALU.subtract).then_inc(split_done, 1)

        CH = 4
        CW = CH * L
        with ExitStack() as early:
            x_t = early.enter_context(nc.sbuf_tensor("x_t", [P, KC, T], F32))
            q32 = [early.enter_context(nc.sbuf_tensor(f"q32_{i}", [KVH * HD, CH, QW], F32)) for i in range(2)]
            qr = [early.enter_context(nc.sbuf_tensor(f"qr{i}", [KVH * HD, CH, QW], F32)) for i in range(2)]
            qp = [k_place[0:KVH * HD].rearrange("p j s -> p (j s)")[:, 0:3 * CH * 2 * QW]
                  .rearrange("p (r b h n) -> p r b h n", r=3, b=CH, h=2) for k_place in ks]
            qp.append(early.enter_context(nc.sbuf_tensor("qp2", [KVH * HD, 3, CH, 2, QW], BF16))[:])
            loaded = sem("a_loaded")
            preset = sem("a_preset")
            q_mm = sem("q_mm")
            q_add = sem("q_add")
            q_hi = sem("q_hi")
            q_r1 = sem("q_r1")
            q_mid = sem("q_mid")
            q_lo = sem("q_lo")
            q_out = [sem(f"q_out{i}") for i in range(3)]
            x_bias = sem("x_bias")
            kv_loaded = sem("kv_loaded")
            zeroed = sem("zeroed")
            late_loaded = sem("late_loaded")

            def half(h):
                return slice(h * KVH * HD // 2, (h + 1) * KVH * HD // 2)
            HEADS = [(h, half(h)) for h in range(2)]
            LATE_LOADS = 6
            CHUNKS = B // CH
            with nc.Block() as block:
                @block.sync
                def _(sp):
                    for dst, src in ((wkv, a["wkv"]), (bkv, a["bkv"])):
                        sp.dma_start(dst[:], src).then_inc(kv_loaded, 16)
                    sp.dma_start(ctx_t[:], ctx_view[0]).then_inc(ctx_in, 16)
                    for dst, src in ((x_t, a["x_t"].rearrange("(c p) t -> p c t", p=P)),
                                     (wq, a["wq"]), (bq, a["bq"])):
                        sp.dma_start(dst[:], src).then_inc(loaded, 16)
                    sp.wait_ge(kv_mm, NC)
                    sp.dma_start(ctx_t[:], ctx_view[1]).then_inc(ctx_in, 16)
                    for dst, src in ((ident, a["ident"]), (bo, a["bo"]), (x_nat, a["x_nat"]),
                                     (wo, a["wo"]), (den_sel, a["den_sel"]), (mask_sel, a["mask_sel"])):
                        sp.dma_start(dst[:], src).then_inc(late_loaded, 16)
                    sp.wait_ge(split_done, 1)
                    store_k(sp, 0)
                    for c in range(CHUNKS):
                        sp.wait_ge(q_lo, 2 * (c + 1))
                        for s, r in enumerate(Q_PIECES):
                            sp.dma_start(q_scr[s, :, c * CH:(c + 1) * CH], qp[c % 3][:, r]).then_inc(q_out[c % 3], 16)
                    for i in range(3):
                        sp.wait_ge(q_out[i], 16 * NS * len(range(i, CHUNKS, 3)))

                @block.gpsimd
                def _(pool):
                    for q in qp:
                        pool.memset(q[:], 0.0).then_inc(zeroed, 1)
                    split_k(pool, 0, kv_t[0][0:KVH * HD])
                    pool.wait_ge(split_done, 1)
                    for c in range(CHUNKS):
                        pool.wait_ge(q_mid, 2 * (c + 1))
                        for h, on in HEADS:
                            pool.tensor_tensor(qp[c % 3][on, 2, :, h], qr[c % 2][on], qp[c % 3][on, 1, :, h],
                                               ALU.subtract).then_inc(q_lo, 1)

                @block.tensor
                def _(pe):
                    pe.wait_ge(kv_loaded, 32)
                    for c in range(NC):
                        kv_chunk(pe, 0, c)
                    pe.wait_ge(loaded, 48)
                    for c in range(CHUNKS):
                        for g in range(G):
                            if c >= 1:
                                pe.wait_ge(q_add, G * (c - 1) + g + 1)
                            for k in range(KC):
                                mm = pe.matmul(ps[0:KVH * HD, g, 0:CW], wq[:, k, g, :],
                                               x_t[:, k, c * CW:(c + 1) * CW], start=(k == 0), stop=(k == KC - 1))
                            mm.then_inc(q_mm, 1)

                @block.vector
                def _(dve):
                    sets = [(ones[:], 1.0)]
                    for i in range(2):
                        sets += [(qs[i][:], 0.0), (ks[i][SROWS:MROWS], 1.0), (vp[i][:], 0.0),
                                 (vp[i][:, :, :, HD:HD + 1], 1.0)]
                    for n, (where, value) in enumerate(sets):
                        dve.memset(where, value).then_inc(preset, 1)
                        dve.wait_ge(preset, n + 1)
                    dve.wait_ge(loaded, 48)
                    for c in range(CHUNKS):
                        for g in range(G):
                            dve.wait_ge(q_mm, G * c + g + 1)
                            if c >= 2:
                                dve.wait_ge(q_hi, 2 * (c - 1))
                                dve.wait_ge(q_r1, 2 * (c - 1))
                            dve.tensor_scalar(q32[c % 2][:, :, g * L:(g + 1) * L],
                                              ps[0:KVH * HD, g, 0:CW].rearrange("p (b l) -> p b l", l=L),
                                              bq[:, g:g + 1], float(HD) ** -0.5, ALU.add, ALU.mult).then_inc(q_add, 1)
                        if c == CHUNKS // 2:
                            dve.wait_ge(late_loaded, 16 * LATE_LOADS)
                            dve.tensor_copy(identb[:], ident[:]).then_inc(x_bias, 1)
                            dve.tensor_tensor(x_nat[:], x_nat[:], bo[:].unsqueeze(1).to_broadcast([P, PAIRS, E]),
                                              ALU.add).then_inc(x_bias, 1)
                        dve.wait_ge(q_hi, 2 * (c + 1))
                        if c >= 2:
                            dve.wait_ge(q_lo, 2 * (c - 1))
                        for h, on in HEADS:
                            dve.tensor_tensor(qr[c % 2][on], q32[c % 2][on], qp[c % 3][on, 0, :, h],
                                              ALU.subtract).then_inc(q_r1, 1)
                    dve.wait_ge(x_bias, 2)

                @block.scalar
                def _(act):
                    def round_q_middle(c):
                        act.wait_ge(q_r1, 2 * (c + 1))
                        for h, on in HEADS:
                            act.activation(qp[c % 3][on, 1, :, h], qr[c % 2][on], ACT.Copy).then_inc(q_mid, 1)

                    act.wait_ge(kv_loaded, 32)
                    for c in range(NC):
                        kv_evacuate(act, 0, c, kv_t[0])
                    round_high(act, 0, kv_t[0][0:KVH * HD])
                    round_middle(act, 0)
                    act.wait_ge(zeroed, len(qp))
                    for c in range(CHUNKS):
                        act.wait_ge(q_add, G * (c + 1))
                        if c >= 3:
                            act.wait_ge(q_out[c % 3], 16 * NS * (c // 3))
                        for h, on in HEADS:
                            act.activation(qp[c % 3][on, 0, :, h], q32[c % 2][on], ACT.Copy).then_inc(q_hi, 1)
                        round_q_middle(c)

        def sp_body(sp, b, par, prev, cur, front, front2, ctx3):
            nx = 1 - par
            if front:
                if prev:
                    wait_apart(sp, passed, score_mm, 24 * b)
                sp.wait_ge(k_out, 48 * (b + 2))
                sp.dma_start(ks[nx][0:SROWS], k_view[nx]).then_inc(k_in, 16)
                sp.dma_start(qs[nx][0:SROWS], q_view[bass.ds(b + 1, 1)].rearrange("o p j h n -> p (o j) h n"))\
                  .then_inc(q_in, 16)
                sp.dma_start(mask[nx][:], at(m_view, b + 1)).then_inc(mask_in, 16)
            if ctx3:
                sp.wait_ge(kv_mm, NC * (b + 3))
                sp.dma_start(ctx_t[:], at4(ctx_view, b + 3)).then_inc(ctx_in, 16)
            if front2:
                wait_apart(sp, passed, split_done, b + 3)
                if not isinstance(b, int) or b >= 0:
                    sp.wait_ge(k_in, 16 * (b + 1))
                store_k(sp, par)

        def pe_scores(pe, b, t, par, any_mask, halves=(0, 1)):
            for half in halves:
                wait = 24 * b + 2 * (t - 1) + half + 1
                if not isinstance(wait, int) or wait > 0:
                    pe.wait_ge(probs_done, wait)

                def products(with_mask):
                    for i in (2 * half, 2 * half + 1):
                        mm = pe.matmul(ps[0:ST, i, 0:PW], ks[par][:, i, t * ST:(t + 1) * ST],
                                       qs[par][:, i].rearrange("p h n -> p (h n)"), start=True, stop=not with_mask)
                        if with_mask:
                            mm = pe.matmul(ps[0:ST, i, 0:PW], mask[par][0:L, t * ST:(t + 1) * ST], mask_sel[:],
                                           start=False, stop=True)
                    mm.then_inc(score_mm, 1)
                with pe.If(any_mask):
                    products(True)
                with pe.Else():
                    products(False)

        def pe_pv(pe, b, t, par, halves=(0, 1)):
            if t == 0 and 0 in halves:
                pe.wait_ge(vt_read, 3 * (b + 1))
                if not isinstance(b, int) or b > 0:
                    pe.wait_ge(acc_read, b)
            if 0 in halves:
                pe.wait_ge(probs_done, 24 * b + 2 * t + 2)
            for h in halves:
                for j in range(NJ):
                    mm = pe.matmul(ps[32 * j:32 * j + 32, ACC, h * QW:(h + 1) * QW], vp[par][:, t, 2 * j + h, :],
                                   probs[t % 2][:, j, h * QW:(h + 1) * QW], start=(t == 0 and h == 0),
                                   stop=(t == NT - 1), skip_group_check=True)
                if h == 1:
                    mm.then_inc(pv_mm, 1)

        def pe_rows(pe, n, par, lo, hi):
            for u in range(lo, hi):
                read = NR * NC * n + u - 1
                if not isinstance(read, int) or read > 0:
                    pe.wait_ge(row_read, read)
                r, c = divmod(u, NC)
                j, h, gp = r // 4, r // 2 % 2, r % 2
                pe.matmul(ps[0:2 * L, FRONT[u % 2], 0:SC], qs[par][0:SROWS, j, h, gp * 2 * L:(gp + 1) * 2 * L],
                          ks[par][0:SROWS, j, c * SC:(c + 1) * SC], start=True, stop=True).then_inc(row_mm, 1)

        def pe_body(pe, b, par, prev, cur, front, front2, ctx3):
            nx = 1 - par
            if cur:
                wait_apart(pe, passed, flag_done, b + 1)
                masked_cur = pe.value_load(flag[0:1, par:par + 1], min_val=0, max_val=1)

            def turn_v(c):
                if c > 0:
                    pe.wait_ge(vt_read, 3 * (b + 1) + c)
                elif prev:
                    pe.wait_ge(inv_done, INV_PARTS * b)
                else:
                    pe.wait_ge(kv_read, NC * (b + 3))
                pe.wait_ge(kv_read, NC * (b + 2))
                for i in range(4):
                    t = 4 * c + i
                    mm = pe.transpose(ps[0:ST, MISC, i * P:(i + 1) * P], kv_t[nx][:, t * ST:(t + 1) * ST], ident[:])
                mm.then_inc(vt_mm, 1)

            if prev:
                pe_pv(pe, b - 1, NT - 1, nx)
            if cur:
                wait_apart(pe, passed, chain, CHAIN * (b + 1))
                pe.transpose(ps[0:3 * NR, MISC, :].bitcast(BF16)[:, 0:2 * L], neg_piece[:].rearrange("p r n -> p (r n)"),
                             identb[0:2 * L, 0:2 * L]).then_inc(neg_mm, 1)
            if front:
                pe.wait_ge(k_in, 16 * (b + 2))
                pe.wait_ge(q_in, 16 * (b + 2))
                pe_rows(pe, b + 1, nx, 0, ROWS_BY[0])
            if cur:
                pe.wait_ge(neg_in, 48 * (b + 1))
                pe_scores(pe, b, 0, par, masked_cur)
            for t in range(1, NT):
                units = iter(range(ROWS_BY[t - 1], ROWS_BY[t]) if front else ())

                def row():
                    u = next(units, None)
                    if u is not None:
                        pe_rows(pe, b + 1, nx, u, u + 1)
                for half in range(2):
                    if cur:
                        pe_scores(pe, b, t, par, masked_cur, (half,))
                    row()
                for half in range(2):
                    if cur:
                        pe_pv(pe, b, t - 1, par, (half,))
                    row()
                if front2 and t in KV_STEPS:
                    if cur and t == KV_STEPS[0]:
                        pe.wait_ge(negt_done, b + 1)
                    kv_chunk(pe, b + 2, KV_STEPS.index(t))
                    row()
                if front and t in TURN_STEPS:
                    turn_v(TURN_STEPS.index(t))
                    row()
                if prev and t == DEN_STEP:
                    pe.wait_ge(acc_read, b)
                    if front2:
                        pe.wait_ge(kv_read, NC * (b + 3))
                    elif cur:
                        pe.wait_ge(negt_done, b + 1)
                    else:
                        pe.wait_ge(x_done, b - 1)
                    pe.matmul(ps[:, MISC, 0:PW], den_sel[:], o_raw[:], start=True, stop=True).then_inc(den_mm, 1)
                if prev and t == OUT_STEP:
                    if front:
                        pe.wait_ge(vt_read, 3 * (b + 2))
                    else:
                        pe.wait_ge(inv_done, INV_PARTS * b)
                    pe.wait_ge(norm_done, b + 1)
                    first = natural(1 - par)
                    for c in range(2 * G):
                        mm = pe.matmul(ps[first:first + L, MISC, 0:E], o_n[:, c * L:(c + 1) * L], wo[:, c],
                                       start=(c == 0), stop=(c == 2 * G - 1))
                        if c == 2 * G - 1:
                            mm.then_inc(out_mm, 1)
                        if c % 2 == 1:
                            row()
                for _ in range(max(STEP_ROWS)):
                    row()
                if front and t == FLAG_STEP:
                    if prev:
                        pe.wait_ge(x_done, b)
                    else:
                        pe.wait_ge(vt_read, 3 * (b + 2))
                    wait_apart(pe, passed, abs_done, b + 2)
                    pe.matmul(ps[0:1, MISC, 0:1], mask_sum[0:L], ones[0:L], start=True, stop=True).then_inc(flag_mm, 1)

            if front:
                pe_rows(pe, b + 1, nx, ROWS_BY[NT - 1], ROWS_BY[NT])

        def act_scores(act, b, t):
            for i in range(2):
                act.wait_ge(score_mm, 24 * b + 2 * t + i + 1)
                wait = 12 * b + t - 1
                if not isinstance(wait, int) or wait > 0:
                    act.wait_ge(pv_mm, wait)
                act.activation(probs[t % 2][:, 2 * i:2 * i + 2, :], ps[0:ST, 2 * i:2 * i + 2, 0:PW],
                               ACT.Exp).then_inc(probs_done, 1)

        def act_body(act, b, par, prev, cur, front, front2, ctx3):
            nx = 1 - par
            if cur:
                act.wait_ge(negt_done, b + 1)
                for r in range(3):
                    act.dma_start(qs[par][SROWS + r:SROWS + r + 1].rearrange("p j h n -> p (j h n)"),
                                  neg_t[r * NR:(r + 1) * NR, :]).then_inc(neg_in, 16)
            if prev:
                act.wait_ge(pv_mm, NT * b)
                act.wait_ge(norm_done, b)
                act.activation(o_raw[:], ps[:, ACC, 0:PW], ACT.Copy).then_inc(acc_read, 1)
            if cur:
                act_scores(act, b, 0)
            for t in range(1, NT):
                if cur:
                    act_scores(act, b, t)
                if front2 and t in KV_STEPS:
                    if cur and t == KV_STEPS[0]:
                        act.wait_ge(split_done, b + 1)
                        act.wait_ge(vt_mm, 3 * (b + 1))
                    kv_evacuate(act, b + 2, KV_STEPS.index(t), kv_t[par])
                    if t == KV_STEPS[-1]:
                        round_high(act, b + 2, kv_t[par][0:KVH * HD])
                if front2 and t == MID_STEP:
                    round_middle(act, b + 2)
                if front and t == 5:
                    act.wait_ge(mask_in, 16 * (b + 2))
                    if not isinstance(b, int) or b >= 0:
                        act.wait_ge(flag_mm, b + 1)
                    act.activation(mask_abs[0:L], mask[nx][0:L], ACT.Abs,
                                   accum_out=mask_sum[0:L]).then_inc(abs_done, 1)

        def dve_body(dve, b, par, prev, cur, front, front2, ctx3):
            nx = 1 - par

            def reduce_rows(step, then=None):
                for u in range(ROWS_BY[step - 1] if step else 0, ROWS_BY[step]):
                    r, c = divmod(u, NC)
                    wait_apart(dve, passed, row_mm, NR * NC * (b + 1) + u + 1)
                    dve.tensor_tensor_reduce(
                        out=masked[:, u % 2], in0=ps[0:2 * L, FRONT[u % 2], 0:SC], in1=mask[nx][:, c * SC:(c + 1) * SC],
                        scale=1.0, scalar=NEG_BIG, op0=ALU.add, op1=ALU.max,
                        accum_out=part_max[:, r, c:c + 1]).then_inc(row_read, 1)
                    if then is not None:
                        then()

            if cur:
                dve.wait_ge(neg_mm, b + 1)
                if not isinstance(b, int) or b > 0:
                    dve.wait_ge(neg_in, 48 * b)
                dve.tensor_copy(neg_t[:], ps[0:3 * NR, MISC, :].bitcast(BF16)[:, 0:2 * L]).then_inc(negt_done, 1)
            if front:
                dve.wait_ge(mask_in, 16 * (b + 2))
                reduce_rows(0)
            for t in range(1, NT):
                inverses = iter(range(INV_PARTS) if prev and t == DEN_STEP + 1 else ())

                def invert():
                    i = next(inverses, None)
                    if i is not None:
                        if i == 0:
                            dve.wait_ge(den_mm, b)
                            dve.wait_ge(norm_done, b)
                        part = slice(i * PW // INV_PARTS, (i + 1) * PW // INV_PARTS)
                        dve.reciprocal(den_inv[:, part], ps[:, MISC, part]).then_inc(inv_done, 1)
                if front:
                    reduce_rows(t, invert)
                for _ in range(INV_PARTS):
                    invert()
                if front and t in TURN_STEPS:
                    c = TURN_STEPS.index(t)
                    dve.wait_ge(vt_mm, 3 * (b + 1) + c + 1)
                    if prev and c == 0:
                        dve.wait_ge(pv_mm, NT * b)
                    dve.tensor_copy(vp[nx][:, 4 * c:4 * c + 4, :, 0:HD],
                                    ps[0:ST, MISC, :].rearrange("p (t h) -> p t h", t=4)[:, :, HALF:P]
                                    .rearrange("p t (k d) -> p t k d", d=HD)).then_inc(vt_read, 1)
                if prev and t == OUT_STEP:
                    dve.wait_ge(out_mm, b + 1)
                    first = natural(1 - par)
                    tile = (b - 1) // 2
                    rows = x_nat[first:first + L, bass.ds(tile, 1), :].rearrange("p o e -> p (o e)")
                    dve.tensor_tensor(rows, ps[first:first + L, MISC, 0:E], rows, ALU.add).then_inc(x_done, 1)
                if front and t == FLAG_STEP:
                    dve.wait_ge(flag_mm, b + 2)
                    dve.tensor_scalar(flag[0:1, nx:nx + 1], ps[0:1, MISC, 0:1], 0.0, None,
                                      ALU.is_gt).then_inc(flag_done, 1)
            if front:
                reduce_rows(NT)
                k = CHAIN * (b + 1)
                dve.wait_ge(row_read, NR * NC * (b + 2))
                if not isinstance(b, int) or b >= 0:
                    dve.wait_ge(neg_mm, b + 1)
                dve.tensor_reduce(row_max[:], part_max[:], AX_X, ALU.max).then_inc(chain, 1)
                dve.wait_ge(chain, k + 1)
                dve.tensor_scalar(neg_piece[:, 0], row_max[:], -1.0, None, ALU.mult).then_inc(chain, 1)
                dve.wait_ge(chain, k + 2)
                dve.scalar_tensor_tensor(neg_rest[:], row_max[:], -1.0, neg_piece[:, 0], ALU.mult,
                                         ALU.subtract).then_inc(chain, 1)
                dve.wait_ge(chain, k + 3)
                dve.tensor_copy(neg_piece[:, 1], neg_rest[:]).then_inc(chain, 1)
                dve.wait_ge(chain, k + 4)
                dve.tensor_tensor(neg_piece[:, 2], neg_rest[:], neg_piece[:, 1], ALU.subtract).then_inc(chain, 1)

        def pool_body(pool, b, par, prev, cur, front, front2, ctx3):
            if front2:
                split_k(pool, b + 2, kv_t[par][0:KVH * HD])
            if prev:
                pool.wait_ge(inv_done, INV_PARTS * b)
                pool.wait_ge(out_mm, b)
                pool.tensor_tensor(o_n[:], o_raw[:], den_inv[:], ALU.mult).then_inc(norm_done, 1)

        def all_bodies(eng, body):
            def one(b, par):
                known = isinstance(b, int)
                body(eng, b, par, not known or b >= 1, not known or 0 <= b < B, not known or b + 1 < B,
                     not known or b + 2 < B, not known or b + 3 < B)
            one(-1, 1)
            one(0, 0)
            with eng.Fori(1, B - 4, 2) as b:
                one(b, 1)
                one(b + 1, 0)
            for b in range(B - 3, B + 1):
                one(b, b % 2)

        with nc.Block() as block:
            @block.sync
            def _(sp):
                all_bodies(sp, sp_body)
                sp.wait_ge(k_out, 48 * B)

            @block.tensor
            def _(pe):
                pe.sem_inc(out_mm, 1)
                all_bodies(pe, pe_body)

            @block.scalar
            def _(act):
                all_bodies(act, act_body)

            @block.vector
            def _(dve):
                all_bodies(dve, dve_body)

            @block.gpsimd
            def _(pool):
                pool.sem_inc(norm_done, 1)
                all_bodies(pool, pool_body)
        clear(nc, sems)


CB = 8
CP = CB // 2
N = CB * L
H, HS = 32, 8
MIX = (1, 0, 2, 3, 4)
VEC = ("ln1_w", "ln1_b", "ln2_w", "ln2_b", "maa_x", "m0", "m1", "m2", "m3", "m4", "td", "gn_w", "gn_b", "u",
       "fmk", "fmr")
LN_EPS = 1e-5
PRODUCTS = {"xt": 2, "lora": 2, "mix": 10, "dec1": 1, "dec2": 2, "key": 2, "val": 2, "rec": 2, "gate": 2,
            "vb": 16, "bonus": 2, "y": 2, "mean": 2, "var": 2, "att": 2, "xt2": 2, "fk": 2, "fr": 2, "fv": 2}


def product_order():
    out = [("xt", 0), ("xt", 1), ("lora", 0), ("lora", 1)]
    projections = {0: ["key"], 1: ["dec1", "dec2"], 2: ["val"], 3: ["rec"], 4: ["gate"]}
    for n in range(len(MIX) + 1):
        if n < len(MIX):
            out += [("mix", 2 * n), ("mix", 2 * n + 1)]
        if n >= 1:
            for name in projections[MIX[n - 1]]:
                out += [(name, i) for i in range(PRODUCTS[name])]
    out += [("vb", i) for i in range(HS + 2)] + [("bonus", 0)]
    out += [("vb", i) for i in range(HS + 2, KC * HS)] + [("bonus", 1)]
    for name in ("mean", "var", "att", "xt2", "fk", "fr", "fv"):
        out += [(name, i) for i in range(2)]
    return out


def rwkv(nc, x_nat, a, tag, after_layer0, passed):
    sems = []
    with ExitStack() as ctx:
        def sb(name, shape, dt=F32):
            return ctx.enter_context(nc.sbuf_tensor(f"{tag}_{name}", shape, dt))

        def sem(name):
            sems.append(ctx.enter_context(nc.semaphore(f"{tag}_{name}")))
            return sems[-1]

        ident = sb("ident", [P, P])
        vec = sb("vec", [P, KC, len(VEC)])
        w1 = sb("w1", [P, KC, 2 * P])
        w2 = sb("w2", [P, 5, E])
        dw1 = sb("dw1", [P, KC, P])
        dw2 = sb("dw2", [P, E])
        wr, wk, wv, wg, wo, fk, fr, fv = [sb(n, [P, KC, E]) for n in "wr wk wv wg wo fk fr fv".split()]
        vsel = sb("vsel", [P, HS, P])
        osel = sb("osel", [P, HS, P])
        head_sum = sb("head_sum", [P, P])
        head_mean = sb("head_mean", [P, P])
        st = sb("st", [P, 2, KC, B])
        s0 = sb("s0", [P, KC, HS, B])
        first_loads = [(ident, "ident"), (vec, tag + "vec"), (st, "st")]
        loads = [(w1, tag + "w1"), (w2, tag + "w2"), (dw1, tag + "dw1"),
                 (dw2, tag + "dw2"), (wr, tag + "wr"), (wk, tag + "wk"), (wv, tag + "wv"), (wg, tag + "wg"),
                 (wo, tag + "wo"), (fk, tag + "fk"), (fr, tag + "fr"), (fv, tag + "fv"), (vsel, "vsel"),
                 (osel, "osel"), (head_sum, "head_sum"), (head_mean, "head_mean"), (s0, "s0")]
        if after_layer0:
            ln0_g, ln0_b = sb("ln0_g", [P, E]), sb("ln0_b", [P, E])
            first_loads += [(ln0_g, "ln0_g"), (ln0_b, "ln0_b")]
        eps = sb("eps", [P, 2])
        stats = sb("stats", [P, CP, 6])
        mv = sb("mv", [P, CP, 2])
        sd = sb("sd", [P, CP])
        rstd = sb("rstd", [P, CP])
        shift = sb("shift", [P, CP])
        xhat = sb("xhat", [P, CP, E])
        xn = sb("xn", [P, KC, N])
        sx = sb("sx", [P, KC, N])
        xx = sb("xx", [P, KC, N])
        th = sb("th", [P, KC, N])
        part = sb("part", [P, 2, KC, N])
        mixed = sb("mixed", [P, 2, KC, N])
        hw = sb("hw", [P, N])
        dec_e = sb("dec_e", [P, KC, N])
        w = sb("w", [P, KC, N])
        kt, vt, rt, gt = [sb(n, [P, KC, N]) for n in ("kt", "vt", "rt", "gt")]
        g_th = sb("g_th", [P, KC, N])
        kv = sb("kv", [P, 3, N])
        state = sb("state", [P, 3, N])
        rs = sb("rs", [P, 3, N])
        ruk = sb("ruk", [P, KC, N])
        cv = sb("cv", [P, KC, N])
        yo = sb("yo", [P, KC, N])
        dev = sb("dev", [P, KC, N])
        sq = sb("sq", [P, KC, N])
        gsd = sb("gsd", [P, KC, N])
        grs = sb("grs", [P, KC, N])
        og = sb("og", [P, KC, N + 8])
        xk2 = sb("xk2", [P, KC, N])
        xr2 = sb("xr2", [P, KC, N + 8])
        relu = sb("relu", [P, KC, N])
        kk = sb("kk", [P, KC, N + 8])
        r_th = sb("r_th", [P, 2, 2 * E])
        rv = sb("rv", [P, 2, 2 * E])
        ps = ctx.enter_context(nc.psum_tensor(f"ps_{tag}", [P, 8, 512], F32))

        made = {n: sem(n + "_made") for n in PRODUCTS}
        used = {n: sem(n + "_used") for n in PRODUCTS}
        names = ("first_loaded loaded preset stat aggr0 aggr1 aggr2 sd0 sd1 sd2 r0 r1 r2 z0 z1 z2 ln0a ln0b ln0c xhat1 xhat2 "
                 "sxa sxb xx part mixed kv_first state rs ruk sq grs og xk2 xr2 "
                 "sx2a sx2b kk x2 dec_w g_th summed").split()
        s = {n: sem(n) for n in names}
        order = product_order()
        bank = {}
        before = {}
        last = {}
        for lap in range(2):
            n = 0
            for unit in order:
                b = n % 7
                n += 1
                before[unit] = (last.get(b), lap)
                bank[unit] = b
                last[b] = (unit, lap)
        Y_BANK = 7

        def v(k, name):
            i = VEC.index(name)
            return vec[:, k, i:i + 1]

        def by_batch(ap):
            return ap.rearrange("p (b l) -> p b l", l=L)

        with nc.Block() as block:
            @block.sync
            def _(sp):
                for dst, name in first_loads:
                    sp.dma_start(dst[:], a[name]).then_inc(s["first_loaded"], 16)
                for dst, name in loads:
                    sp.dma_start(dst[:], a[name]).then_inc(s["loaded"], 16)
                sp.wait_ge(s["loaded"], 16 * len(loads))

            @block.tensor
            def _(pe):
                pe.wait_ge(s["first_loaded"], 16 * len(first_loads))
                pe.wait_ge(s["preset"], 6)
                cell = {}

                def room(unit, c):
                    (prev, prev_lap), lap = before[unit]
                    name, i = prev
                    count = PRODUCTS[name]
                    if prev_lap == lap:
                        pe.wait_ge(used[name], count * c + i + 1)
                    elif not isinstance(c, int) or c > 0:
                        pe.wait_ge(used[name], count * c)

                def out(unit, rows=P, n=N):
                    return ps[0:rows, bank[unit], 0:n]

                def project(unit, c, w_sb, x_sb, m):
                    room(unit, c)
                    for k in range(KC):
                        mm = pe.matmul(out(unit), w_sb[:, k, m * P:(m + 1) * P], x_sb[:, k, 0:N],
                                       start=(k == 0), stop=(k == KC - 1))
                    mm.then_inc(made[unit[0]], 1)

                def natural_rows_of(unit, c, x_sb, w_sb):
                    room(unit, c)
                    i = unit[1]
                    for g in range(2):
                        for r in range(2):
                            t0 = ((2 * i + g) * 2 + r) * L
                            for k in range(KC):
                                mm = pe.matmul(ps[HALF * r:HALF * r + HALF, bank[unit], g * E:(g + 1) * E],
                                               x_sb[:, k, t0:t0 + HALF], w_sb[:, k, :],
                                               start=(k == 0), stop=(k == KC - 1))
                    mm.then_inc(made[unit[0]], 1)

                def turn(unit, c):
                    room(unit, c)
                    for g in range(CP):
                        mm = pe.transpose(ps[:, bank[unit], g * P:(g + 1) * P],
                                          xhat[:, g, unit[1] * P:(unit[1] + 1) * P], ident[:])
                    mm.then_inc(made[unit[0]], 1)

                def chunk(c):
                    for unit in order:
                        name, i = unit
                        if name == "xt":
                            pe.wait_ge(s["xhat1"], CP * (c + 1))
                            turn(unit, c)
                        elif name == "xt2":
                            pe.wait_ge(s["xhat2"], CP * (c + 1))
                            turn(unit, c)
                        elif name == "lora":
                            if isinstance(c, int) and i == 0:
                                pe.wait_ge(s["loaded"], 16 * len(loads))
                            pe.wait_ge(s["xx"], 2 * (c + 1))
                            project(unit, c, w1, xx, i)
                        elif name == "mix":
                            j = MIX[i // 2]
                            pe.wait_ge(used["lora"], 2 * (c + 1))
                            room(unit, c)
                            pe.matmul(out(unit), w2[:, j, (i % 2) * P:(i % 2 + 1) * P], th[:, j // 4, :],
                                      start=True, stop=True).then_inc(made["mix"], 1)
                        elif name in ("dec1", "key", "val", "rec", "gate"):
                            n = MIX.index({"dec1": 1, "key": 0, "val": 2, "rec": 3, "gate": 4}[name])
                            pe.wait_ge(s["mixed"], 5 * c + n + 1)
                            w_sb = {"dec1": dw1, "key": wk, "val": wv, "rec": wr, "gate": wg}[name]
                            project(unit, c, w_sb, mixed[:, n % 2], i)
                        elif name == "dec2":
                            pe.wait_ge(used["dec1"], c + 1)
                            room(unit, c)
                            pe.matmul(out(unit), dw2[:, i * P:(i + 1) * P], hw[:], start=True,
                                      stop=True).then_inc(made["dec2"], 1)
                        elif name == "vb":
                            k, j = i // HS, i % HS
                            if j == 0:
                                pe.wait_ge(used["val"], 2 * c + k + 1)
                            room(unit, c)
                            pe.matmul(out(unit), vsel[:, j], vt[:, k], start=True, stop=True).then_inc(made["vb"], 1)
                            if i >= 2:
                                sum_state(c, i - 2)
                        elif name == "bonus":
                            pe.wait_ge(s["ruk"], 2 * c + i + 1)
                            room(unit, c)
                            pe.matmul(out(unit), head_sum[:], ruk[:, i], start=True, stop=True)\
                              .then_inc(made["bonus"], 1)
                            if i == 1:
                                sum_state(c, KC * HS - 2)
                                sum_state(c, KC * HS - 1)
                        elif name == "mean":
                            pe.wait_ge(used["y"], 2 * c + i + 1)
                            room(unit, c)
                            pe.matmul(out(unit), head_mean[:], yo[:, i], start=True, stop=True)\
                              .then_inc(made["mean"], 1)
                        elif name == "var":
                            pe.wait_ge(s["sq"], 2 * c + i + 1)
                            room(unit, c)
                            pe.matmul(out(unit), head_mean[:], sq[:, i], start=True, stop=True)\
                              .then_inc(made["var"], 1)
                        elif name == "att":
                            pe.wait_ge(s["og"], 2 * (c + 1))
                            natural_rows_of(unit, c, og, wo)
                        elif name == "fk":
                            pe.wait_ge(s["xk2"], 2 * (c + 1))
                            project(unit, c, fk, xk2, i)
                        elif name == "fr":
                            pe.wait_ge(s["xr2"], 2 * (c + 1))
                            natural_rows_of(unit, c, xr2, fr)
                        elif name == "fv":
                            pe.wait_ge(s["kk"], 2 * (c + 1))
                            natural_rows_of(unit, c, kk, fv)

                def sum_state(c, i):
                    k, j = divmod(i, HS)
                    if j == 0 and (not isinstance(c, int) or c + k > 0):
                        pe.wait_ge(used["y"], 2 * c + k)
                    pe.wait_ge(s["rs"], 16 * c + HS * k + j + 1)
                    mm = pe.matmul(ps[:, Y_BANK, 0:N], osel[:, j], rs[:, (HS * k + j) % 3], start=(j == 0),
                                   stop=(j == HS - 1))
                    mm.then_inc(s["summed"], 1)

                chunk(0)
                with pe.Fori(1, B // CB) as c:
                    chunk(c)

            @block.scalar
            def _(act):
                act.wait_ge(s["first_loaded"], 16 * len(first_loads))
                act.wait_ge(s["preset"], 6)

                def deviation(c, n, which):
                    act.wait_ge(s[f"aggr{n}"], CP * (c + 1))
                    act.activation(sd[:], mv[:, :, 1], ACT.Sqrt, bias=eps[:, which:which + 1]).then_inc(s[f"sd{n}"], 1)

                def read(name, c, i, out_ap, func, in_ap=None, **more):
                    act.wait_ge(made[name], PRODUCTS[name] * c + i + 1)
                    in_ap = ps[:, bank[name, i], 0:N] if in_ap is None else in_ap
                    return act.activation(out_ap, in_ap, func, **more)

                def chunk(c):
                    if after_layer0:
                        deviation(c, 0, 1)
                    deviation(c, 1, 0)
                    for k in range(KC):
                        src = ps[:, bank["xt", k], :].rearrange("p (b l) -> p b l", l=HALF)[:, :, 0:L]
                        read("xt", c, k, by_batch(xn[:, k]), ACT.Identity, src, scale=v(k, "ln1_w"),
                             bias=v(k, "ln1_b")).then_inc(used["xt"], 1)
                    for i in range(2):
                        read("lora", c, i, th[:, i], ACT.Tanh).then_inc(used["lora"], 1)
                    read("dec1", c, 0, hw[:], ACT.Tanh).then_inc(used["dec1"], 1)
                    for k in range(KC):
                        read("dec2", c, k, dec_e[:, k], ACT.Exp, bias=v(k, "td")).then_inc(used["dec2"], 1)
                    for k in range(KC):
                        act.wait_ge(used["dec2"], 2 * c + k + 1)
                        act.activation(by_batch(w[:, k])[:, :, 1:L], by_batch(dec_e[:, k])[:, :, 0:L - 1], ACT.Exp,
                                       scale=-1.0).then_inc(s["dec_w"], 1)
                    for name, dst in (("key", kt), ("val", vt), ("rec", rt)):
                        for k in range(KC):
                            read(name, c, k, dst[:, k], ACT.Copy).then_inc(used[name], 1)
                    for k in range(KC):
                        read("gate", c, k, g_th[:, k], ACT.Tanh, scale=0.5).then_inc(s["g_th"], 1)
                    for k in range(KC):
                        act.wait_ge(used["mean"], 2 * c + k + 1)
                        act.activation(sq[:, k], dev[:, k], ACT.Square).then_inc(s["sq"], 1)
                    for k in range(KC):
                        read("var", c, k, gsd[:, k], ACT.Sqrt, bias=eps[:, 0:1]).then_inc(used["var"], 1)
                    deviation(c, 2, 0)
                    for k in range(KC):
                        src = ps[:, bank["xt2", k], :].rearrange("p (b l) -> p b l", l=HALF)[:, :, 0:L]
                        read("xt2", c, k, by_batch(xn[:, k]), ACT.Identity, src, scale=v(k, "ln2_w"),
                             bias=v(k, "ln2_b")).then_inc(used["xt2"], 1)
                    for k in range(KC):
                        read("fk", c, k, relu[:, k], ACT.Relu).then_inc(used["fk"], 1)
                    for i in range(2):
                        read("fr", c, i, r_th[:, i], ACT.Tanh, ps[:, bank["fr", i], :], scale=0.5)\
                            .then_inc(used["fr"], 1)

                with act.Fori(0, B // CB) as c:
                    chunk(c)

            @block.vector
            def _(dve):
                dve.wait_ge(s["first_loaded"], 16 * len(first_loads))
                dve.wait_ge(s["preset"], 6)

                def normalize(c, n, rows, done):
                    for g in range(CP):
                        dve.bn_stats(stats[:, g], rows[:, g]).then_inc(s["stat"], 1)
                    per = CP * (3 if after_layer0 else 2)
                    first = {0: 0, 1: CP if after_layer0 else 0, 2: per - CP}[n]
                    wait_apart(dve, passed, s["stat"], per * c + first + CP)
                    for g in range(CP):
                        dve.bn_aggr(mv[:, g], stats[:, g]).then_inc(s[f"aggr{n}"], 1)
                    dve.wait_ge(s[f"sd{n}"], c + 1)
                    dve.reciprocal(rstd[:], sd[:]).then_inc(s[f"r{n}"], 1)
                    dve.wait_ge(s[f"r{n}"], c + 1)
                    dve.scalar_tensor_tensor(shift[:], mv[:, :, 0], -1.0, rstd[:], ALU.mult, ALU.mult)\
                       .then_inc(s[f"z{n}"], 1)
                    dve.wait_ge(s[f"z{n}"], c + 1)
                    for g in range(CP):
                        dve.tensor_scalar(xhat[:, g], rows[:, g], rstd[:, g:g + 1], shift[:, g:g + 1],
                                          ALU.mult, ALU.add).then_inc(s[done], 1)

                def token_shift(c, row, xa, xb):
                    name = "xt" if row == 1 else "xt2"
                    dve.wait_ge(used[name], 2 * (c + 1))
                    x4 = xn[:].rearrange("p k (b l) -> p k b l", l=L)
                    s4 = sx[:].rearrange("p k (b l) -> p k b l", l=L)
                    dve.tensor_tensor(s4[:, :, :, 1:L], x4[:, :, :, 0:L - 1], x4[:, :, :, 1:L], ALU.subtract)\
                       .then_inc(s[xa], 1)
                    dve.tensor_tensor(s4[:, :, :, 0], st[:, row][:, :, bass.ds(c * CB, CB)], x4[:, :, :, 0],
                                      ALU.subtract).then_inc(s[xb], 1)
                    dve.wait_ge(s[xa], c + 1)
                    dve.wait_ge(s[xb], c + 1)

                def chunk(c):
                    rows = x_nat[:, bass.ds(c * CP, CP), :]
                    if after_layer0:
                        normalize(c, 0, rows, "ln0a")
                        dve.wait_ge(s["ln0a"], CP * (c + 1))
                        dve.tensor_tensor(xhat[:], xhat[:], ln0_g[:].unsqueeze(1).to_broadcast([P, CP, E]), ALU.mult)\
                           .then_inc(s["ln0b"], 1)
                        dve.wait_ge(s["ln0b"], c + 1)
                        dve.tensor_tensor(rows, xhat[:], ln0_b[:].unsqueeze(1).to_broadcast([P, CP, E]), ALU.add)\
                           .then_inc(s["ln0c"], 1)
                        wait_apart(dve, passed, s["ln0c"], c + 1)
                    normalize(c, 1, rows, "xhat1")
                    token_shift(c, 1, "sxa", "sxb")
                    for k in range(KC):
                        dve.scalar_tensor_tensor(xx[:, k], sx[:, k], v(k, "maa_x"), xn[:, k], ALU.mult, ALU.add)\
                           .then_inc(s["xx"], 1)
                    for n, j in enumerate(MIX):
                        for k in range(KC):
                            dve.wait_ge(made["mix"], 10 * c + 2 * n + k + 1)
                            if n >= 2:
                                dve.wait_ge(s["mixed"], 5 * c + n - 1)
                            dve.scalar_tensor_tensor(part[:, n % 2, k], ps[:, bank["mix", 2 * n + k], 0:N],
                                                     v(k, f"m{j}"), sx[:, k], ALU.add, ALU.mult)\
                               .then_inc(used["mix"], 1)
                    dve.wait_ge(used["rec"], 2 * (c + 1))
                    for k in range(KC):
                        dve.scalar_tensor_tensor(ruk[:, k], rt[:, k], v(k, "u"), kt[:, k], ALU.mult, ALU.mult)\
                           .then_inc(s["ruk"], 1)
                    for k in range(KC):
                        dve.wait_ge(made["gate"], 2 * c + k + 1)
                        dve.wait_ge(s["g_th"], 2 * c + k + 1)
                        dve.scalar_tensor_tensor(gt[:, k], g_th[:, k], 1.0, ps[:, bank["gate", k], 0:N],
                                                 ALU.add, ALU.mult).then_inc(used["gate"], 1)

                    def head_output(k):
                        dve.wait_ge(made["bonus"], 2 * c + k + 1)
                        dve.tensor_tensor(cv[:, k], ps[:, bank["bonus", k], 0:N], vt[:, k], ALU.mult)\
                           .then_inc(used["bonus"], 1)
                        dve.wait_ge(s["summed"], 16 * c + HS * (k + 1))
                        dve.wait_ge(used["bonus"], 2 * c + k + 1)
                        dve.tensor_tensor(yo[:, k], ps[:, Y_BANK, 0:N], cv[:, k], ALU.add).then_inc(used["y"], 1)

                    dve.wait_ge(s["dec_w"], 2 * (c + 1))
                    for i in range(KC * HS + 1):
                        if i < KC * HS:
                            k, j = divmod(i, HS)
                            dve.wait_ge(made["vb"], 16 * c + i + 1)
                            if i >= 3:
                                dve.wait_ge(s["state"], 16 * c + i - 2)
                            dve.tensor_tensor(by_batch(kv[:, i % 3])[:, :, 1:L], by_batch(kt[:, k])[:, :, 0:L - 1],
                                              by_batch(ps[:, bank["vb", i], 0:N])[:, :, 0:L - 1], ALU.mult)\
                               .then_inc(used["vb"], 1)
                        if i >= 1:
                            m = i - 1
                            k = m // HS
                            dve.wait_ge(used["vb"], 16 * c + m + 1)
                            dve.wait_ge(s["kv_first"], 16 * c + m + 1)
                            if m >= 3:
                                dve.wait_ge(s["rs"], 16 * c + m - 2)
                            dve.tensor_tensor_scan(state[:, m % 3], w[:, k], kv[:, m % 3], 0.0, ALU.mult, ALU.add)\
                               .then_inc(s["state"], 1)
                        if i == HS + 2:
                            head_output(0)
                    head_output(1)
                    for k in range(KC):
                        dve.wait_ge(made["mean"], 2 * c + k + 1)
                        dve.tensor_tensor(dev[:, k], yo[:, k], ps[:, bank["mean", k], 0:N], ALU.subtract)\
                           .then_inc(used["mean"], 1)
                    for k in range(KC):
                        dve.wait_ge(used["var"], 2 * c + k + 1)
                        dve.reciprocal(grs[:, k], gsd[:, k]).then_inc(s["grs"], 1)
                        dve.wait_ge(s["grs"], 3 * (2 * c + k) + 1)
                        dve.tensor_tensor(yo[:, k], dev[:, k], grs[:, k], ALU.mult).then_inc(s["grs"], 1)
                        dve.wait_ge(s["grs"], 3 * (2 * c + k) + 2)
                        dve.tensor_scalar(yo[:, k], yo[:, k], v(k, "gn_w"), v(k, "gn_b"), ALU.mult, ALU.add)\
                           .then_inc(s["grs"], 1)
                        dve.wait_ge(s["grs"], 3 * (2 * c + k) + 3)
                        dve.scalar_tensor_tensor(og[:, k, 0:N], yo[:, k], 0.5, gt[:, k], ALU.mult, ALU.mult)\
                           .then_inc(s["og"], 1)
                    for i in range(2):
                        dve.wait_ge(made["att"], 2 * c + i + 1)
                        two = x_nat[:, bass.ds(c * CP + 2 * i, 2), :]
                        dve.tensor_tensor(two, ps[:, bank["att", i], :].rearrange("p (g e) -> p g e", g=2), two,
                                          ALU.add).then_inc(used["att"], 1)
                    wait_apart(dve, passed, used["att"], 2 * (c + 1))
                    normalize(c, 2, rows, "xhat2")
                    token_shift(c, 0, "sx2a", "sx2b")
                    for name, dst, vname in (("xk2", xk2, "fmk"), ("xr2", xr2, "fmr")):
                        for k in range(KC):
                            dve.scalar_tensor_tensor(dst[:, k, 0:N], sx[:, k], v(k, vname), xn[:, k], ALU.mult,
                                                     ALU.add).then_inc(s[name], 1)
                    for i in range(2):
                        dve.wait_ge(made["fv"], 2 * c + i + 1)
                        dve.wait_ge(used["fr"], 2 * c + i + 1)
                        dve.scalar_tensor_tensor(rv[:, i], r_th[:, i], 1.0, ps[:, bank["fv", i], :], ALU.add,
                                                 ALU.mult).then_inc(used["fv"], 1)
                    for i in range(2):
                        dve.wait_ge(used["fv"], 2 * c + i + 1)
                        two = x_nat[:, bass.ds(c * CP + 2 * i, 2), :]
                        dve.scalar_tensor_tensor(two, rv[:, i].rearrange("p (g e) -> p g e", g=2), 0.5, two,
                                                 ALU.mult, ALU.add).then_inc(s["x2"], 1)
                    dve.wait_ge(s["x2"], 2 * (c + 1))

                with dve.Fori(0, B // CB) as c:
                    chunk(c)

            @block.gpsimd
            def _(pool):
                sets = [(eps[:, 0:1], LN_EPS), (eps[:, 1:2], 1e-6), (w[:], 0.0), (og[:, :, N:N + 8], 0.0),
                        (xr2[:, :, N:N + 8], 0.0), (kk[:, :, N:N + 8], 0.0)]
                for n, (where, value) in enumerate(sets):
                    pool.memset(where, value).then_inc(s["preset"], 1)
                    pool.wait_ge(s["preset"], n + 1)
                pool.wait_ge(s["loaded"], 16 * len(loads))

                def chunk(c):
                    for n in range(len(MIX)):
                        pool.wait_ge(used["mix"], 10 * c + 2 * n + 2)
                        if n >= 2:
                            name = ("dec1", "key", "val")[n - 2]
                            pool.wait_ge(made[name], PRODUCTS[name] * (c + 1))
                        pool.tensor_tensor(mixed[:, n % 2], part[:, n % 2], xn[:], ALU.add).then_inc(s["mixed"], 1)
                    pool.wait_ge(used["rec"], 2 * (c + 1))
                    for i in range(KC * HS + 1):
                        if i < KC * HS:
                            k, j = divmod(i, HS)
                            if i >= 3:
                                pool.wait_ge(s["state"], 16 * c + i - 2)
                            pool.tensor_copy(by_batch(kv[:, i % 3])[:, :, 0], s0[:, k, j, :][:, bass.ds(c * CB, CB)])\
                                .then_inc(s["kv_first"], 1)
                        if i >= 1:
                            m = i - 1
                            k = m // HS
                            pool.wait_ge(s["state"], 16 * c + m + 1)
                            if m >= 3:
                                pool.wait_ge(s["summed"], 16 * c + m - 2)
                            pool.tensor_tensor(rs[:, m % 3], rt[:, k], state[:, m % 3], ALU.mult).then_inc(s["rs"], 1)
                    for k in range(KC):
                        pool.wait_ge(used["fk"], 2 * c + k + 1)
                        pool.tensor_tensor(kk[:, k, 0:N], relu[:, k], relu[:, k], ALU.mult).then_inc(s["kk"], 1)

                with pool.Fori(0, B // CB) as c:
                    chunk(c)
        clear(nc, sems)


NH2, HD2 = 16, 16
NQ = 4
PARTS = ((0, 1, 2), (3,))
SQ = S // NQ
TQ = SQ // ST
NP = NH2 // 2
SLOT = NH2 // KC * L
TILES = NQ * TQ + 1
S2 = S + L
MASKED = -1.0e30
RMS_EPS = 1e-6
FF = 4 * E
FC = FF // P


def latent_attention(nc, x_nat, y_nat, a, passed):
    mb_scr = nc.dram_tensor("mb_scr", [B, NQ, SQ], F32).ap()
    sems = []
    with ExitStack() as ctx:
        def sb(name, shape, dt=F32):
            return ctx.enter_context(nc.sbuf_tensor("c_" + name, shape, dt))

        def sem(name):
            sems.append(ctx.enter_context(nc.semaphore("c_" + name)))
            return sems[-1]

        ident = sb("ident", [P, P])
        identb = sb("identb", [P, P], BF16)
        kv_w = sb("kv_w", [P, KC, 2 * E])
        kv_b = sb("kv_b", [P, 4])
        q_w = sb("q_w", [P, KC, E])
        q_b = sb("q_b", [P, KC])
        out_w = sb("out_w", [P, KC, E])
        out_b = sb("out_b", [P, E])
        head_scale = sb("head_scale", [P, 8])
        odd_mask = sb("odd_mask", [P, 2])
        qt = sb("qt", [P, KC, T])
        kv_lat = sb("kv_lat", [P, 4, T])
        mask_i = sb("mask_i", [P, SQ], I32)
        mask_b = sb("mask_b", [P, SQ])
        mask_a = sb("mask_a", [P, SQ])
        active = sb("active", [P, 1])
        part_active = sb("part_active", [1, B, len(PARTS)])
        flags = sb("flags", [1, B, len(PARTS)], I32)
        mask_ti = sb("mask_ti", [ST, B, NT], I32)
        bias_t = sb("bias_t", [ST, B, NT])
        ps = ctx.enter_context(nc.psum_tensor("ps_c", [P, 8, 512], F32))
        loads = [(ident, "ident"), (kv_w, "c_kv_w"), (kv_b, "c_kv_b"), (q_w, "c_q_w"),
                 (q_b, "c_q_b"), (out_w, "c_out_w"), (out_b, "c_out_b"), (head_scale, "head_scale"),
                 (odd_mask, "odd_mask"), (mask_i, "mask_q"), (mask_ti, "mask_t")]

        with ExitStack() as early:
            x_t = early.enter_context(nc.sbuf_tensor("c_x_t", [P, KC, T], F32))
            loaded, turned, copied, made, kept, neg, act_row, act_t, fl, bt, yb, mb_out = [
                sem("0_" + n)
                for n in "loaded turned copied made kept neg act_row act_t fl bt yb mb_out".split()]
            CW = T // 4
            G4 = PAIRS // 4
            UNITS = [(c, m) for c in range(4) for m in range(6)]
            with nc.Block() as block:
                @block.sync
                def _(sp):
                    for dst, name in loads:
                        sp.dma_start(dst[:], a[name]).then_inc(loaded, 16)
                    sp.wait_ge(neg, 1)
                    sp.dma_start(mb_scr.rearrange("b q s -> (b q) s"), mask_b[:]).then_inc(mb_out, 16)
                    sp.wait_ge(mb_out, 16)

                @block.tensor
                def _(pe):
                    pe.wait_ge(loaded, 16 * len(loads))
                    for c in range(4):
                        for k in range(KC):
                            for g in range(G4):
                                mm = pe.transpose(ps[:, 2 * c + k, g * P:(g + 1) * P],
                                                  x_nat[:, c * G4 + g, k * P:(k + 1) * P], ident[:])
                            mm.then_inc(turned, 1)
                    for n, (c, m) in enumerate(UNITS):
                        pe.wait_ge(copied, 2 * c + 2)
                        if n < 8:
                            pe.wait_ge(copied, n + 1)
                        else:
                            pe.wait_ge(kept, n - 7)
                        for k in range(KC):
                            w = q_w[:, k, m * P:(m + 1) * P] if m < 2 else kv_w[:, k, (m - 2) * P:(m - 1) * P]
                            mm = pe.matmul(ps[:, n % 8, 0:CW], w, x_t[:, k, c * CW:(c + 1) * CW],
                                           start=(k == 0), stop=(k == KC - 1))
                        mm.then_inc(made, 1)
                    pe.wait_ge(act_row, 1)
                    pe.wait_ge(kept, len(UNITS) - 7)
                    pe.transpose(ps[0:1, 0, 0:P], active[:], ident[:]).then_inc(act_t, 1)

                @block.scalar
                def _(act):
                    act.wait_ge(loaded, 16 * len(loads))
                    for c in range(4):
                        for k in range(KC):
                            act.wait_ge(turned, 2 * c + k + 1)
                            act.activation(x_t[:, k, c * CW:(c + 1) * CW].rearrange("p (b l) -> p b l", l=L),
                                           ps[:, 2 * c + k, :].rearrange("p (b l) -> p b l", l=HALF)[:, :, 0:L],
                                           ACT.Copy).then_inc(copied, 1)
                    for n, (c, m) in enumerate(UNITS):
                        act.wait_ge(made, n + 1)
                        if m < 2:
                            dst, bias = qt[:, m, c * CW:(c + 1) * CW], q_b[:, m:m + 1]
                        else:
                            dst, bias = kv_lat[:, m - 2, c * CW:(c + 1) * CW], kv_b[:, m - 2:m - 1]
                        act.activation(dst, ps[:, n % 8, 0:CW], ACT.Identity, bias=bias).then_inc(kept, 1)

                @block.vector
                def _(dve):
                    dve.wait_ge(loaded, 16 * len(loads))
                    dve.tensor_copy(identb[:], ident[:]).then_inc(bt, 1)
                    dve.tensor_scalar(mask_b[:], mask_i[:], 0.0, MASKED, ALU.is_equal, ALU.mult).then_inc(neg, 1)
                    dve.tensor_scalar(mask_a[:], mask_i[:], 0.0, None, ALU.not_equal).then_inc(fl, 1)
                    dve.wait_ge(fl, 1)
                    dve.tensor_reduce(active[:], mask_a[:], AX_X, ALU.max).then_inc(act_row, 1)
                    dve.tensor_scalar(bias_t[:], mask_ti[:], 0.0, MASKED, ALU.is_equal, ALU.mult).then_inc(bt, 1)
                    dve.tensor_tensor(y_nat[:], x_nat[:], out_b[:].unsqueeze(1).to_broadcast([P, PAIRS, E]),
                                      ALU.add).then_inc(yb, 1)
                    dve.wait_ge(act_t, 1)
                    active_q = ps[0:1, 0, 0:P].rearrange("o (b q) -> o b q", q=NQ)
                    for i, part in enumerate(PARTS):
                        dve.tensor_reduce(part_active[:, :, i], active_q[:, :, part[0]:part[-1] + 1], AX_X, ALU.max)\
                           .then_inc(fl, 1)
                    dve.wait_ge(fl, 1 + len(PARTS))
                    dve.tensor_copy(flags[:], part_active[:]).then_inc(fl, 1)

        ctx_q = [sb(f"ctx_q{i}", [P, KC, SQ]) for i in range(2)]
        mb = [sb(f"mb{i}", [2 * L, SQ]) for i in range(2)]
        ctx_last = [sb(f"ctx_last{i}", [P, KC, SQ]) for i in range(2)]
        mb_last = [sb(f"mb_last{i}", [2 * L, SQ]) for i in range(2)]
        kt = [sb(f"kt{i}", [P, KC, S2]) for i in range(2)]
        vt_q = sb("vt_q", [P, KC, SQ])
        v_lat = sb("v_lat", [P, KC, L])
        v_nat = [sb(f"v_nat{i}", [ST, NT + 1, E]) for i in range(2)]
        q_blk = [sb(f"q_blk{i}", [P, KC, 8, L]) for i in range(2)]
        probs = sb("probs", [ST, 2, KC, SLOT])
        masked = sb("masked", [2 * L, 2, SQ])
        part_max = sb("part_max", [2 * L, NP, NQ + 1])
        row_max = sb("row_max", [2 * L, NP])
        neg_rest = sb("neg_rest", [2 * L, NP])
        neg_piece = sb("neg_piece", [2 * L, 3, NP], BF16)
        neg_t = sb("neg_t", [3 * NP, 2 * L], BF16)
        neg_row = sb("neg_row", [P, KC, SLOT], BF16)
        ones3 = sb("ones3", [P, ST], BF16)
        ones_v = sb("ones_v", [ST, 32])
        num = sb("num", [P, KC, 2, L])
        den = sb("den", [P, KC, 2, L])
        o_even = sb("o_even", [P, KC, L])
        o = sb("o", [P, KC, L])
        AC, DE = 6, 7
        preset, neg_in = sem("preset"), sem("neg_in")
        ctx_in = [sem(f"ctx_in{i}") for i in range(2)]
        mb_in = [sem(f"mb_in{i}") for i in range(2)]
        ctx_last_in = [sem(f"ctx_last_in{i}") for i in range(2)]
        mb_last_in = [sem(f"mb_last_in{i}") for i in range(2)]
        kv_mm, kv_rd, vt_mm, vt_rd, row_mm, row_rd = map(sem, "kv_mm kv_rd vt_mm vt_rd row_mm row_rd".split())
        lat_kv, lat_q, latrow_mm, latrow_rd, latv_mm, latv_rd = map(
            sem, "lat_kv lat_q latrow_mm latrow_rd latv_mm latv_rd".split())
        chain, neg_mm, negt = map(sem, "chain neg_mm negt".split())
        sc_mm, pr, pv_mm, num_rd, den_rd, o_sem, out_mm, y_done = map(
            sem, "sc_mm pr pv_mm num_rd den_rd o_sem out_mm y_done".split())
        CHAIN, O_STEPS = 5, 4
        ctx_view = a["ctx_t"].rearrange("b (c p) s -> b p c s", p=P)

        def flag_of(eng, b, i):
            return eng.value_load(flags[0:1, bass.ds(b, 1), i], min_val=0, max_val=1)

        def pass_over(eng, done):
            for which, base, n in done:
                if not isinstance(base, int) or base > 0:
                    eng.wait_ge(which, base)
                eng.sem_inc(which, n)

        def plus(x):
            return not isinstance(x, int) or x > 0

        def load(sp, b, q, ctx_to, ctx_sem, mb_to, mb_sem):
            sp.dma_start(ctx_to[:], ctx_view[bass.ds(b, 1)].rearrange("o p c s -> p (o c) s")
                         [:, :, q * SQ:(q + 1) * SQ]).then_inc(ctx_sem, 16)
            sp.dma_start(mb_to[:], mb_scr[bass.ds(b, 1), q, :].to_broadcast([2 * L, SQ])).then_inc(mb_sem, 16)

        def load_last(sp, b, par):
            loads_before = 8 * (b - par)
            with sp.If(flag_of(sp, b, 1)):
                if plus(b - 1):
                    wait_apart(sp, passed, kv_mm, 4 * NQ * (b - 1))
                    sp.wait_ge(row_rd, NP * NQ * (b - 1))
                load(sp, b, NQ - 1, ctx_last[par], ctx_last_in[par], mb_last[par], mb_last_in[par])
            with sp.Else():
                pass_over(sp, [(ctx_last_in[par], loads_before, 16), (mb_last_in[par], loads_before, 16)])

        def sp_body(sp, b, par, one, two, three):
            ahead = not isinstance(b, int) or b + 1 < B
            if two:
                wait_apart(sp, passed, negt, b)
                if plus(b - 1):
                    sp.wait_ge(sc_mm, KC * TILES * (b - 1))
                for r in range(3):
                    sp.dma_start(neg_row[r:r + 1].rearrange("p k n -> p (k n)"), neg_t[r * NP:(r + 1) * NP, :])\
                      .then_inc(neg_in, 16)
            if one:
                with sp.If(flag_of(sp, b, 0)):
                    for q in PARTS[0]:
                        n = b * NQ + q
                        if plus(n - 1):
                            wait_apart(sp, passed, kv_mm, 4 * (n - 1))
                            sp.wait_ge(row_rd, NP * (n - 1))
                        load(sp, b, q, ctx_q[q % 2], ctx_in[q % 2], mb[q % 2], mb_in[q % 2])
                with sp.Else():
                    pass_over(sp, [(ctx_in[0], 32 * b, 32), (mb_in[0], 32 * b, 32), (ctx_in[1], 16 * b, 16),
                                   (mb_in[1], 16 * b, 16)])
            if ahead:
                load_last(sp, b + 1, 1 - par)

        def arrived(eng, b, par, q, which):
            if q == NQ - 1:
                eng.wait_ge((ctx_last_in, mb_last_in)[which][par], 8 * (b - par) + 16)
                return ctx_last[par], mb_last[par]
            uses = 2 * b + q // 2 if q % 2 == 0 else b
            eng.wait_ge((ctx_in, mb_in)[which][q % 2], 16 * (uses + 1))
            return ctx_q[q % 2], mb[q % 2]

        def pe_body(pe, b, par, one, two, three):
            old = 1 - par
            flag = [flag_of(pe, b, i) for i in range(len(PARTS))] if one else []
            flag_old = [flag_of(pe, b - 1, i) for i in range(len(PARTS))] if two else []
            if two:
                pe.wait_ge(chain, CHAIN * b)
                pe.transpose(ps[0:3 * NP, 2, :].bitcast(BF16)[:, 0:2 * L], neg_piece[:].rearrange("p r n -> p (r n)"),
                             identb[0:2 * L, 0:2 * L]).then_inc(neg_mm, 1)
            def keys(i, part):
                n0 = b * NQ + part[0]
                with pe.If(flag[i]):
                    for q in part:
                        n = b * NQ + q
                        context, _ = arrived(pe, b, par, q, 0)
                        if plus(n):
                            pe.wait_ge(row_rd, NP * n)
                        for m in range(4):
                            for k in range(KC):
                                mm = pe.matmul(ps[:, m, 0:SQ], kv_w[:, k, m * P:(m + 1) * P], context[:, k],
                                               start=(k == 0), stop=(k == KC - 1))
                            mm.then_inc(kv_mm, 1)
                        pe.wait_ge(kv_rd, 4 * n + 4)
                        for t in range(TQ):
                            for k in range(KC):
                                mm = pe.transpose(ps[0:ST, t // 2, (t % 2 * 2 + k) * P:(t % 2 * 2 + k + 1) * P],
                                                  vt_q[:, k, t * ST:(t + 1) * ST], ident[:])
                            if t % 2 == 1 or t == TQ - 1:
                                mm.then_inc(vt_mm, 1)
                        pe.wait_ge(lat_q, b + 1)
                        for p in range(NP):
                            if p in (2, 3):
                                pe.wait_ge(vt_rd, 2 * n + p - 1)
                            if p >= 4:
                                pe.wait_ge(row_rd, NP * n + p - 3)
                            k, i = divmod(p, 4)
                            pe.matmul(ps[0:2 * L, (2 + p) % 4, 0:SQ],
                                      q_blk[par][:, k, 2 * i:2 * i + 2].rearrange("p h l -> p (h l)"),
                                      kt[par][:, k, q * SQ:(q + 1) * SQ], start=True, stop=True).then_inc(row_mm, 1)
                with pe.Else():
                    m = len(part)
                    pass_over(pe, [(kv_mm, 4 * n0, 4 * m), (vt_mm, 2 * n0, 2 * m), (row_mm, NP * n0, NP * m)])


            def scores(n, rows, tokens):
                at = TILES * (b - 1) + n
                for k in range(KC):
                    if plus(at):
                        pe.wait_ge(pr, KC * (at - 1) + k + 1)
                    pe.matmul(ps[0:rows, 4 + k, 0:SLOT], kt[old][:, k, tokens],
                              q_blk[old][:, k].rearrange("p h l -> p (h l)"), start=True, stop=False)
                    mm = pe.matmul(ps[0:rows, 4 + k, 0:SLOT], ones3[:, 0:rows], neg_row[:, k], start=False, stop=True)
                    mm.then_inc(sc_mm, 1)

            def sums(n, rows, tile):
                at = TILES * (b - 1) + n
                if n == 0 and plus(b - 1):
                    pe.wait_ge(num_rd, b - 1)
                    pe.wait_ge(den_rd, b - 1)
                wait_apart(pe, passed, pr, KC * (at + 1))
                for k, bank in ((0, AC), (1, AC), (0, DE), (1, DE)):
                    for i in range(4):
                        p = 4 * k + i
                        lhs = v_nat[old][0:rows, tile, p * 32:p * 32 + 32] if bank == AC else ones_v[0:rows]
                        mm = pe.matmul(ps[32 * i:32 * i + 32, bank, k * 2 * L:(k + 1) * 2 * L], lhs,
                                       probs[0:rows, (old + n) % 2, k, i * 2 * L:(i + 1) * 2 * L],
                                       start=(n == 0 and k == 0), stop=(n == TILES - 1), skip_group_check=True)
                mm.then_inc(pv_mm, 1)

            def values(i, part):
                first, end = part[0] * TQ, (part[-1] + 1) * TQ
                base = TILES * (b - 1) + 1 + first
                with pe.If(flag_old[i]):
                    for tile in range(first, end + 1):
                        if tile < end:
                            scores(1 + tile, ST, slice(tile * ST, (tile + 1) * ST))
                        if tile > first:
                            sums(tile, ST, tile - 1)
                with pe.Else():
                    pass_over(pe, [(sc_mm, KC * base, KC * (end - first)), (pv_mm, base, end - first)])

            if one:
                if plus(b):
                    pe.wait_ge(latrow_rd, b)
                    pe.wait_ge(latv_rd, b)
                if two:
                    pe.wait_ge(negt, b)
                if three:
                    pe.wait_ge(y_done, b - 1)
                for i, part in enumerate(PARTS):
                    keys(i, part)
                pe.wait_ge(lat_kv, 2 * (b + 1))
                pe.wait_ge(lat_q, b + 1)
                pe.wait_ge(row_rd, NP * NQ * (b + 1) - 2)
                for p in range(NP):
                    k, i = divmod(p, 4)
                    mm = pe.matmul(ps[0:2 * L, 2, p * L:(p + 1) * L],
                                   q_blk[par][:, k, 2 * i:2 * i + 2].rearrange("p h l -> p (h l)"),
                                   kt[par][:, k, S:S2], start=True, stop=True)
                mm.then_inc(latrow_mm, 1)
                for k in range(KC):
                    mm = pe.transpose(ps[0:L, 3, k * P:(k + 1) * P], v_lat[:, k], ident[:])
                mm.then_inc(latv_mm, 1)
            if two:
                pe.wait_ge(neg_in, 48 * b)
                scores(0, L, slice(S, S2))
            if three:
                pe.wait_ge(o_sem, O_STEPS * b)
                if one:
                    pe.wait_ge(row_rd, NP * NQ * (b + 1))
                first = natural(par)
                for k in range(KC):
                    mm = pe.matmul(ps[first:first + L, 0, 0:E], o[:, k], out_w[:, k], start=(k == 0),
                                   stop=(k == KC - 1))
                mm.then_inc(out_mm, 1)
            if two:
                sums(0, L, NT)
                for i, part in enumerate(PARTS):
                    values(i, part)

        def act_body(act, b, par, one, two, three):
            def exps(n, rows, bias):
                at = TILES * (b - 1) + n
                if plus(at - 1):
                    act.wait_ge(pv_mm, at - 1)
                more = {} if bias is None else {"bias": bias}
                for k in range(KC):
                    wait_apart(act, passed, sc_mm, KC * at + k + 1)
                    act.activation(probs[0:rows, (1 - par + n) % 2, k], ps[0:rows, 4 + k, 0:SLOT], ACT.Exp, **more)\
                       .then_inc(pr, 1)

            if one:
                for i, part in enumerate(PARTS):
                    with act.If(flag_of(act, b, i)):
                        if plus(b - 1):
                            act.wait_ge(sc_mm, KC * TILES * (b - 1))
                        for q in part:
                            for m in range(4):
                                act.wait_ge(kv_mm, 4 * (b * NQ + q) + m + 1)
                                dst = kt[par][:, m, q * SQ:(q + 1) * SQ] if m < KC else vt_q[:, m - KC]
                                act.activation(dst, ps[:, m, 0:SQ], ACT.Identity, bias=kv_b[:, m:m + 1])\
                                   .then_inc(kv_rd, 1)
                    with act.Else():
                        pass_over(act, [(kv_rd, 4 * (b * NQ + part[0]), 4 * len(part))])
            if two:
                exps(0, L, None)
                for i, part in enumerate(PARTS):
                    first, end = part[0] * TQ, (part[-1] + 1) * TQ
                    with act.If(flag_of(act, b - 1, i)):
                        for tile in range(first, end):
                            exps(1 + tile, ST, bias_t[:, bass.ds(b - 1, 1), tile])
                    with act.Else():
                        pass_over(act, [(pr, KC * (TILES * (b - 1) + 1 + first), KC * (end - first))])
            if two:
                act.wait_ge(pv_mm, TILES * b)
                act.wait_ge(o_sem, O_STEPS * b)
                act.activation(num[:].rearrange("p k h l -> p (k h l)"), ps[:, AC, 0:2 * KC * L], ACT.Copy)\
                   .then_inc(num_rd, 1)

        def dve_body(dve, b, par, one, two, three):
            def invert():
                dve.wait_ge(pv_mm, TILES * (b - 1))
                dve.wait_ge(o_sem, O_STEPS * (b - 1))
                dve.reciprocal(den[:].rearrange("p k h l -> p (k h l)"), ps[:, DE, 0:2 * KC * L]).then_inc(den_rd, 1)

            def quarter(q):
                n = b * NQ + q
                for i, tiles in enumerate(((0, 2), (2, TQ))):
                    dve.wait_ge(vt_mm, 2 * n + i + 1)
                    t0, t1 = q * TQ + tiles[0], q * TQ + tiles[1]
                    dve.tensor_copy(v_nat[par][:, t0:t1, :].rearrange("p t e -> p (t e)"),
                                    ps[0:ST, i, 0:(t1 - t0) * E]).then_inc(vt_rd, 1)
                _, mask_add = arrived(dve, b, par, q, 1)
                for p in range(NP):
                    if p >= 2 or plus(n):
                        dve.wait_ge(row_rd, NP * n + p - 1)
                    wait_apart(dve, passed, row_mm, NP * n + p + 1)
                    dve.tensor_tensor_reduce(
                        out=masked[:, p % 2], in0=ps[0:2 * L, (2 + p) % 4, 0:SQ], in1=mask_add[:], scale=1.0,
                        scalar=NEG_BIG, op0=ALU.add, op1=ALU.max,
                        accum_out=part_max[:, p, q:q + 1]).then_inc(row_rd, 1)

            if two:
                dve.wait_ge(neg_mm, b)
                if plus(b - 1):
                    dve.wait_ge(neg_in, 48 * (b - 1))
                dve.tensor_copy(neg_t[:], ps[0:3 * NP, 2, :].bitcast(BF16)[:, 0:2 * L]).then_inc(negt, 1)
            if one:
                if plus(b - 1):
                    dve.wait_ge(sc_mm, KC * TILES * (b - 1))
                dve.tensor_tensor(q_blk[par][:],
                                  qt[:, :, bass.ds(b * L, L)].unsqueeze(2).to_broadcast([P, KC, 8, L]),
                                  head_scale[:].unsqueeze(1).unsqueeze(3).to_broadcast([P, KC, 8, L]), ALU.mult)\
                   .then_inc(lat_q, 1)
                if three:
                    invert()
                if plus(b - 1):
                    dve.wait_ge(pv_mm, TILES * (b - 1))
                for i, part in enumerate(PARTS):
                    n0 = b * NQ + part[0]
                    with dve.If(flag_of(dve, b, i)):
                        for q in part:
                            quarter(q)
                    with dve.Else():
                        m = len(part)
                        pass_over(dve, [(vt_rd, 2 * n0, 2 * m), (row_rd, NP * n0, NP * m - 1)])
                        dve.memset(part_max[:, :, part[0]:part[-1] + 1], NEG_BIG).then_inc(row_rd, 1)
                dve.wait_ge(latrow_mm, b + 1)
                dve.tensor_reduce(part_max[:, :, NQ], ps[0:2 * L, 2, 0:NP * L].rearrange("p (h l) -> p h l", l=L),
                                  AX_X, ALU.max).then_inc(latrow_rd, 1)
                dve.wait_ge(latv_mm, b + 1)
                dve.tensor_copy(v_nat[par][0:L, NT, :], ps[0:L, 3, 0:E]).then_inc(latv_rd, 1)
                k = CHAIN * b
                dve.wait_ge(row_rd, NP * NQ * (b + 1))
                dve.wait_ge(latrow_rd, b + 1)
                if plus(b):
                    dve.wait_ge(neg_mm, b)
                dve.tensor_reduce(row_max[:], part_max[:], AX_X, ALU.max).then_inc(chain, 1)
                dve.wait_ge(chain, k + 1)
                dve.tensor_scalar(neg_piece[:, 0], row_max[:], -1.0, None, ALU.mult).then_inc(chain, 1)
                dve.wait_ge(chain, k + 2)
                dve.scalar_tensor_tensor(neg_rest[:], row_max[:], -1.0, neg_piece[:, 0], ALU.mult,
                                         ALU.subtract).then_inc(chain, 1)
                dve.wait_ge(chain, k + 3)
                dve.tensor_copy(neg_piece[:, 1], neg_rest[:]).then_inc(chain, 1)
                dve.wait_ge(chain, k + 4)
                dve.tensor_tensor(neg_piece[:, 2], neg_rest[:], neg_piece[:, 1], ALU.subtract).then_inc(chain, 1)
            if three:
                if not one:
                    invert()
                dve.wait_ge(out_mm, b)
                first = natural(par)
                rows = y_nat[first:first + L, bass.ds((b - 2) // 2, 1), :].rearrange("p o e -> p (o e)")
                dve.tensor_tensor(rows, ps[first:first + L, 0, 0:E], rows, ALU.add).then_inc(y_done, 1)

        def pool_body(pool, b, par, one, two, three):
            if one:
                if plus(b - 1):
                    pool.wait_ge(sc_mm, KC * TILES * (b - 1))
                pool.tensor_copy(kt[par][:, :, S:S2], kv_lat[:, 0:KC, bass.ds(b * L, L)]).then_inc(lat_kv, 1)
                if plus(b):
                    pool.wait_ge(latv_mm, b)
                pool.tensor_copy(v_lat[:], kv_lat[:, KC:2 * KC, bass.ds(b * L, L)]).then_inc(lat_kv, 1)
            if three:
                pool.wait_ge(num_rd, b - 1)
                pool.wait_ge(den_rd, b - 1)
                done = O_STEPS * (b - 1)
                pool.tensor_tensor(num[:], num[:], den[:], ALU.mult).then_inc(o_sem, 1)
                wait_apart(pool, passed, o_sem, done + 1)
                pool.tensor_scalar(o_even[:], num[:, :, 0], odd_mask[:, 0:1], None, ALU.mult).then_inc(o_sem, 1)
                wait_apart(pool, passed, out_mm, b - 1)
                pool.tensor_scalar(o[:], num[:, :, 1], odd_mask[:, 1:2], None, ALU.mult).then_inc(o_sem, 1)
                pool.wait_ge(o_sem, done + 3)
                pool.tensor_tensor(o[:], o[:], o_even[:], ALU.add).then_inc(o_sem, 1)

        def all_bodies(eng, body, loop_end):
            def one(b, par):
                known = isinstance(b, int)
                body(eng, b, par, not known or b < B, not known or 1 <= b <= B, not known or b >= 2)
            one(0, 0)
            one(1, 1)
            with eng.Fori(2, loop_end - 1, 2) as b:
                one(b, 0)
                one(b + 1, 1)
            for b in range(loop_end, B + 2):
                one(b, b % 2)

        with nc.Block() as block:
            @block.sync
            def _(sp):
                sp.wait_ge(preset, 4)
                load_last(sp, 0, 0)
                all_bodies(sp, sp_body, B - 2)

            @block.tensor
            def _(pe):
                pe.wait_ge(preset, 4)
                pe.sem_inc(out_mm, 1)
                all_bodies(pe, pe_body, B)

            @block.scalar
            def _(act):
                all_bodies(act, act_body, B)

            @block.vector
            def _(dve):
                dve.sem_inc(y_done, 1)
                all_bodies(dve, dve_body, B)

            @block.gpsimd
            def _(pool):
                sets = [(neg_row[:], 0.0), (ones3[:], 0.0), (ones3[0:3], 1.0), (ones_v[:], 1.0)]
                for n, (where, value) in enumerate(sets):
                    pool.memset(where, value).then_inc(preset, 1)
                    pool.wait_ge(preset, n + 1)
                pool.sem_inc(o_sem, O_STEPS)
                all_bodies(pool, pool_body, B)
        clear(nc, sems)


def mlp(nc, x_nat, y_nat, a):
    GM = 4
    NM = GM * P
    with ExitStack() as ctx:
        def sb(name, shape, dt=F32):
            return ctx.enter_context(nc.sbuf_tensor("m_" + name, shape, dt))

        ident = sb("ident", [P, P])
        w1 = sb("w1", [P, KC, FF])
        b1 = sb("b1", [P, FC])
        w2 = sb("w2", [P, FC, E])
        b2 = sb("b2", [P, E])
        norm_w = sb("norm_w", [P, KC])
        loads = [(ident, "ident"), (w1, "mlp_w1"), (b1, "mlp_b1"), (w2, "mlp_w2"), (b2, "mlp_b2"),
                 (norm_w, "postnorm")]
        eps = sb("eps", [P, 1])
        square = sb("square", [P, 2, E])
        sum_sq = sb("sum_sq", [P, PAIRS])
        rms = sb("rms", [P, PAIRS])
        rrms = sb("rrms", [P, PAIRS])
        yn = sb("yn", [P, GM, E])
        yt = sb("yt", [P, KC, NM])
        h = sb("h", [P, FC, NM])
        ps = ctx.enter_context(nc.psum_tensor("ps_m", [P, 8, 512], F32))
        sems = loaded, preset, squared, rms_set, rrms_set, based, normed, turned, yt_set, hid_mm, hid, out_mm, out_rd = [
            ctx.enter_context(nc.semaphore("m_" + n)) for n in
            "loaded preset squared rms_set rrms_set based normed turned yt_set hid_mm hid out_mm out_rd".split()]

        def later(c):
            return not isinstance(c, int) or c > 0

        with nc.Block() as block:
            @block.sync
            def _(sp):
                for dst, name in loads:
                    sp.dma_start(dst[:], a[name]).then_inc(loaded, 16)
                sp.wait_ge(loaded, 16 * len(loads))

            @block.gpsimd
            def _(pool):
                pool.memset(eps[:], RMS_EPS).then_inc(preset, 1)

            @block.tensor
            def _(pe):
                pe.wait_ge(loaded, 16 * len(loads))

                def output(c, m):
                    pe.wait_ge(hid, FC * c + m + 1)
                    for g in range(GM):
                        mm = pe.matmul(ps[:, 6 + g // 2, g % 2 * E:(g % 2 + 1) * E], h[:, m, g * P:(g + 1) * P],
                                       w2[:, m], start=(m == 0 and g % 2 == 0), stop=(m == FC - 1),
                                       skip_group_check=True)
                    return mm

                pe.sem_inc(out_mm, 1)
                with pe.Fori(0, PAIRS // GM) as c:
                    for k in range(KC):
                        pe.wait_ge(normed, GM * (c + 1))
                        for g in range(GM):
                            mm = pe.transpose(ps[:, k, g * P:(g + 1) * P], yn[:, g, k * P:(k + 1) * P], ident[:])
                        mm.then_inc(turned, 1)
                    pe.wait_ge(yt_set, KC * (c + 1))
                    for m in range(FC):
                        if m >= 4:
                            pe.wait_ge(hid, FC * c + m - 3)
                        for k in range(KC):
                            mm = pe.matmul(ps[:, 2 + m % 4, :], w1[:, k, m * P:(m + 1) * P], yt[:, k],
                                           start=(k == 0), stop=(k == KC - 1))
                        mm.then_inc(hid_mm, 1)
                        if m >= 2:
                            if m == 2:
                                pe.wait_ge(out_rd, 2 * (c + 1))
                            output(c, m - 2)
                    output(c, FC - 2)
                    output(c, FC - 1).then_inc(out_mm, 1)

            @block.scalar
            def _(act):
                for g in range(PAIRS):
                    if g >= 2:
                        act.wait_ge(squared, g - 1)
                    act.activation(square[:, g % 2], y_nat[:, g], ACT.Square,
                                   accum_out=sum_sq[:, g:g + 1]).then_inc(squared, 1)
                act.wait_ge(preset, 1)
                act.wait_ge(squared, PAIRS)
                act.activation(rms[:], sum_sq[:], ACT.Sqrt, scale=1.0 / E, bias=eps[:]).then_inc(rms_set, 1)
                act.wait_ge(loaded, 16 * len(loads))
                with act.Fori(0, PAIRS // GM) as c:
                    for k in range(KC):
                        act.wait_ge(turned, KC * c + k + 1)
                        act.activation(yt[:, k], ps[:, k], ACT.Identity, scale=norm_w[:, k:k + 1]).then_inc(yt_set, 1)
                    for m in range(FC):
                        act.wait_ge(hid_mm, FC * c + m + 1)
                        if m == 0:
                            act.wait_ge(out_mm, c + 1)
                        act.activation(h[:, m], ps[:, 2 + m % 4], ACT.Gelu_apprx_tanh,
                                       bias=b1[:, m:m + 1]).then_inc(hid, 1)

            @block.vector
            def _(dve):
                dve.wait_ge(loaded, 16 * len(loads))
                dve.tensor_tensor(x_nat[:], x_nat[:], b2[:].unsqueeze(1).to_broadcast([P, PAIRS, E]),
                                  ALU.add).then_inc(based, 1)
                dve.wait_ge(rms_set, 1)
                dve.reciprocal(rrms[:], rms[:]).then_inc(rrms_set, 1)
                dve.wait_ge(rrms_set, 1)
                dve.wait_ge(based, 1)

                def normalise(c, g):
                    if later(c):
                        dve.wait_ge(turned, KC * c)
                    tile = bass.ds(c * GM + g, 1)
                    dve.tensor_scalar(yn[:, g], y_nat[:, tile, :].rearrange("p o e -> p (o e)"), rrms[:, tile], None,
                                      ALU.mult).then_inc(normed, 1)

                def output_rows(c):
                    dve.wait_ge(out_mm, c + 2)
                    for i in range(2):
                        rows = x_nat[:, bass.ds(c * GM + 2 * i, 2), :].rearrange("p g e -> p (g e)")
                        dve.tensor_tensor(rows, ps[:, 6 + i], rows, ALU.add).then_inc(out_rd, 1)

                dve.sem_inc(out_rd, 2)
                for g in range(GM):
                    normalise(0, g)
                with dve.Fori(0, PAIRS // GM - 1) as c:
                    for g in range(GM):
                        normalise(c + 1, g)
                    output_rows(c)
                output_rows(PAIRS // GM - 1)
        clear(nc, sems)


def rows_first(w):
    return w.reshape(-1, P, w.shape[-1]).transpose(1, 0, 2)


def natural_rows(x):
    n = np.zeros((2, HALF, PAIRS, x.shape[-1]), x.dtype)
    n[:, :L] = x.reshape(PAIRS, 2, L, -1).transpose(1, 2, 0, 3)
    return n.reshape(P, PAIRS, -1)


def layout(i):
    d = {}
    x, c = i["x"], i["ctx_2048"]
    d["x_nat"] = natural_rows(x)
    d["x_t"] = x.reshape(T, E).T
    d["ctx_t"] = c.transpose(0, 2, 1)
    m0 = i["mask_Bx1xSxS2_ff0"][:, 0]
    d["mask0"] = np.concatenate([m0, m0], 1)
    d["ident"] = np.eye(P, dtype=np.float32)
    def by_pair(w):
        return w.reshape(w.shape[:-1] + (NJ, 2, HD)).swapaxes(-3, -2).swapaxes(-2, -1).reshape(w.shape)

    w = by_pair(i["L0_xattn_Wq"].reshape(E, KVH, G, HD).transpose(0, 2, 1, 3).reshape(E, G, KVH * HD))
    d["wq"] = rows_first(w.reshape(E, -1)).reshape(P, KC, G, KVH * HD)
    d["bq"] = by_pair(i["L0_xattn_bq"].reshape(KVH, G, HD).transpose(1, 0, 2).reshape(G, KVH * HD)).T
    d["wkv"] = rows_first(np.concatenate([by_pair(i["L0_xattn_Wk"]), i["L0_xattn_Wv"]], 1))
    d["bkv"] = np.concatenate([by_pair(i["L0_xattn_bk"]), i["L0_xattn_bv"]]).reshape(P, 1)
    wo = np.zeros((NJ, 32, 2, G, E), np.float32)
    wo[:, :HD] = i["L0_xattn_Wo"].reshape(NJ, 2, G, HD, E).transpose(0, 3, 1, 2, 4)
    d["wo"] = wo.reshape(P, 2 * G, E)
    d["bo"] = np.broadcast_to(i["L0_xattn_bo"], (P, E))
    d["ln0_g"] = np.broadcast_to(i["L0_xattn_gamma"], (P, E))
    d["ln0_b"] = np.broadcast_to(i["L0_xattn_beta"], (P, E))
    sel = np.zeros((NJ, 32, NJ, 32), np.float32)
    for j in range(NJ):
        sel[j, HD, j, :] = 1.0
    d["den_sel"] = sel.reshape(P, P)
    d["mask_sel"] = np.tile(np.eye(L, dtype=np.float32), (1, 2 * G))
    for tag, src, n in (("b", "L1_xattn_", {"u": "faaaa", "dw1": "decay_w1", "dw2": "decay_w2", "fk": "ffn_Wk",
                                           "fr": "ffn_Wr", "fv": "ffn_Wv"}),
                        ("d", "L3_xattn_", {"u": "u", "dw1": "td_w1", "dw2": "td_w2", "fk": "Wfk", "fr": "Wfr",
                                           "fv": "Wfv"})):
        m = i[src + "maa_stack"].reshape(5, E)
        vec = {"ln1_w": i[src + "ln1_w"], "ln1_b": i[src + "ln1_b"], "ln2_w": i[src + "ln2_w"],
               "ln2_b": i[src + "ln2_b"], "maa_x": i[src + "maa_x"], "td": i[src + "time_decay"],
               "gn_w": i[src + "gn_w"], "gn_b": i[src + "gn_b"], "u": i[src + n["u"]],
               "fmk": i[src + "ffn_maa_k"], "fmr": i[src + "ffn_maa_r"]} | {f"m{j}": m[j] for j in range(5)}
        d[tag + "vec"] = rows_first(np.stack([vec[k].reshape(E) for k in VEC], 1))
        w1 = np.zeros((E, 2 * P), np.float32)
        w1[:, :160] = i[src + "maa_w1"]
        d[tag + "w1"] = rows_first(w1)
        w2 = np.zeros((P, 5, E), np.float32)
        for j in range(5):
            w2[32 * (j % 4):32 * (j % 4) + 32, j] = i[src + "maa_w2"][j]
        d[tag + "w2"] = w2
        dw1 = np.zeros((E, P), np.float32)
        dw1[:, :64] = i[src + n["dw1"]]
        d[tag + "dw1"] = rows_first(dw1)
        dw2 = np.zeros((P, E), np.float32)
        dw2[:64] = i[src + n["dw2"]]
        d[tag + "dw2"] = dw2
        for k, name in (("wr", "Wr"), ("wk", "Wk"), ("wv", "Wv"), ("wg", "Wg"), ("wo", "Wo"), ("fk", n["fk"]),
                        ("fr", n["fr"]), ("fv", n["fv"])):
            d[tag + k] = rows_first(i[src + name].T)
    vsel = np.zeros((16, HS, HS, 16, HS), np.float32)
    for h in range(16):
        for j in range(HS):
            vsel[h, j, j, h, :] = 1.0
    d["vsel"] = vsel.reshape(P, HS, P)
    d["osel"] = vsel.reshape(P, HS, P).transpose(2, 1, 0)
    blocks = np.kron(np.eye(16, dtype=np.float32), np.ones((HS, HS), np.float32))
    d["head_sum"] = blocks
    d["head_mean"] = blocks / np.float32(HS)
    d["st"] = c[:, 0:2].reshape(B, 2, KC, P).transpose(3, 1, 2, 0)
    d["s0"] = c[:, 2:2 + HS].reshape(B, KC, P, HS).transpose(2, 1, 3, 0)
    kv_w, kv_b = i["L2_xattn_kv_w"].reshape(E, E, 2), i["L2_xattn_kv_b"].reshape(E, 2)
    d["c_kv_w"] = rows_first(np.concatenate([kv_w[:, :, 0], kv_w[:, :, 1]], 1))
    d["c_kv_b"] = np.concatenate([kv_b[:, 0], kv_b[:, 1]]).reshape(4, P).T
    d["c_q_w"], d["c_q_b"] = rows_first(i["L2_xattn_q_w"]), i["L2_xattn_q_b"].reshape(KC, P).T
    d["c_out_w"], d["c_out_b"] = rows_first(i["L2_xattn_out_w"]), np.broadcast_to(i["L2_xattn_out_b"], (P, E))
    d["head_scale"] = np.kron(np.eye(8, dtype=np.float32), np.ones((HD2, 1), np.float32)) / np.float32(HD2)
    d["odd_mask"] = np.kron(np.tile(np.eye(2, dtype=np.float32), (4, 1)), np.ones((HD2, 1), np.float32))
    mask = i["mask_BxS2_ik0"]
    d["mask_q"] = mask.reshape(B * NQ, SQ)
    d["mask_t"] = mask.reshape(B, NT, ST).transpose(2, 0, 1)
    d["mlp_w1"], d["mlp_b1"] = rows_first(i["L2_xattn_mlp_w1"]), i["L2_xattn_mlp_b1"].reshape(FC, P).T
    d["mlp_w2"], d["mlp_b2"] = rows_first(i["L2_xattn_mlp_w2"]), np.broadcast_to(i["L2_xattn_mlp_b2"], (P, E))
    d["postnorm"] = i["L2_xattn_postnorm_w"].reshape(KC, P).T
    return d


def program(nc, a, out):
    with nc.sbuf_tensor("x_nat", [P, PAIRS, E], F32) as x_nat, nc.semaphore("stored") as stored, \
            nc.semaphore("passed") as passed:

        layer0(nc, x_nat, a, passed)
        rwkv(nc, x_nat, a, "b", True, passed)
        with nc.sbuf_tensor("y_nat", [P, PAIRS, E], F32) as y_nat:
            latent_attention(nc, x_nat, y_nat, a, passed)
            mlp(nc, x_nat, y_nat, a)
        rwkv(nc, x_nat, a, "d", False, passed)
        with nc.Block() as block:
            @block.sync
            def _(sp):
                for par in range(2):
                    sp.dma_start(out.rearrange("(g r) l e -> r l g e", r=2)[par],
                                 x_nat[HALF * par:HALF * par + L]).then_inc(stored, 16)
                sp.wait_ge(stored, 32)


def kernel(**inputs):
    import numpy as _np
    import concourse.bacc as _bacc
    from concourse import mybir as _mybir
    from concourse.bass_utils import run_bass_kernel_spmd as _run

    arrays = layout({k: _np.asarray(v) for k, v in inputs.items()})
    nc = _bacc.Bacc("TRN2", target_bir_lowering=False, num_devices=1)
    args = {}
    feed = {}
    for name, v in arrays.items():
        v = _np.ascontiguousarray(v)
        feed[f"in_{name}"] = v
        args[name] = nc.dram_tensor(f"in_{name}", v.shape, _mybir.dt.from_np(v.dtype), kind="ExternalInput").ap()
    out = nc.dram_tensor("out_0", (B, L, E), F32, kind="ExternalOutput").ap()
    program(nc, args, out)
    r = _run(nc, [feed], core_ids=[0])
    return r.results[0]["out_0"]
```
